# Optimizing a Trainium2 kernel written in Bass

```python
import numpy as np
import jax
import jax.numpy as jnp

def _softmax(x, axis=-1):
    return jax.nn.softmax(x, axis=axis)

def _gelu(x):
    return jax.nn.gelu(x, approximate=True)

def _silu(x):
    return jax.nn.silu(x)

def _sigmoid(x):
    return jax.nn.sigmoid(x)

def _layernorm(x, axis=-1, eps=1e-05):
    m = jnp.mean(x, axis=axis, keepdims=True)
    v = jnp.var(x, axis=axis, keepdims=True)
    return (x - m) / jnp.sqrt(v + eps)

def _scatter_add(tgt, idx, src, axis=0):
    return tgt.at[idx].add(src)

def _segment_sum(src, seg, n):
    return jax.ops.segment_sum(src, seg, n)
kernel_name = 'mk_xattn_ffn_d1_seqx_r4_360664'

def setup_inputs(seed: int=0):
    np.random.seed(seed)
    _w = jnp.asarray

    def _rec_inputs():
        import jax
        import jax.numpy as jnp
        _rk = jax.random.key(seed)
        x = 7.22e-05 + 1 * jax.random.normal(jax.random.fold_in(_rk, 1), (4, 512, 512), jnp.float32)
        _lenS = 512 - jax.random.randint(jax.random.fold_in(_rk, 7), (4,), 0, max(1, 512 // 4) + 1, jnp.int32)
        _lenS2 = 512 - jax.random.randint(jax.random.fold_in(_rk, 8), (4,), 0, max(1, 512 // 4) + 1, jnp.int32)
        _ctx_1024P = jax.random.normal(jax.random.fold_in(_rk, 11), (4, 16, 256), jnp.float32)
        _ctx_1024c = jax.random.dirichlet(jax.random.fold_in(_rk, 511), 0.3 * jnp.ones((16,), jnp.float32), (4, 512))
        _ctx_1024t = jnp.einsum('bsk,bkd->bsd', _ctx_1024c, _ctx_1024P)
        _ctx_1024t = _ctx_1024t * jax.lax.rsqrt(jnp.mean(jnp.square(_ctx_1024t)) + 1e-12) * 0.953939
        ctx_1024 = -0.000673644 + 1.00013 * (_ctx_1024t + 0.3 * jax.random.normal(jax.random.fold_in(_rk, 611), (4, 512, 256), jnp.float32))
        return (x, ctx_1024)
    x, ctx_1024 = _rec_inputs()

    def _L0_xattn_setup():
        import jax, jax.numpy as jnp
        import numpy as np
        B, S1, S2, DCA = (2, 512, 256, 16)
        QDIM, KDIM, H = (512, 256, 16)
        HD = QDIM // H
        SCALE = HD ** (-0.5)
        EPS = 1e-06
        DCA_WEIGHT = 1.0

        def _ln(t, w, b):
            m = jnp.mean(t, axis=-1, keepdims=True)
            v = jnp.var(t, axis=-1, keepdims=True)
            return (t - m) * jax.lax.rsqrt(v + EPS) * w + b

        def _attn(q, k, v):
            s = jnp.einsum('bhqd,bhkd->bhqk', q, k) * SCALE
            p = jax.nn.softmax(s, axis=-1)
            return jnp.einsum('bhqk,bhkd->bhqd', p, v)
        key = jax.random.key(seed)
        ks = jax.random.split(key, 8)
        w = lambda k, shape: jax.random.normal(k, shape, jnp.float32) * 0.02
        return {'x': jax.random.normal(ks[0], (B, S1, QDIM), jnp.float32), 'y': jax.random.normal(ks[1], (B, S2 + DCA, KDIM), jnp.float32), 'Wq': w(ks[2], (QDIM, QDIM)), 'bq': jnp.zeros((QDIM,), jnp.float32), 'Wk': w(ks[3], (KDIM, QDIM)), 'bk': jnp.zeros((QDIM,), jnp.float32), 'Wv': w(ks[4], (KDIM, QDIM)), 'bv': jnp.zeros((QDIM,), jnp.float32), 'Wkv_dca': w(ks[5], (KDIM, 2 * QDIM)), 'bkv_dca': jnp.zeros((2 * QDIM,), jnp.float32), 'qn_w': jnp.ones((HD,), jnp.float32), 'qn_b': jnp.zeros((HD,), jnp.float32), 'kn_w': jnp.ones((HD,), jnp.float32), 'kn_b': jnp.zeros((HD,), jnp.float32), 'kn_dca_w': jnp.ones((HD,), jnp.float32), 'kn_dca_b': jnp.zeros((HD,), jnp.float32), 'Wo': w(ks[6], (QDIM, QDIM)), 'bo': jnp.zeros((QDIM,), jnp.float32)}
    _L0_xattn_all = _L0_xattn_setup()
    _L0_xattn_in = {k: v for k, v in _L0_xattn_all.items() if k in ('Wq', 'bq', 'Wk', 'bk', 'Wv', 'bv', 'Wkv_dca', 'bkv_dca', 'qn_w', 'qn_b', 'kn_w', 'kn_b', 'kn_dca_w', 'kn_dca_b', 'Wo', 'bo')}
    del _L0_xattn_all

    def _L0_ffn_setup():
        import jax, jax.numpy as jnp
        import numpy as np
        H = 512
        I = 512
        E_ROUTED = 7
        NS = 1
        TOPK = 2
        TEMP = 1.0

        def _moe_forward(x, Wr, br, gate_bias, Wup, bup, Wgate, bgate, Wdown, bdown, Wsu, bsu, Wsg, bsg, Wsd, bsd):
            B, S, _ = x.shape
            xt = x.reshape(-1, H)
            N = xt.shape[0]
            gate = (xt @ Wr + br) / TEMP
            bias_gate = gate + gate_bias
            _, ids = jax.lax.top_k(bias_gate, TOPK)
            sel_logits = jnp.take_along_axis(gate, ids, axis=-1)
            masked = jnp.full_like(gate, -jnp.inf)
            masked = masked.at[jnp.arange(N)[:, None], ids].set(sel_logits)
            probs = jax.nn.softmax(masked, axis=-1)
            u = jnp.einsum('nh,ehi->eni', xt, Wup) + bup[:, None, :]
            g = jax.nn.silu(jnp.einsum('eni,eij->enj', u, Wgate) + bgate[:, None, :]) * u
            eo = jnp.einsum('enj,ejh->enh', g, Wdown) + bdown[:, None, :]
            out = jnp.einsum('ne,enh->nh', probs, eo)
            su = (xt @ Wsu + bsu).reshape(N, NS, I)
            sg = jax.nn.silu(su @ Wsg + bsg) * su
            so = (sg @ Wsd + bsd).sum(axis=1)
            out = out + so
            return out.reshape(B, S, H)
        key = jax.random.key(seed)
        ks = jax.random.split(key, 20)
        s = lambda fan_in: 1.0 / np.sqrt(fan_in)
        inp = {'x': jax.random.normal(ks[0], (4, 256, H), dtype=jnp.float32), 'Wr': jax.random.normal(ks[1], (H, E_ROUTED), jnp.float32) * s(H), 'br': jax.random.normal(ks[2], (E_ROUTED,), jnp.float32) * s(H), 'gate_bias': jnp.zeros((E_ROUTED,), jnp.float32), 'Wup': jax.random.normal(ks[3], (E_ROUTED, H, I), jnp.float32) * s(H), 'bup': jax.random.normal(ks[4], (E_ROUTED, I), jnp.float32) * s(H), 'Wgate': jax.random.normal(ks[5], (E_ROUTED, I, I), jnp.float32) * s(I), 'bgate': jax.random.normal(ks[6], (E_ROUTED, I), jnp.float32) * s(I), 'Wdown': jax.random.normal(ks[7], (E_ROUTED, I, H), jnp.float32) * s(I), 'bdown': jax.random.normal(ks[8], (E_ROUTED, H), jnp.float32) * s(I), 'Wsu': jax.random.normal(ks[9], (H, NS * I), jnp.float32) * s(H), 'bsu': jax.random.normal(ks[10], (NS * I,), jnp.float32) * s(H), 'Wsg': jax.random.normal(ks[11], (I, I), jnp.float32) * s(I), 'bsg': jax.random.normal(ks[12], (I,), jnp.float32) * s(I), 'Wsd': jax.random.normal(ks[13], (I, H), jnp.float32) * s(I), 'bsd': jax.random.normal(ks[14], (H,), jnp.float32) * s(I)}
        return inp
    _L0_ffn_all = _L0_ffn_setup()
    _L0_ffn_in = {k: v for k, v in _L0_ffn_all.items() if k in ('Wr', 'br', 'gate_bias', 'Wup', 'bup', 'Wgate', 'bgate', 'Wdown', 'bdown', 'Wsu', 'bsu', 'Wsg', 'bsg', 'Wsd', 'bsd')}
    del _L0_ffn_all
    return {'x': x, 'ctx_1024': ctx_1024, 'L0_xattn_Wq': _L0_xattn_in['Wq'], 'L0_xattn_bq': _L0_xattn_in['bq'], 'L0_xattn_Wk': _L0_xattn_in['Wk'], 'L0_xattn_bk': _L0_xattn_in['bk'], 'L0_xattn_Wv': _L0_xattn_in['Wv'], 'L0_xattn_bv': _L0_xattn_in['bv'], 'L0_xattn_Wkv_dca': _L0_xattn_in['Wkv_dca'], 'L0_xattn_bkv_dca': _L0_xattn_in['bkv_dca'], 'L0_xattn_qn_w': _L0_xattn_in['qn_w'], 'L0_xattn_qn_b': _L0_xattn_in['qn_b'], 'L0_xattn_kn_w': _L0_xattn_in['kn_w'], 'L0_xattn_kn_b': _L0_xattn_in['kn_b'], 'L0_xattn_kn_dca_w': _L0_xattn_in['kn_dca_w'], 'L0_xattn_kn_dca_b': _L0_xattn_in['kn_dca_b'], 'L0_xattn_Wo': _L0_xattn_in['Wo'], 'L0_xattn_bo': _L0_xattn_in['bo'], 'L0_ffn_Wr': _L0_ffn_in['Wr'], 'L0_ffn_br': _L0_ffn_in['br'], 'L0_ffn_gate_bias': _L0_ffn_in['gate_bias'], 'L0_ffn_Wup': _L0_ffn_in['Wup'], 'L0_ffn_bup': _L0_ffn_in['bup'], 'L0_ffn_Wgate': _L0_ffn_in['Wgate'], 'L0_ffn_bgate': _L0_ffn_in['bgate'], 'L0_ffn_Wdown': _L0_ffn_in['Wdown'], 'L0_ffn_bdown': _L0_ffn_in['bdown'], 'L0_ffn_Wsu': _L0_ffn_in['Wsu'], 'L0_ffn_bsu': _L0_ffn_in['bsu'], 'L0_ffn_Wsg': _L0_ffn_in['Wsg'], 'L0_ffn_bsg': _L0_ffn_in['bsg'], 'L0_ffn_Wsd': _L0_ffn_in['Wsd'], 'L0_ffn_bsd': _L0_ffn_in['bsd']}

def reference(x, ctx_1024, L0_xattn_Wq, L0_xattn_bq, L0_xattn_Wk, L0_xattn_bk, L0_xattn_Wv, L0_xattn_bv, L0_xattn_Wkv_dca, L0_xattn_bkv_dca, L0_xattn_qn_w, L0_xattn_qn_b, L0_xattn_kn_w, L0_xattn_kn_b, L0_xattn_kn_dca_w, L0_xattn_kn_dca_b, L0_xattn_Wo, L0_xattn_bo, L0_ffn_Wr, L0_ffn_br, L0_ffn_gate_bias, L0_ffn_Wup, L0_ffn_bup, L0_ffn_Wgate, L0_ffn_bgate, L0_ffn_Wdown, L0_ffn_bdown, L0_ffn_Wsu, L0_ffn_bsu, L0_ffn_Wsg, L0_ffn_bsg, L0_ffn_Wsd, L0_ffn_bsd):
    import jax
    import jax.numpy as jnp

    def _L0_xattn_ref(x, y, Wq, bq, Wk, bk, Wv, bv, Wkv_dca, bkv_dca, qn_w, qn_b, kn_w, kn_b, kn_dca_w, kn_dca_b, Wo, bo):
        import jax, jax.numpy as jnp
        import numpy as np
        B, S1, S2, DCA = (2, 512, 256, 16)
        QDIM, KDIM, H = (512, 256, 16)
        HD = QDIM // H
        SCALE = HD ** (-0.5)
        EPS = 1e-06
        DCA_WEIGHT = 1.0

        def _ln(t, w, b):
            m = jnp.mean(t, axis=-1, keepdims=True)
            v = jnp.var(t, axis=-1, keepdims=True)
            return (t - m) * jax.lax.rsqrt(v + EPS) * w + b

        def _attn(q, k, v):
            s = jnp.einsum('bhqd,bhkd->bhqk', q, k) * SCALE
            p = jax.nn.softmax(s, axis=-1)
            return jnp.einsum('bhqk,bhkd->bhqd', p, v)
        b, s1, _ = x.shape
        y_dca = y[:, -DCA:, :]
        y_main = y[:, :-DCA, :]
        kv_dca = (y_dca @ Wkv_dca + bkv_dca).reshape(b, DCA, 2, H, HD)
        k_dca = _ln(kv_dca[:, :, 0], kn_dca_w, kn_dca_b)
        v_dca = kv_dca[:, :, 1]
        s2 = y_main.shape[1]
        q = _ln((x @ Wq + bq).reshape(b, s1, H, HD), qn_w, qn_b)
        kv = jnp.concatenate([y_main @ Wk + bk, y_main @ Wv + bv], axis=-1)
        kv = kv.reshape(b, s2, H, 2 * HD)
        k = _ln(kv[..., :HD], kn_w, kn_b)
        v = kv[..., HD:]
        qT = q.transpose(0, 2, 1, 3)
        ctx = _attn(qT, k.transpose(0, 2, 1, 3), v.transpose(0, 2, 1, 3))
        ctx = ctx.transpose(0, 2, 1, 3).reshape(b, s1, QDIM)
        ctx_dca = _attn(qT, k_dca.transpose(0, 2, 1, 3), v_dca.transpose(0, 2, 1, 3))
        ctx_dca = ctx_dca.transpose(0, 2, 1, 3).reshape(b, s1, QDIM)
        ctx = ctx + DCA_WEIGHT * ctx_dca
        return ctx @ Wo + bo

    def _L0_ffn_ref(x, Wr, br, gate_bias, Wup, bup, Wgate, bgate, Wdown, bdown, Wsu, bsu, Wsg, bsg, Wsd, bsd):
        import jax, jax.numpy as jnp
        import numpy as np
        H = 512
        I = 512
        E_ROUTED = 7
        NS = 1
        TOPK = 2
        TEMP = 1.0

        def _moe_forward(x, Wr, br, gate_bias, Wup, bup, Wgate, bgate, Wdown, bdown, Wsu, bsu, Wsg, bsg, Wsd, bsd):
            B, S, _ = x.shape
            xt = x.reshape(-1, H)
            N = xt.shape[0]
            gate = (xt @ Wr + br) / TEMP
            bias_gate = gate + gate_bias
            _, ids = jax.lax.top_k(bias_gate, TOPK)
            sel_logits = jnp.take_along_axis(gate, ids, axis=-1)
            masked = jnp.full_like(gate, -jnp.inf)
            masked = masked.at[jnp.arange(N)[:, None], ids].set(sel_logits)
            probs = jax.nn.softmax(masked, axis=-1)
            u = jnp.einsum('nh,ehi->eni', xt, Wup) + bup[:, None, :]
            g = jax.nn.silu(jnp.einsum('eni,eij->enj', u, Wgate) + bgate[:, None, :]) * u
            eo = jnp.einsum('enj,ejh->enh', g, Wdown) + bdown[:, None, :]
            out = jnp.einsum('ne,enh->nh', probs, eo)
            su = (xt @ Wsu + bsu).reshape(N, NS, I)
            sg = jax.nn.silu(su @ Wsg + bsg) * su
            so = (sg @ Wsd + bsd).sum(axis=1)
            out = out + so
            return out.reshape(B, S, H)
        return _moe_forward(x, Wr, br, gate_bias, Wup, bup, Wgate, bgate, Wdown, bdown, Wsu, bsu, Wsg, bsg, Wsd, bsd)
    x = x + _L0_xattn_ref(_layernorm(x, axis=-1), ctx_1024, L0_xattn_Wq, L0_xattn_bq, L0_xattn_Wk, L0_xattn_bk, L0_xattn_Wv, L0_xattn_bv, L0_xattn_Wkv_dca, L0_xattn_bkv_dca, L0_xattn_qn_w, L0_xattn_qn_b, L0_xattn_kn_w, L0_xattn_kn_b, L0_xattn_kn_dca_w, L0_xattn_kn_dca_b, L0_xattn_Wo, L0_xattn_bo)
    x = x + _L0_ffn_ref(_layernorm(x, axis=-1), L0_ffn_Wr, L0_ffn_br, L0_ffn_gate_bias, L0_ffn_Wup, L0_ffn_bup, L0_ffn_Wgate, L0_ffn_bgate, L0_ffn_Wdown, L0_ffn_bdown, L0_ffn_Wsu, L0_ffn_bsu, L0_ffn_Wsg, L0_ffn_bsg, L0_ffn_Wsd, L0_ffn_bsd)
    return x

_drawn_inputs = setup_inputs


def setup_inputs(seed=0):
    import zlib

    import numpy as np

    out = dict(_drawn_inputs(seed))
    spreads = {'L0_xattn_bq': (0.0, 0.281),
     'L0_xattn_bk': (0.0, 0.1),
     'L0_xattn_bv': (0.0, 0.1),
     'L0_xattn_bkv_dca': (0.0, 0.1),
     'L0_xattn_qn_w': (1.0, 0.6),
     'L0_xattn_qn_b': (0.0, 0.513),
     'L0_xattn_kn_w': (1.0, 0.6),
     'L0_xattn_kn_b': (0.0, 0.8),
     'L0_xattn_kn_dca_w': (1.0, 0.2),
     'L0_xattn_kn_dca_b': (0.0, 0.8),
     'L0_xattn_bo': (0.0, 0.1),
     'L0_ffn_gate_bias': (0.0, 0.1)}
    factors = {'L0_ffn_bgate': 3.541}
    for name, (base, spread) in spreads.items():
        noise = np.random.default_rng([zlib.crc32(name.encode()), seed]).standard_normal(out[name].shape)
        drawn = base * np.exp(spread * noise) if base else spread * noise
        out[name] = jnp.asarray(drawn.astype(out[name].dtype))
    for name, factor in factors.items():
        out[name] = (out[name] * factor).astype(out[name].dtype)
    return out
```

```python
from contextlib import ExitStack

import numpy as np

import concourse.bass as bass
from concourse import mybir

F32 = mybir.dt.float32
F16 = mybir.dt.float16
I32 = mybir.dt.int32
U32 = mybir.dt.uint32
ALU = mybir.AluOpType
ACT = mybir.ActivationFunctionType
AX = mybir.AxisListType
ds = bass.ds

P = 128
B = 4
S = 512
D = 512
C = 256
H = 16
HD = D // H
NDCA = 16
NMAIN = S - NDCA
TB = S // P
NT = B * TB
KD = D // P
KC = C // P
CH = D // P
E = 7
NM = 3
TOP = 2
NBLK = (B * S * TOP + E * (P - 1)) // P
NSLOT = NBLK * P
WS = 16.0
QS = 32.0
LN_EPS = 1e-5
HEAD_EPS = 1e-6
VSEG = 5
VW = 2 * HD + 1
PAIR = 2
SBUF_LO, SBUF_HI = 16512, 229344


def at_least(eng, sem, value):
    if isinstance(value, int) and value <= 0:
        return
    eng.wait_ge(sem, value)


class Map:

    def __init__(self, nc, base, limit):
        self.nc, self.at, self.limit = nc, base, limit

    def __call__(self, name, shape, dt):
        size = int(np.prod(shape[1:])) * (2 if dt == F16 else 4)
        t = self.nc.alloc_sbuf_tensor_at(name, shape, dt, offset=self.at)
        self.at += -(-size // 32) * 32
        assert self.at <= self.limit, (name, self.at, self.limit)
        return t


def build(nc, t, out, upto=99, dbg=None):
    ctx = ExitStack()

    mine = []

    def sem(name):
        mine.append(nc.alloc_semaphore(name=name))
        return mine[-1]

    def end_stage():
        nc.clear_and_free_semaphores(mine)
        nc.all_engine_barrier()
        mine.clear()

    def dram(name, shape, dt):
        return nc.dram_tensor(name, shape, dt, kind="Internal").ap()

    with ctx:
        q_dram = dram("q_dram", (2, B * D, S), F16)
        k_dram = dram("k_dram", (2, B * D, S), F16)
        x1_dram = dram("x1_dram", (B * S, D), F32)
        xs_dram = dram("xs_dram", (NSLOT + B * S, D), F32)
        ys_dram = dram("ys_dram", (NSLOT, D), F32)

        W_BYTES = E * NM * 2 * KD * D * 2
        PER_E = W_BYTES // E
        w_exp = nc.alloc_sbuf_tensor_at("w_exp", [P, E, NM, 2, KD, D], F16, offset=SBUF_LO)
        V_BYTES = B * H * VSEG * VW * 2
        O_BYTES = B * H * TB * HD * 4
        CONST = 2624
        const = Map(nc, SBUF_HI - CONST, SBUF_HI)
        ident = const("ident", [P, P], F32)
        m_main = const("m_main", [P, 1], F32)
        m_dca = const("m_dca", [P, 1], F32)
        slot = const("slot", [P, TOP, NT], I32)
        prob = const("prob", [P, TOP, NT], F32)
        pmat = const("pmat", [P, NT, 3, E + 1], F32)
        blk_e = const("blk_e", [P, NBLK], I32)
        ws_tile = const("ws_tile", [P, 1], F32)
        seen = const("seen", [P, 1], F32)
        V_AT = (SBUF_HI - CONST - V_BYTES) // 32 * 32
        v_all = nc.alloc_sbuf_tensor_at("v_all", [P, B * H, VSEG, VW], F16, offset=V_AT)
        O_AT = V_AT - O_BYTES
        o_all = nc.alloc_sbuf_tensor_at("o_all", [P, TB, B * H, HD], F32, offset=O_AT)
        w_names = ("L0_ffn_Wup", "L0_ffn_Wgate", "L0_ffn_Wdown")
        s_dram = [t[n].rearrange("(k p) n -> p k n", p=P) for n in ("L0_ffn_Wsu", "L0_ffn_Wsg", "L0_ffn_Wsd")]
        w_dram = [t[n].rearrange("e (k p) n -> p (e k) n", p=P) for n in w_names]
        raw_free = sem("w_raw_free")
        w_scaled = sem("w_scaled")
        mine.clear()

        def load_matrix(sp, raw, loaded, e, m, n, half):
            sp.wait_ge(raw_free, 2 * n + half + 1)
            if sp is nc.gpsimd and not isinstance(n, int):
                sp.tensor_tensor(seen[:, :], ws_tile[:, :], ws_tile[:, :], ALU.add)
            src = s_dram[m][:, 2 * half:2 * half + 2, :] if e is None else w_dram[m][:, ds(e * KD + 2 * half, 2), :]
            sp.dma_start(raw[:, half], src).then_inc(loaded[half], 16)

        def split_matrix(pool, raw, loaded, since, e, m, n, half):
            e = 0 if e is None else e
            hi, lo = (w_exp[:, ds(e, 1), m, x, 2 * half:2 * half + 2, :].rearrange("p o k n -> p (o k n)") for x in range(2))
            w = raw[:, half].rearrange("p k n -> p (k n)")
            pool.wait_ge(loaded[half], 16 * (n - since) + 16)
            ws = ws_tile[:, :].broadcast_to([P, KD // 2 * D])
            pool.tensor_tensor(hi, w, ws, ALU.mult).then_inc(w_scaled, 1)
            pool.wait_ge(w_scaled, 4 * n + 2 * half + 1)
            pool.tensor_tensor(w, w, ws, ALU.mult).then_inc(w_scaled, 1)
            pool.wait_ge(w_scaled, 4 * n + 2 * half + 2)
            pool.tensor_tensor(lo, w, hi, ALU.subtract).then_inc(raw_free, 1)

        plan = dict(locals())
        project(nc, t, sem, plan)
        end_stage()
        if upto > 1:
            attend(nc, t, sem, plan)
        if upto > 2:
            output(nc, t, sem, plan)
            route(nc, t, sem, plan)
        if upto > 3:
            feed_forward(nc, t, sem, plan, False, out)
            feed_forward(nc, t, sem, plan, True, out)
        if dbg is not None:
            dbg(nc, plan, sem)


def project(nc, t, sem, g_):
    ident, v_all, m_main, m_dca = (g_[k] for k in ("ident", "v_all", "m_main", "m_dca"))
    q_dram, k_dram = g_["q_dram"], g_["k_dram"]
    sb = Map(nc, SBUF_LO, g_["V_AT"])
    wq_raw = sb("wq_raw", [P, KD, D], F32)
    wkv_raw = sb("wkv_raw", [P, KC, 2 * D], F32)
    wdca_raw = sb("wdca_raw", [P, KC, 2 * D], F32)
    wq = sb("wq", [P, 2, KD, D], F16)
    wkv = sb("wkv", [P, 2, KC, 2 * D], F16)
    wdca = sb("wdca", [P, 2, KC, 2 * D], F16)
    bq = sb("bq", [P, D], F32)
    bkv = sb("bkv", [P, 2, 2 * D], F32)
    wsum = sb("wsum", [P, KD + 2 * KC + 3, H], F32)
    affine = sb("affine", [P, 6], F32)
    affine_s = sb("affine_s", [P, 6], F32)
    x_in = sb("x_in", [P, 2, D], F32)
    c_in = sb("c_in", [P, 2, C], F32)
    st = sb("st", [P, 2, 6], F32)
    st_seen = sb("st_seen", [P, 1], F32)
    mv = sb("mv", [P, 2, 2], F32)
    ve = sb("ve", [P, 2, 1], F32)
    sd = sb("sd", [P, 2, 1], F32)
    rs = sb("rs", [P, 2, 1], F32)
    xn = sb("xn", [P, 2, D], F32)
    xT = sb("xT", [P, 2, 2, KD, P], F16)
    cT = sb("cT", [P, 2, 2, KC, P], F16)
    cTm = sb("cTm", [P, 2, KC, P], F16)
    cTd = sb("cTd", [P, 2, KC, P], F16)
    qf = sb("qf", [P, 2, D], F32)
    kf = sb("kf", [P, 2, D], F32)
    vf = sb("vf", [P, 2, D], F32)
    vm = sb("vm", [P, 2, D], F32)
    sq = sb("sq", [P, 2, D], F32)
    hv = sb("hv", [P, 2, 2 * H], F32)
    hs_ = sb("hs_", [P, 2, 2 * H], F32)
    hr = sb("hr", [P, 2, 2 * H], F32)
    qn = sb("qn", [P, D], F32)
    kn = sb("kn", [P, D], F32)
    qa = sb("qa", [P, CH, P], F32)
    ka = sb("ka", [P, CH, P], F32)
    q_st = sb("q_st", [P, 2, 2, CH, PAIR * P], F16)
    k_st = sb("k_st", [P, 2, 2, CH, PAIR * P], F16)

    names = """consts masks w_loaded b_loaded a_loaded w_sum w_cent b_cent w_hi w_lo aff
        stats aggr veps sd_r rs_r xn_r xT_t cT_t xT_h cT_h xT_l cT_l q_mm k_mm v_mm q_ev k_ev v_ev
        sq_r hv_s hv_r hs_r hr_r qn_r kn_r vm_r v_h v_l qT_t kT_t qa_r ka_r q_h k_h q_l k_l"""
    s = {n: sem("p_" + n) for n in names.split()}
    x_ld = [sem("p_x_loaded0"), sem("p_x_loaded1")]
    c_ld = [sem("p_c_loaded0"), sem("p_c_loaded1")]
    st_q = [sem("p_q_stored0"), sem("p_q_stored1")]
    st_k = [sem("p_k_stored0"), sem("p_k_stored1")]

    with ExitStack() as ps:
        def bank(name):
            return ps.enter_context(nc.psum_tensor(name, [P, 512], F32))
        psX, psC, psQ, psK, psV, psQT, psKT = (bank("p_" + n) for n in ("psX", "psC", "psQ", "psK", "psV", "psQT", "psKT"))
        block = ps.enter_context(nc.Block())

        def g_of(b, j):
            return b * TB + j

        def load(sp, b, j):
            if isinstance(b, int):
                b, j = b + j // TB, j % TB
            else:
                b, j = (b + 1, j - TB) if j >= TB else (b, j)
            g = g_of(b, j)
            at_least(sp, s["xn_r"], g - 1)
            sp.dma_start(x_in[:, j % 2], t["x"][b, j * P:(j + 1) * P, :] if isinstance(b, int)
                         else t["x"].rearrange("b s d -> (b s) d")[ds(g * P, P), :]).then_inc(x_ld[j % 2], 16)
            at_least(sp, s["cT_t"], g - 1)
            sp.dma_start(c_in[:, j % 2], t["ctx_1024"].rearrange("b s d -> (b s) d")[ds(g * P, P), :]).then_inc(c_ld[j % 2], 16)

        def store(sp, b, j):
            if j < 0:
                b, j = b - 1, j + TB
            g = g_of(b, j)
            slot = j // PAIR
            for buf, dst, hi, lo, done in ((q_st, q_dram, "q_h", "q_l", st_q), (k_st, k_dram, "k_h", "k_l", st_k)):
                sp.wait_ge(s[hi], g + 1)
                sp.wait_ge(s[lo], g + 1)
                for part in range(2):
                    d = dst[part, ds(b * D, D), slot * PAIR * P:(slot + 1) * PAIR * P]
                    sp.dma_start(d.rearrange("(c p) t -> p c t", p=P), buf[:, slot, part]).then_inc(done[slot], 16)

        def v_view(b, seg):
            return v_all[:, ds(b * H, H), seg, :]

        @block.sync
        def _(sp):
            sp.dma_start(wq_raw[:, :, :], t["L0_xattn_Wq"].rearrange("(k p) n -> p k n", p=P)).then_inc(s["w_loaded"], 16)
            for c in range(KC):
                for half, name in ((0, "L0_xattn_Wk"), (1, "L0_xattn_Wv")):
                    for kv in range(2):
                        src = t[name][c * P:(c + 1) * P, :].rearrange("p (h two d) -> p h two d", two=2, d=HD)[:, :, kv, :]
                        dst = wkv_raw[:, c, kv * D + half * C:kv * D + half * C + C].rearrange("p (h d) -> p h d", d=HD)
                        sp.dma_start(dst, src).then_inc(s["w_loaded"], 16)
            sp.dma_start(wdca_raw[:, :, :], t["L0_xattn_Wkv_dca"].rearrange("(k p) n -> p k n", p=P)).then_inc(s["w_loaded"], 16)
            for b, j in [(0, 0), (0, 1)]:
                load(sp, b, j)

            def steps(b, last):
                for j in range(TB):
                    if not (last and j >= TB - 2):
                        load(sp, b, j + 2)
                    if j % PAIR == 0 and not (isinstance(b, int) and b == 0 and j == 0):
                        store(sp, b, j - 1)
            steps(0, False)
            with sp.Fori(1, B - 1) as b:
                steps(b, False)
            steps(B - 1, True)
            store(sp, B - 1, TB - 1)
            for q in st_q + st_k:
                sp.wait_ge(q, 2 * 16 * NT // PAIR // 2)

        @block.gpsimd
        def _(pool):
            pool.memset(ident[:, :], 0.0).then_inc(s["consts"], 1)
            pool.memset(m_dca[:, :], 0.0).then_inc(s["consts"], 1)
            pool.memset(m_main[:, :], 1.0).then_inc(s["consts"], 1)
            pool.wait_ge(s["consts"], 3)
            pool.affine_select(out=ident[:, :], in_=ident[:, :], compare_op=ALU.not_equal, fill=1.0, base=0,
                               pattern=[[-1, P]], channel_multiplier=1).then_inc(s["masks"], 1)
            pool.affine_select(out=m_main[:, :], in_=m_main[:, :], compare_op=ALU.is_ge, fill=0.0, base=P - NDCA - 1,
                               pattern=[[0, 1]], channel_multiplier=-1).then_inc(s["masks"], 1)
            pool.affine_select(out=m_dca[:, :], in_=m_dca[:, :], compare_op=ALU.is_ge, fill=1.0, base=P - NDCA - 1,
                               pattern=[[0, 1]], channel_multiplier=-1).then_inc(s["masks"], 1)
            pool.memset(v_all[:, :, 0:3, HD:HD + 1], 1.0).then_inc(s["masks"], 1)
            pool.memset(cTm[:, :, :, :], 0.0).then_inc(s["masks"], 1)
            pool.memset(cTd[:, :, :, :], 0.0).then_inc(s["masks"], 1)

            def mid(b, j):
                g = g_of(b, j)
                pool.wait_ge(s["hr_r"], g + 1)
                for n, (src, dst, dn, free) in enumerate(((qf, qn, "qn_r", "qT_t"), (kf, kn, "kn_r", "kT_t"))):
                    at_least(pool, s[free], g)
                    r = hr[:, j % 2, n * H:(n + 1) * H].unsqueeze(2).broadcast_to([P, H, HD])
                    pool.tensor_tensor(dst[:, :].rearrange("p (h d) -> p h d", d=HD),
                                       src[:, j % 2].rearrange("p (h d) -> p h d", d=HD), r, ALU.mult).then_inc(s[dn], 1)
                if j < TB - 1:
                    pool.wait_ge(s["v_h"], b * (TB + 1) + j + 1)
                    v = v_view(b, j)
                    pool.tensor_tensor(v[:, :, HD + 1:], vf[:, j % 2].rearrange("p (h d) -> p h d", d=HD),
                                       v[:, :, 0:HD], ALU.subtract).then_inc(s["v_l"], 1)
                else:
                    for n in range(2):
                        pool.wait_ge(s["v_h"], b * (TB + 1) + j + 1 + n)
                        v = v_view(b, j + n)
                        pool.tensor_tensor(v[:, :, HD + 1:], vm[:, n].rearrange("p (h d) -> p h d", d=HD),
                                           v[:, :, 0:HD], ALU.subtract).then_inc(s["v_l"], 1)

            def back(b, j):
                g = g_of(b, j)
                for buf, src, hi, dn in ((q_st, qa, "q_h", "q_l"), (k_st, ka, "k_h", "k_l")):
                    pool.wait_ge(s[hi], g + 1)
                    c = (j % PAIR) * P
                    pool.tensor_tensor(buf[:, j // PAIR, 1, :, c:c + P], src[:, :, :],
                                       buf[:, j // PAIR, 0, :, c:c + P], ALU.subtract).then_inc(s[dn], 1)

            def steps(b, first):
                for j in range(TB):
                    mid(b, j)
                    if j:
                        back(b, j - 1)
                    elif not first:
                        back(b - 1, TB - 1)
            steps(0, True)
            with pool.Fori(1, B) as b:
                steps(b, False)
            back(B - 1, TB - 1)

        @block.scalar
        def _(act):
            act.dma_start(bq[:, :], t["L0_xattn_bq"].partition_broadcast(P)).then_inc(s["b_loaded"], 16)
            for v, kv in ((0, 0), (0, 1), (1, 0), (1, 1)):
                for half, name in ((0, "L0_xattn_bk"), (1, "L0_xattn_bv")):
                    src = t[name].rearrange("(h two d) -> h two d", two=2, d=HD)[:, kv, :]
                    n = P if v == 0 else P - NDCA
                    dst = bkv[0:n, v, kv * D + half * C:kv * D + half * C + C].rearrange("p (h d) -> p h d", d=HD)
                    act.dma_start(dst, src.partition_broadcast(n)).then_inc(s["b_loaded"], 16)
            act.dma_start(bkv[P - NDCA:P, 1, :], t["L0_xattn_bkv_dca"].partition_broadcast(NDCA)).then_inc(s["b_loaded"], 16)
            for n, name in enumerate(("qn_w", "qn_b", "kn_w", "kn_b", "kn_dca_w", "kn_dca_b")):
                for q in range(P // HD):
                    act.dma_start(affine[q * HD:(q + 1) * HD, n:n + 1],
                                  t["L0_xattn_" + name].rearrange("(d o) -> d o", o=1)).then_inc(s["a_loaded"], 16)
            act.wait_ge(s["w_cent"], 3)
            for n, (src, dst) in enumerate(((wq_raw, wq), (wkv_raw, wkv), (wdca_raw, wdca))):
                act.activation(dst[:, 0], src[:, :, :], ACT.Copy, scale=WS).then_inc(s["w_hi"], 1)

            def front(b, j):
                g = g_of(b, j)
                act.wait_ge(s["veps"], g + 1)
                act.activation(sd[:, j % 2], ve[:, j % 2], ACT.Sqrt).then_inc(s["sd_r"], 1)
                act.wait_ge(s["xT_t"], g + 1)
                at_least(act, s["q_mm"], g - 1)
                act.activation(xT[:, j % 2, 0], psX[:, :].rearrange("p (k n) -> p k n", n=P), ACT.Copy).then_inc(s["xT_h"], 1)
                act.wait_ge(s["cT_t"], g + 1)
                pc = psC[:, 0:C].rearrange("p (k n) -> p k n", n=P)
                if j < TB - 1:
                    at_least(act, s["v_mm"], g - 1)
                    act.activation(cT[:, j % 2, 0], pc, ACT.Copy).then_inc(s["cT_h"], 1)
                else:
                    at_least(act, s["v_mm"], g)
                    m = P - NDCA
                    act.activation(cTm[:, 0, :, 0:m], pc[:, :, 0:m], ACT.Copy)
                    act.activation(cTd[:, 0, :, m:P], pc[:, :, m:P], ACT.Copy).then_inc(s["cT_h"], 1)

            def mid(b, j):
                g = g_of(b, j)
                at_least(act, s["hv_s"], g)
                act.wait_ge(s["q_ev"], g + 1)
                act.activation(sq[:, 0], qf[:, j % 2], ACT.Square)
                act.wait_ge(s["k_ev"], g + 1)
                act.activation(sq[:, 1], kf[:, j % 2], ACT.Square).then_inc(s["sq_r"], 1)
                if j < TB - 1:
                    act.wait_ge(s["v_ev"], g + 1)
                    act.activation(v_view(b, j)[:, :, 0:HD], vf[:, j % 2].rearrange("p (h d) -> p h d", d=HD),
                                   ACT.Copy).then_inc(s["v_h"], 1)
                else:
                    for n in range(2):
                        act.wait_ge(s["vm_r"], 2 * b + n + 1)
                        act.activation(v_view(b, j + n)[:, :, 0:HD], vm[:, n].rearrange("p (h d) -> p h d", d=HD),
                                       ACT.Copy).then_inc(s["v_h"], 1)
                act.wait_ge(s["hv_r"], g + 1)
                act.activation(hs_[:, j % 2], hv[:, j % 2], ACT.Sqrt).then_inc(s["hs_r"], 1)

            def back(b, j):
                g = g_of(b, j)
                act.wait_ge(s["aff"], 1)
                gp = b * (TB // PAIR) + j // PAIR
                for buf, a, p_t, tt, dn, hi, lo, stored, w in (
                        (q_st, qa, psQT, "qT_t", "qa_r", "q_h", "q_l", st_q, 0),
                        (k_st, ka, psKT, "kT_t", "ka_r", "k_h", "k_l", st_k, 2)):
                    act.wait_ge(s[tt], g + 1)
                    at_least(act, s[lo], g)
                    pt = p_t[:, :].rearrange("p (c n) -> p c n", n=P)
                    m = P - NDCA if (w == 2 and j == TB - 1) else P
                    ins = act.activation(a[:, :, 0:m], pt[:, :, 0:m], ACT.Identity,
                                         scale=affine_s[:, w:w + 1], bias=affine_s[:, w + 1:w + 2])
                    if m < P:
                        ins = act.activation(a[:, :, m:P], pt[:, :, m:P], ACT.Identity,
                                             scale=affine_s[:, 4:5], bias=affine_s[:, 5:6])
                    ins.then_inc(s[dn], 1)
                    act.wait_ge(s[dn], g + 1)
                    if j % PAIR == 0:
                        at_least(act, stored[j // PAIR], 2 * 16 * b)
                    c = (j % PAIR) * P
                    act.activation(buf[:, j // PAIR, 0, :, c:c + P], a[:, :, :], ACT.Copy).then_inc(s[hi], 1)

            def steps(b, first, last):
                for j in range(TB):
                    if j < TB - 1:
                        front(b, j + 1)
                    elif not last:
                        front(b + 1, 0)
                    mid(b, j)
                    if j:
                        back(b, j - 1)
                    elif not first:
                        back(b - 1, TB - 1)
            front(0, 0)
            steps(0, True, False)
            with act.Fori(1, B - 1) as b:
                steps(b, False, False)
            steps(B - 1, False, True)
            back(B - 1, TB - 1)

        @block.vector
        def _(dve):
            dve.wait_ge(s["w_loaded"], 16 * (2 + 4 * KC))
            dve.wait_ge(s["b_loaded"], 16 * 10)
            dve.wait_ge(s["a_loaded"], 16 * 24)
            groups = [(wq_raw[:, :, :], KD), (wkv_raw[:, :, 0:D], KC), (wdca_raw[:, :, 0:D], KC),
                      (bq[:, :].rearrange("p (o n) -> p o n", o=1), 1), (bkv[:, :, 0:D], 2)]
            at = 0
            spans = []
            for v, n in groups:
                v4 = [v[:, i, :].rearrange("p (h d) -> p h d", d=HD) for i in range(n)]
                for x in v4:
                    dve.tensor_reduce(wsum[:, at, :], x, AX.X, ALU.add).then_inc(s["w_sum"], 1)
                    spans.append((x, at))
                    at += 1
            dve.wait_ge(s["w_sum"], at)
            done = {KD - 1: 1, KD + KC - 1: 1, KD + 2 * KC - 1: 1}
            for x, i in spans:
                ins = dve.scalar_tensor_tensor(x, wsum[:, i, :].unsqueeze(2).broadcast_to([P, H, HD]), -1.0 / HD, x,
                                               ALU.mult, ALU.add)
                if i in done:
                    ins.then_inc(s["w_cent"], 1)
                elif i == len(spans) - 1:
                    ins.then_inc(s["b_cent"], 1)
            dve.tensor_scalar(affine_s[:, :], affine[:, :], QS, None, ALU.mult).then_inc(s["aff"], 1)
            for n, (src, dst) in enumerate(((wq_raw, wq), (wkv_raw, wkv), (wdca_raw, wdca))):
                dve.wait_ge(s["w_hi"], n + 1)
                dve.scalar_tensor_tensor(dst[:, 1].rearrange("p k n -> p (k n)"), src[:, :, :].rearrange("p k n -> p (k n)"),
                                         WS, dst[:, 0].rearrange("p k n -> p (k n)"), ALU.mult, ALU.subtract).then_inc(s["w_lo"], 1)
            dve.wait_ge(s["masks"], 3)
            dve.tensor_copy(v_all[:, :, 3, HD:HD + 1], m_main[:, :].unsqueeze(1).broadcast_to([P, B * H, 1]))
            dve.tensor_copy(v_all[:, :, 4, HD:HD + 1], m_dca[:, :].unsqueeze(1).broadcast_to([P, B * H, 1]))

            def front_a(b, j):
                g = g_of(b, j)
                dve.wait_ge(x_ld[j % 2], 16 * (b * (TB // 2) + j // 2 + 1))
                dve.bn_stats(st[:, j % 2], x_in[:, j % 2]).then_inc(s["stats"], 1)
                dve.wait_ge(s["stats"], g + 1)
                dve.tensor_copy(st_seen[:, :], st[:, j % 2, 0:1])
                dve.bn_aggr(mv[:, j % 2], st[:, j % 2]).then_inc(s["aggr"], 1)
                dve.wait_ge(s["aggr"], g + 1)
                dve.tensor_scalar(ve[:, j % 2], mv[:, j % 2, 1:2], LN_EPS, None, ALU.add).then_inc(s["veps"], 1)

            def front_b(b, j):
                g = g_of(b, j)
                dve.wait_ge(s["sd_r"], g + 1)
                dve.reciprocal(rs[:, j % 2], sd[:, j % 2]).then_inc(s["rs_r"], 1)
                dve.wait_ge(s["rs_r"], g + 1)
                at_least(dve, s["xT_t"], g - 1)
                dve.tensor_scalar(xn[:, j % 2], x_in[:, j % 2], mv[:, j % 2, 0:1], rs[:, j % 2],
                                  ALU.subtract, ALU.mult).then_inc(s["xn_r"], 1)

            def front_c(b, j):
                g = g_of(b, j)
                dve.wait_ge(s["xT_h"], g + 1)
                dve.tensor_tensor(xT[:, j % 2, 1], psX[:, :].rearrange("p (k n) -> p k n", n=P), xT[:, j % 2, 0],
                                  ALU.subtract).then_inc(s["xT_l"], 1)
                dve.wait_ge(s["cT_h"], g + 1)
                pc = psC[:, 0:C].rearrange("p (k n) -> p k n", n=P)
                if j < TB - 1:
                    dve.tensor_tensor(cT[:, j % 2, 1], pc, cT[:, j % 2, 0], ALU.subtract).then_inc(s["cT_l"], 1)
                else:
                    m = P - NDCA
                    dve.wait_ge(s["masks"], 6)
                    dve.tensor_tensor(cTm[:, 1, :, 0:m], pc[:, :, 0:m], cTm[:, 0, :, 0:m], ALU.subtract)
                    dve.tensor_tensor(cTd[:, 1, :, m:P], pc[:, :, m:P], cTd[:, 0, :, m:P], ALU.subtract).then_inc(s["cT_l"], 1)

            def mid(b, j):
                g = g_of(b, j)
                dve.wait_ge(s["q_mm"], g + 1)
                at_least(dve, s["qn_r"], g - 1)
                dve.scalar_tensor_tensor(qf[:, j % 2], psQ[:, :], 1.0 / WS, bq[:, :], ALU.mult, ALU.add).then_inc(s["q_ev"], 1)
                var = 1 if j == TB - 1 else 0
                dve.wait_ge(s["k_mm"], g + 1)
                at_least(dve, s["kn_r"], g - 1)
                dve.scalar_tensor_tensor(kf[:, j % 2], psK[:, :], 1.0 / WS, bkv[:, var, 0:D], ALU.mult, ALU.add).then_inc(s["k_ev"], 1)
                dve.wait_ge(s["v_mm"], g + 1)
                at_least(dve, s["v_l"], b * (TB + 1) + j - 1)
                dve.scalar_tensor_tensor(vf[:, j % 2], psV[:, :], 1.0 / WS, bkv[:, var, D:2 * D], ALU.mult, ALU.add).then_inc(s["v_ev"], 1)
                if var:
                    dve.wait_ge(s["v_ev"], g + 1)
                    at_least(dve, s["v_l"], b * (TB + 1))
                    dve.tensor_scalar(vm[:, 0], vf[:, j % 2], m_main[:, :], None, ALU.mult).then_inc(s["vm_r"], 1)
                    dve.tensor_scalar(vm[:, 1], vf[:, j % 2], m_dca[:, :], None, ALU.mult).then_inc(s["vm_r"], 1)
                dve.wait_ge(s["sq_r"], g + 1)
                dve.tensor_reduce(hv[:, j % 2], sq[:, :, :].rearrange("p n (h d) -> p (n h) d", d=HD), AX.X, ALU.add).then_inc(s["hv_s"], 1)
                dve.wait_ge(s["hv_s"], g + 1)
                dve.tensor_scalar(hv[:, j % 2], hv[:, j % 2], 1.0 / HD, HEAD_EPS, ALU.mult, ALU.add).then_inc(s["hv_r"], 1)

            def mid_b(b, j):
                g = g_of(b, j)
                dve.wait_ge(s["hs_r"], g + 1)
                at_least(dve, s["kn_r"], g - 1)
                dve.reciprocal(hr[:, j % 2], hs_[:, j % 2]).then_inc(s["hr_r"], 1)

            def steps(b, first, last):
                for j in range(TB):
                    nxt = (b, j + 1) if j < TB - 1 else (b + 1, 0)
                    if not (last and j == TB - 1):
                        front_a(*nxt)
                        front_b(*nxt)
                        front_c(*nxt)
                    mid(b, j)
                    mid_b(b, j)
            front_a(0, 0)
            front_b(0, 0)
            front_c(0, 0)
            dve.wait_ge(s["b_cent"], 1)
            steps(0, True, False)
            with dve.Fori(1, B - 1) as b:
                steps(b, False, False)
            steps(B - 1, False, True)

        @block.tensor
        def _(pe):
            pe.wait_ge(s["masks"], 1)

            def front(b, j):
                g = g_of(b, j)
                pe.wait_ge(s["xn_r"], g + 1)
                at_least(pe, s["xT_l"], g)
                for c in range(KD):
                    ins = pe.transpose(psX[:, c * P:(c + 1) * P], xn[:, j % 2, c * P:(c + 1) * P], ident[:, :])
                ins.then_inc(s["xT_t"], 1)
                pe.wait_ge(c_ld[j % 2], 16 * (b * (TB // 2) + j // 2 + 1))
                at_least(pe, s["cT_l"], g)
                for c in range(KC):
                    ins = pe.transpose(psC[:, c * P:(c + 1) * P], c_in[:, j % 2, c * P:(c + 1) * P], ident[:, :])
                ins.then_inc(s["cT_t"], 1)

            def product(dst, terms):
                for n, (a, w) in enumerate(terms):
                    ins = pe.matmul(dst, a, w, start=(n == 0), stop=(n == len(terms) - 1))
                return ins

            def passes(a, w, cols, chunks):
                return [(a[:, x, c, :], w[:, y, c, cols]) for c in range(chunks) for x, y in ((0, 0), (1, 0), (0, 1))]

            def mid(b, j):
                g = g_of(b, j)
                pe.wait_ge(s["xT_l"], g + 1)
                pe.wait_ge(s["w_lo"], 3)
                at_least(pe, s["q_ev"], g)
                product(psQ[:, :], passes(xT[:, j % 2], wq, slice(0, D), KD)).then_inc(s["q_mm"], 1)
                pe.wait_ge(s["cT_l"], g + 1)
                for dst, ev, mm, cols in ((psK, "k_ev", "k_mm", slice(0, D)), (psV, "v_ev", "v_mm", slice(D, 2 * D))):
                    at_least(pe, s[ev], g)
                    if j < TB - 1:
                        terms = passes(cT[:, j % 2], wkv, cols, KC)
                    else:
                        terms = passes(cTm, wkv, cols, KC) + passes(cTd, wdca, cols, KC)
                    product(dst[:, :], terms).then_inc(s[mm], 1)

            def back(b, j):
                g = g_of(b, j)
                for src, dst, rdy, used, dn in ((qn, psQT, "qn_r", "qa_r", "qT_t"), (kn, psKT, "kn_r", "ka_r", "kT_t")):
                    pe.wait_ge(s[rdy], g + 1)
                    at_least(pe, s[used], g)
                    for c in range(CH):
                        ins = pe.transpose(dst[:, c * P:(c + 1) * P], src[:, c * P:(c + 1) * P], ident[:, :])
                    ins.then_inc(s[dn], 1)

            def steps(b, first, last):
                for j in range(TB):
                    nxt = (b, j + 1) if j < TB - 1 else (b + 1, 0)
                    if not (last and j == TB - 1):
                        front(*nxt)
                    mid(b, j)
                    if j:
                        back(b, j - 1)
                    elif not first:
                        back(b - 1, TB - 1)
            front(0, 0)
            steps(0, True, False)
            with pe.Fori(1, B - 1) as b:
                steps(b, False, False)
            steps(B - 1, False, True)
            back(B - 1, TB - 1)


E_EARLY = 3
SCALE = float(HD) ** -0.5


def attend(nc, t, sem, g_):
    ident, v_all, o_all = g_["ident"], g_["v_all"], g_["o_all"]
    q_dram, k_dram = g_["q_dram"], g_["k_dram"]
    N = B * H
    G = 4
    SLOTS = G
    K3 = 3 * HD
    KR = K3 + 2
    sb = Map(nc, SBUF_LO + E_EARLY * g_["PER_E"], g_["O_AT"])
    raw = sb("a_raw", [P, 2, 2, D], F32)
    q_stk = sb("q_stk", [P, SLOTS, S], F16)
    k_stk = sb("k_stk", [P, SLOTS, S], F16)
    nm = sb("nm", [P, 2, TB, 2], F32)
    pf = sb("pf", [P, TB, S], F32)
    ph = sb("ph", [P, 2, TB, S], F16)
    pl = sb("pl", [P, 2, TB, S], F16)
    oe = sb("oe", [P, 2, TB, 2, VW], F32)
    on = sb("on", [P, 2, TB, 2, HD], F32)
    orc = sb("orc", [P, 2, TB, 2, 1], F32)
    om = sb("om", [P, 2, TB, 2, HD], F32)
    zero = sb("zero", [P, D], F32)
    HI_ACT, LO_DVE = (0, 2), (0, 1)

    names = """zeroed sel max m_mm mrow s_mm t_mm exp o_mm o_ev h_act h_dve l_dve l_pool num rec mul out"""
    s = {n: sem("a_" + n) for n in names.split()}
    raw_ld = [sem("a_raw_loaded0"), sem("a_raw_loaded1")]
    loaded = [sem(f"a_stack_loaded{n}") for n in range(SLOTS)]

    with ExitStack() as ps:
        psS = ps.enter_context(nc.psum_tensor("a_psS", [P, 2, 512], F32))
        psT = ps.enter_context(nc.psum_tensor("a_psT", [P, 2, 512], F32))
        psO = ps.enter_context(nc.psum_tensor("a_psO", [P, 2, 512], F32))
        psM = ps.enter_context(nc.psum_tensor("a_psM", [P, 512], F32))
        block = ps.enter_context(nc.Block())

        def live(u, lag, end=N):
            return not isinstance(u, int) or lag <= u < end + lag

        def run(eng, step, tail, first=0, last=N // G):
            for j in range(G):
                step(j, j)
            with eng.Fori(1, N // G) as g:
                for j in range(G):
                    step(g * G + j, j)
            for j in range(tail):
                step(N + j, j % G)

        @block.sync
        def _(sp):
            def step(u, j, g):
                at_least(sp, s["t_mm"], TB * (u - 3) if not isinstance(u, int) else max(0, TB * (u - 3)))
                for n, (stk, dr, parts) in enumerate(((q_stk, q_dram, (0, 0, 1)), (k_stk, k_dram, (0, 1, 0)))):
                    for r, part in enumerate(parts):
                        sp.dma_start(stk[r * HD:(r + 1) * HD, j, :], dr[part, ds(u * HD, HD), :]).then_inc(loaded[j], 16)
            for j in range(G):
                step(j, j, 0)
            sp.wait_ge(g_["raw_free"], 2)
            sp.dma_start(g_["xs_dram"][0:NSLOT, :].rearrange("(n p) d -> p n d", p=P),
                         zero[:, :].unsqueeze(1).broadcast_to([P, NBLK, D])).then_inc(s["zeroed"], 16)
            for m in range(NM):
                with sp.Fori(1 + m * E_EARLY, 1 + (m + 1) * E_EARLY) as g:
                    for j in range(G):
                        step(g * G + j, j, g)
                        if j % 2 == 0:
                            g_["load_matrix"](sp, raw, raw_ld, g - (1 + m * E_EARLY), m, g - 1, j // 2)
            with sp.Fori(1 + NM * E_EARLY, N // G) as g:
                for j in range(G):
                    step(g * G + j, j, g)
            sp.wait_ge(s["zeroed"], 16)

        @block.gpsimd
        def _(pool):
            pool.memset(k_stk[K3:KR, :, :], QS).then_inc(s["sel"], 1)
            pool.wait_ge(s["sel"], 1)
            pool.memset(zero[:, :], 0.0).then_inc(g_["raw_free"], 1)
            pool.wait_ge(g_["raw_free"], 1)
            pool.memset(g_["ws_tile"][:, :], WS).then_inc(g_["raw_free"], 1)
            pool.wait_ge(g_["raw_free"], 2)
            sel = k_stk[K3:KR, :, :]
            pool.affine_select(out=sel, in_=sel, compare_op=ALU.is_ge, fill=0.0, base=NMAIN - 1,
                               pattern=[[0, SLOTS], [-1, S]], channel_multiplier=1000).then_inc(s["sel"], 1)
            pool.wait_ge(s["sel"], 2)
            pool.affine_select(out=sel, in_=sel, compare_op=ALU.is_ge, fill=0.0, base=1000 - NMAIN,
                               pattern=[[0, SLOTS], [1, S]], channel_multiplier=-1000).then_inc(s["sel"], 1)

            def step(u, j):
                if live(u, 1):
                    w = u - 1
                    sl = (j - 1) % 2
                    for n, k in enumerate(k for k in range(TB) if k not in LO_DVE):
                        if k in HI_ACT:
                            pool.wait_ge(s["h_act"], len(HI_ACT) * w + HI_ACT.index(k) + 1)
                        else:
                            pool.wait_ge(s["h_dve"], (TB - len(HI_ACT)) * w + [x for x in range(TB) if x not in HI_ACT].index(k) + 1)
                        pool.tensor_tensor(pl[:, sl, k], pf[:, k], ph[:, sl, k], ALU.subtract).then_inc(s["l_pool"], 1)
                if live(u, 3):
                    w = u - 3
                    sl = (j - 3) % 2
                    pool.wait_ge(s["rec"], w + 1)
                    pool.tensor_tensor(om[:, sl].rearrange("p q s d -> p (q s) d"), on[:, sl].rearrange("p q s d -> p (q s) d"),
                                       orc[:, sl].rearrange("p q s o -> p (q s) o").broadcast_to([P, TB * 2, HD]), ALU.mult).then_inc(s["mul"], 1)
                    pool.wait_ge(s["mul"], w + 1)
                    pool.tensor_tensor(o_all[:, :, ds(w, 1), :].rearrange("p q o d -> p (q o) d"), om[:, sl, :, 0, :], om[:, sl, :, 1, :], ALU.add).then_inc(s["out"], 1)
            for j in range(G):
                step(j, j)
            for m in range(NM):
                with pool.Fori(1 + m * E_EARLY, 1 + (m + 1) * E_EARLY) as g:
                    for j in range(G):
                        step(g * G + j, j)
                        if j % 2 == 1:
                            g_["split_matrix"](pool, raw, raw_ld, 0, g - (1 + m * E_EARLY), m, g - 1, j // 2)
            with pool.Fori(1 + NM * E_EARLY, N // G) as g:
                for j in range(G):
                    step(g * G + j, j)
            for j in range(3):
                step(N + j, j)

        @block.scalar
        def _(act):
            def exps(w, sl, k):
                act.wait_ge(s["t_mm"], TB * w + k + 1)
                if k in LO_DVE:
                    at_least(act, s["l_dve"], len(LO_DVE) * (w - 1) + LO_DVE.index(k) + 1)
                else:
                    at_least(act, s["l_pool"], 2 * (w - 1) + (k - 2) + 1)
                act.activation(pf[:, k], psT[:, k % 2], ACT.Exp, scale=SCALE / (QS * QS)).then_inc(s["exp"], 1)
                if k in HI_ACT:
                    act.wait_ge(s["exp"], TB * w + k + 1)
                    at_least(act, s["o_mm"], 2 * (w - 1))
                    act.activation(ph[:, sl, k], pf[:, k], ACT.Copy).then_inc(s["h_act"], 1)

            def evac(w, sl, p):
                act.wait_ge(s["o_mm"], 2 * w + p + 1)
                if p == 0:
                    at_least(act, s["rec"], w - 1)
                act.activation(oe[:, sl, 2 * p:2 * p + 2].rearrange("p q s v -> p (q s v)"), psO[:, p, 0:4 * VW], ACT.Copy).then_inc(s["o_ev"], 1)

            def step(u, j):
                if live(u, 3):
                    evac(u - 3, (j - 3) % 2, 1)
                if live(u, 1):
                    w = u - 1
                    act.wait_ge(s["m_mm"], w + 1)
                    act.activation(q_stk[K3:KR, (j - 1) % SLOTS, :], psM[0:2, :], ACT.Copy, scale=1.0 / QS).then_inc(s["mrow"], 1)
                    exps(w, (j - 1) % 2, 0)
                if live(u, 2):
                    evac(u - 2, (j - 2) % 2, 0)
                if live(u, 1):
                    for k in range(1, TB):
                        exps(u - 1, (j - 1) % 2, k)
            run(act, step, 4)

        @block.vector
        def _(dve):
            def maxima(u, j, p):
                sl = j % 2
                dve.wait_ge(s["s_mm"], 2 * u + p + 1)
                at_least(dve, s["m_mm"], u - 1)
                dve.tensor_reduce(nm[:, sl, 2 * p:2 * p + 2, 0:1].rearrange("p q o -> p (q o)"), psS[:, :, 0:NMAIN], AX.X, ALU.max, negate=True)
                dve.tensor_reduce(nm[:, sl, 2 * p:2 * p + 2, 1:2].rearrange("p q o -> p (q o)"), psS[:, :, NMAIN:S], AX.X, ALU.max, negate=True).then_inc(s["max"], 1)

            def hi(w, sl, k):
                dve.wait_ge(s["exp"], TB * w + k + 1)
                at_least(dve, s["o_mm"], 2 * (w - 1))
                dve.tensor_copy(ph[:, sl, k], pf[:, k]).then_inc(s["h_dve"], 1)

            def lo(w, sl, k):
                if k in HI_ACT:
                    dve.wait_ge(s["h_act"], len(HI_ACT) * w + HI_ACT.index(k) + 1)
                else:
                    dve.wait_ge(s["h_dve"], 2 * w + k // 2 + 1)
                dve.tensor_tensor(pl[:, sl, k], pf[:, k], ph[:, sl, k], ALU.subtract).then_inc(s["l_dve"], 1)

            def norm(w, sl):
                dve.wait_ge(s["o_ev"], 2 * w + 2)
                at_least(dve, s["mul"], w - 1)
                e = oe[:, sl].rearrange("p q s v -> p (q s) v")
                dve.tensor_tensor(on[:, sl].rearrange("p q s d -> p (q s) d"), e[:, :, 0:HD], e[:, :, HD + 1:], ALU.add)
                dve.reciprocal(orc[:, sl].rearrange("p q s o -> p (q s) o"), e[:, :, HD:HD + 1]).then_inc(s["rec"], 1)

            def step(u, j):
                if live(u, 0):
                    maxima(u, j, 0)
                if live(u, 3):
                    norm(u - 3, (j - 3) % 2)
                if live(u, 1):
                    w, sl = u - 1, (j - 1) % 2
                    lo(w, sl, 0)
                    hi(w, sl, 1)
                    lo(w, sl, 1)
                if live(u, 0):
                    maxima(u, j, 1)
                if live(u, 1):
                    hi(u - 1, (j - 1) % 2, 3)
            run(dve, step, 4)

        @block.tensor
        def _(pe):
            def scores(u, j, q):
                if q == 0:
                    pe.wait_ge(loaded[j], (u - j) * (6 * 16 // G) + 6 * 16)
                if q % 2 == 0:
                    at_least(pe, s["max"], 2 * u + q // 2)
                ins = pe.matmul(psS[:, q % 2], q_stk[0:K3, j, q * P:(q + 1) * P], k_stk[0:K3, j, :], start=True, stop=True)
                if q % 2:
                    ins.then_inc(s["s_mm"], 1)

            def max_rows(w, sl):
                pe.wait_ge(s["max"], 2 * w + 2)
                at_least(pe, s["mrow"], w)
                for q in range(TB):
                    ins = pe.transpose(psM[0:2, q * P:(q + 1) * P], nm[:, sl, q, :], ident[:, :])
                ins.then_inc(s["m_mm"], 1)

            def scores_t(w, j, k):
                if k == 0:
                    pe.wait_ge(s["mrow"], w + 1)
                    if isinstance(w, int) and w == 0:
                        pe.wait_ge(s["sel"], 3)
                at_least(pe, s["exp"], TB * w + k - 1)
                pe.matmul(psT[:, k % 2], k_stk[0:KR, j, k * P:(k + 1) * P], q_stk[0:KR, j, :], start=True, stop=True).then_inc(s["t_mm"], 1)

            def values(w, sl, q):
                if q == 0:
                    pe.wait_ge(s["h_act"], 2 * w + 2)
                    pe.wait_ge(s["h_dve"], 2 * w + 2)
                    pe.wait_ge(s["l_dve"], 2 * w + 2)
                    pe.wait_ge(s["l_pool"], 2 * w + 2)
                if q % 2 == 0:
                    at_least(pe, s["o_ev"], 2 * (w - 1) + q // 2 + 1)
                at = (q % 2) * 2 * VW
                c = slice(q * P, (q + 1) * P)
                for seg, keys in ((1, [TB - 1]), (0, range(TB))):
                    keys = list(keys)
                    dst = psO[:, q // 2, at + seg * VW:at + (seg + 1) * VW]
                    for k in keys:
                        v = v_all[:, ds(w, 1), k + seg, :].rearrange("p o v -> p (o v)")
                        pe.matmul(dst, ph[:, sl, k, c], v, start=(k == keys[0]), stop=False)
                        ins = pe.matmul(dst[:, 0:HD + 1], pl[:, sl, k, c], v[:, 0:HD + 1], start=False, stop=(k == keys[-1]))
                if q % 2:
                    ins.then_inc(s["o_mm"], 1)

            def step(u, j):
                s0, s1, s2 = live(u, 0), live(u, 1), live(u, 2)
                if s0:
                    scores(u, j, 0)
                    scores(u, j, 1)
                if s1:
                    max_rows(u - 1, (j - 1) % 2)
                if s2:
                    values(u - 2, j % 2, 0)
                    values(u - 2, j % 2, 1)
                for k in range(TB):
                    if s1:
                        scores_t(u - 1, (j - 1) % SLOTS, k)
                    if s0 and k % 2 == 0:
                        scores(u, j, 2 + k // 2)
                    if s2 and k % 2:
                        values(u - 2, j % 2, 2 + k // 2)
            run(pe, step, 2)


def output(nc, t, sem, g_):
    ident, o_all = g_["ident"], g_["o_all"]
    sb = Map(nc, SBUF_LO + E_EARLY * g_["PER_E"], g_["O_AT"])
    xn2 = g_["xn2"] = sb("xn2", [P, NT, D], F32)
    logits = g_["logits"] = sb("logits", [P, NT, E + 1], F32)
    low, sb = sb, Map(nc, g_["V_AT"], SBUF_HI - g_["CONST"])
    wo_raw = sb("wo_raw", [P, KD, D], F32)
    wo = sb("wo", [P, 2, KD, D], F16)
    wr = sb("wr", [P, KD, E], F32)
    bo = sb("bo", [P, D], F32)
    x_in = low("o_x", [P, 2, D], F32)
    xb = low("o_xb", [P, 2, D], F32)
    x1 = low("o_x1", [P, 2, D], F32)
    o_in = low("o_in", [P, 2, D], F32)
    xn = low("o_xn", [P, 2, D], F32)
    oT = sb("oT", [P, 2, 2, KD, P], F16)
    nT = sb("nT", [P, KD, P], F32)
    st = sb("o_st", [P, 2, 6], F32)
    st_seen = sb("o_st_seen", [P, 1], F32)
    mv = sb("o_mv", [P, 2, 2], F32)
    ve = sb("o_ve", [P, 2, 1], F32)
    sd = sb("o_sd", [P, 2, 1], F32)
    rs = sb("o_rs", [P, 2, 1], F32)
    names = """w_loaded w_hi w_lo b_loaded xb_r oT_t oT_h oT_l y_mm x1_r stats aggr veps sd_r rs_r xn_r nT_t nT_c r_mm logit"""
    s = {n: sem("o_" + n) for n in names.split()}
    x_ld = [sem("o_x_loaded0"), sem("o_x_loaded1")]
    o_ld = [sem("o_o_copied0"), sem("o_o_copied1")]
    x1_st = [sem("o_x1_stored0"), sem("o_x1_stored1")]
    xn_st = [sem("o_xn_stored0"), sem("o_xn_stored1")]

    with ExitStack() as ps:
        def bank(name):
            return ps.enter_context(nc.psum_tensor(name, [P, 512], F32))
        psX, psY, psN, psR = (bank("o_" + n) for n in ("psX", "psY", "psN", "psR"))
        block = ps.enter_context(nc.Block())

        def g_of(b, j):
            return b * TB + j

        def loop(eng, step):
            for j in range(TB):
                step(0, j, True, False)
            with eng.Fori(1, B - 1) as b:
                for j in range(TB):
                    step(b, j, False, False)
            for j in range(TB):
                step(B - 1, j, False, True)

        @block.sync
        def _(sp):
            sp.dma_start(wo_raw[:, :, :], t["L0_xattn_Wo"].rearrange("(k p) n -> p k n", p=P)).then_inc(s["w_loaded"], 16)
            sp.dma_start(wr[:, :, :], t["L0_ffn_Wr"].rearrange("(k p) n -> p k n", p=P)).then_inc(s["b_loaded"], 16)
            sp.dma_start(bo[:, :], t["L0_xattn_bo"].partition_broadcast(P)).then_inc(s["b_loaded"], 16)
            x_rows = t["x"].rearrange("b s d -> (b s) d")

            def load(b, j):
                b, j = (b + 1, j - TB) if j >= TB else (b, j)
                g = g_of(b, j)
                at_least(sp, s["xb_r"], g - 1)
                sp.dma_start(x_in[:, j % 2], x_rows[ds(g * P, P), :]).then_inc(x_ld[j % 2], 16)
                at_least(sp, s["oT_t"], g - 1)
                sp.dma_start(o_in[:, j % 2], o_all[:, j % TB, ds(b * H, H), :].rearrange("p h d -> p (h d)")).then_inc(o_ld[j % 2], 16)
            load(0, 0)
            load(0, 1)

            def step(b, j, first, last):
                g = g_of(b, j)
                if not (last and j >= TB - 2):
                    load(b, j + 2)
                sp.wait_ge(s["x1_r"], g + 1)
                sp.dma_start(g_["x1_dram"][ds(g * P, P), :], x1[:, j % 2]).then_inc(x1_st[j % 2], 16)
                sp.wait_ge(s["xn_r"], g + 1)
                sp.dma_start(g_["xs_dram"][ds(NSLOT + g * P, P), :], xn[:, j % 2]).then_inc(xn_st[j % 2], 16)
                sp.dma_start(xn2[:, ds(g, 1), :].rearrange("p o d -> p (o d)"), xn[:, j % 2]).then_inc(xn_st[j % 2], 16)
            loop(sp, step)
            for q in x1_st:
                sp.wait_ge(q, 8 * NT)
            for q in xn_st:
                sp.wait_ge(q, 16 * NT)

        @block.gpsimd
        def _(pool):
            pool.wait_ge(s["b_loaded"], 32)

            def step(b, j, first, last):
                g = g_of(b, j)
                pool.wait_ge(x_ld[j % 2], 16 * (b * (TB // 2) + j // 2 + 1))
                at_least(pool, s["x1_r"], g - 1)
                pool.tensor_tensor(xb[:, j % 2], x_in[:, j % 2], bo[:, :], ALU.add).then_inc(s["xb_r"], 1)
            loop(pool, step)

        @block.scalar
        def _(act):
            act.wait_ge(s["w_loaded"], 16)
            act.activation(wo[:, 0], wo_raw[:, :, :], ACT.Copy, scale=WS).then_inc(s["w_hi"], 1)

            def front(b, j):
                g = g_of(b, j)
                act.wait_ge(s["oT_t"], g + 1)
                at_least(act, s["y_mm"], g - 1)
                act.activation(oT[:, j % 2, 0], psX[:, :].rearrange("p (k n) -> p k n", n=P), ACT.Copy).then_inc(s["oT_h"], 1)

            def back(b, j):
                g = g_of(b, j)
                act.wait_ge(s["nT_t"], g + 1)
                at_least(act, s["r_mm"], g)
                act.activation(nT[:, :, :], psN[:, :].rearrange("p (k n) -> p k n", n=P), ACT.Copy).then_inc(s["nT_c"], 1)

            def step(b, j, first, last):
                g = g_of(b, j)
                if not (last and j == TB - 1):
                    front(*((b, j + 1) if j < TB - 1 else (b + 1, 0)))
                act.wait_ge(s["veps"], g + 1)
                act.activation(sd[:, j % 2], ve[:, j % 2], ACT.Sqrt).then_inc(s["sd_r"], 1)
                if not (first and j == 0):
                    back(*((b, j - 1) if j else (b - 1, TB - 1)))
            front(0, 0)
            loop(act, step)
            back(B - 1, TB - 1)

        @block.vector
        def _(dve):
            dve.wait_ge(s["w_hi"], 1)
            dve.scalar_tensor_tensor(wo[:, 1].rearrange("p k n -> p (k n)"), wo_raw[:, :, :].rearrange("p k n -> p (k n)"),
                                     WS, wo[:, 0].rearrange("p k n -> p (k n)"), ALU.mult, ALU.subtract).then_inc(s["w_lo"], 1)

            def front(b, j):
                g = g_of(b, j)
                dve.wait_ge(s["oT_h"], g + 1)
                dve.tensor_tensor(oT[:, j % 2, 1], psX[:, :].rearrange("p (k n) -> p k n", n=P), oT[:, j % 2, 0],
                                  ALU.subtract).then_inc(s["oT_l"], 1)

            def step(b, j, first, last):
                g = g_of(b, j)
                if not (last and j == TB - 1):
                    front(*((b, j + 1) if j < TB - 1 else (b + 1, 0)))
                dve.wait_ge(s["y_mm"], g + 1)
                dve.wait_ge(s["xb_r"], g + 1)
                at_least(dve, x1_st[j % 2], (b * (TB // 2) + j // 2) * 16)
                dve.scalar_tensor_tensor(x1[:, j % 2], psY[:, :], 1.0 / WS, xb[:, j % 2], ALU.mult, ALU.add).then_inc(s["x1_r"], 1)
                dve.wait_ge(s["x1_r"], g + 1)
                dve.bn_stats(st[:, j % 2], x1[:, j % 2]).then_inc(s["stats"], 1)
                dve.wait_ge(s["stats"], g + 1)
                dve.tensor_copy(st_seen[:, :], st[:, j % 2, 0:1])
                dve.bn_aggr(mv[:, j % 2], st[:, j % 2]).then_inc(s["aggr"], 1)
                dve.wait_ge(s["aggr"], g + 1)
                dve.tensor_scalar(ve[:, j % 2], mv[:, j % 2, 1:2], LN_EPS, None, ALU.add).then_inc(s["veps"], 1)
                dve.wait_ge(s["sd_r"], g + 1)
                dve.reciprocal(rs[:, j % 2], sd[:, j % 2]).then_inc(s["rs_r"], 1)
                dve.wait_ge(s["rs_r"], g + 1)
                at_least(dve, xn_st[j % 2], (b * (TB // 2) + j // 2) * 32)
                at_least(dve, s["nT_t"], g - 1)
                dve.tensor_scalar(xn[:, j % 2], x1[:, j % 2], mv[:, j % 2, 0:1], rs[:, j % 2],
                                  ALU.subtract, ALU.mult).then_inc(s["xn_r"], 1)
            front(0, 0)
            loop(dve, step)
            dve.wait_ge(s["r_mm"], NT)
            dve.tensor_copy(logits[:, :, 0:E], psR[:, 0:NT * (E + 1)].rearrange("p (n e) -> p n e", e=E + 1)[:, :, 0:E]).then_inc(s["logit"], 1)

        @block.tensor
        def _(pe):
            def front(b, j):
                g = g_of(b, j)
                pe.wait_ge(o_ld[j % 2], 16 * (b * (TB // 2) + j // 2 + 1))
                at_least(pe, s["oT_l"], g)
                for c in range(KD):
                    ins = pe.transpose(psX[:, c * P:(c + 1) * P], o_in[:, j % 2, c * P:(c + 1) * P], ident[:, :])
                ins.then_inc(s["oT_t"], 1)

            def back(b, j):
                g = g_of(b, j)
                pe.wait_ge(s["xn_r"], g + 1)
                at_least(pe, s["nT_c"], g)
                for c in range(KD):
                    ins = pe.transpose(psN[:, c * P:(c + 1) * P], xn[:, j % 2, c * P:(c + 1) * P], ident[:, :])
                ins.then_inc(s["nT_t"], 1)

            def router(b, j):
                g = g_of(b, j)
                pe.wait_ge(s["nT_c"], g + 1)
                for c in range(KD):
                    ins = pe.matmul(psR[:, ds(g * (E + 1), E)], nT[:, c, :], wr[:, c, :], start=(c == 0), stop=(c == KD - 1))
                ins.then_inc(s["r_mm"], 1)

            pe.wait_ge(s["w_lo"], 1)
            pe.wait_ge(s["b_loaded"], 32)

            def step(b, j, first, last):
                g = g_of(b, j)
                before = None if first and j == 0 else ((b, j - 1) if j else (b - 1, TB - 1))
                if not (last and j == TB - 1):
                    front(*((b, j + 1) if j < TB - 1 else (b + 1, 0)))
                if before:
                    back(*before)
                pe.wait_ge(s["oT_l"], g + 1)
                at_least(pe, s["x1_r"], g)
                n = 0
                for c in range(KD):
                    for x, y in ((0, 0), (1, 0), (0, 1)):
                        ins = pe.matmul(psY[:, :], oT[:, j % 2, x, c, :], wo[:, y, c, :], start=(n == 0), stop=(n == 3 * KD - 1))
                        n += 1
                ins.then_inc(s["y_mm"], 1)
                if before:
                    router(*before)
            front(0, 0)
            loop(pe, step)
            back(B - 1, TB - 1)
            router(B - 1, TB - 1)


def route(nc, t, sem, g_):
    xn2, logits, slot, prob, pmat, blk_e = (g_[k] for k in ("xn2", "logits", "slot", "prob", "pmat", "blk_e"))
    sb = Map(nc, SBUF_LO + E_EARLY * g_["PER_E"] + (NT * D + NT * (E + 1)) * 4, g_["V_AT"])
    R = [P, NT, E]
    br = sb("br", [P, E], F32)
    gb = sb("gb", [P, E], F32)
    tri = sb("tri", [P, P], F32)
    ones = sb("ones", [P, P], F32)
    ramp_i = sb("ramp_i", [P, E], I32)
    ramp = sb("ramp", [P, E], F32)
    bidx_i = sb("bidx_i", [P, NBLK], I32)
    bidx = sb("bidx", [P, NBLK], F32)
    lg, bg, eq, cand, prod, member, within, tile_n, scan_a, scan_b, place = (
        sb("r_" + n, R, F32) for n in "lg bg eq cand prod member within tile_n scan_a scan_b place".split())
    oh = [sb(f"oh{k}", R, F32) for k in range(TOP)]
    top = sb("top", [P, NT], F32)
    sel = sb("sel_l", [P, TOP, NT], F32)
    mx = sb("r_mx", [P, NT], F32)
    ex = sb("r_ex", [P, TOP, NT], F32)
    den = sb("r_den", [P, NT], F32)
    ph16 = sb("ph16", [P, NT, E + 1], F16)
    cnt_i = sb("cnt_i", [P, E], I32)
    nblk = sb("nblk", [P, E], F32)
    cum_a = sb("cum_a", [P, E], F32)
    cum_b = sb("cum_b", [P, E], F32)
    base = sb("base", [P, E], F32)
    slot_f = sb("slot_f", [P, TOP, NT], F32)
    cmpb = sb("cmpb", [P, NBLK, E - 1], F32)
    blk_f = sb("blk_f", [P, NBLK], F32)
    names = "loaded const0 const1 iota member prefix exp_in exp slots scattered"
    s = {n: sem("r_" + n) for n in names.split()}
    dve_step = sem("r_dve_step")

    def over_tiles(x):
        return x.unsqueeze(1).broadcast_to(R)

    def over_experts(x):
        return x.unsqueeze(2).broadcast_to(R)

    with ExitStack() as ps:
        psW = ps.enter_context(nc.psum_tensor("r_psW", [P, 512], F32))
        psN = ps.enter_context(nc.psum_tensor("r_psN", [P, 512], F32))
        block = ps.enter_context(nc.Block())

        @block.sync
        def _(sp):
            sp.dma_start(br[:, :], t["L0_ffn_br"].partition_broadcast(P)).then_inc(s["loaded"], 16)
            sp.dma_start(gb[:, :], t["L0_ffn_gate_bias"].partition_broadcast(P)).then_inc(s["loaded"], 16)

        @block.gpsimd
        def _(pool):
            pool.memset(tri[:, :], 1.0).then_inc(s["const0"], 1)
            pool.memset(ones[:, :], 1.0).then_inc(s["const1"], 1)
            pool.iota(ramp_i[:, :], pattern=[[-1, E]], base=E, channel_multiplier=0).then_inc(s["iota"], 1)
            pool.iota(bidx_i[:, :], pattern=[[1, NBLK]], base=0, channel_multiplier=0).then_inc(s["iota"], 1)
            pool.wait_ge(s["const0"], 1)
            pool.affine_select(out=tri[:, :], in_=tri[:, :], compare_op=ALU.is_ge, fill=0.0, base=-1,
                               pattern=[[1, P]], channel_multiplier=-1).then_inc(s["const1"], 1)
            pool.wait_ge(s["slots"], 1)
            for k in range(TOP):
                for g in range(NT):
                    pool.indirect_dma_start(g_["xs_dram"][0:NSLOT, :], bass.IndirectOffsetOnAxis(ap=slot[:, k, g:g + 1], axis=0),
                                            xn2[:, g, :], None).then_inc(s["scattered"], 16)
            pool.wait_ge(s["scattered"], 16 * TOP * NT)

        @block.tensor
        def _(pe):
            pe.wait_ge(s["const1"], 2)
            pe.wait_ge(s["member"], 1)
            m = member[:, :, :].rearrange("p n e -> p (n e)")
            pe.matmul(psW[:, 0:NT * E], tri[:, :], m, start=True, stop=True)
            pe.matmul(psN[:, 0:NT * E], ones[:, :], m, start=True, stop=True).then_inc(s["prefix"], 1)

        @block.scalar
        def _(act):
            act.wait_ge(s["exp_in"], 1)
            act.activation(ex[:, :, :], sel[:, :, :], ACT.Exp).then_inc(s["exp"], 1)

        @block.vector
        def _(dve):
            n = [0]

            def link(ins):
                n[0] += 1
                ins.then_inc(dve_step, 1)
                dve.wait_ge(dve_step, n[0])

            dve.wait_ge(s["iota"], 2)
            link(dve.tensor_copy(ramp[:, :], ramp_i[:, :]))
            link(dve.tensor_copy(bidx[:, :], bidx_i[:, :]))
            dve.wait_ge(s["loaded"], 32)
            link(dve.tensor_tensor(lg[:, :, :], logits[:, :, 0:E], over_tiles(br[:, :]), ALU.add))
            link(dve.tensor_tensor(bg[:, :, :], lg[:, :, :], over_tiles(gb[:, :]), ALU.add))
            for k in range(TOP):
                link(dve.tensor_reduce(top[:, :], bg[:, :, :], AX.X, ALU.max))
                link(dve.tensor_tensor(eq[:, :, :], bg[:, :, :], over_experts(top[:, :]), ALU.is_equal))
                link(dve.tensor_tensor(cand[:, :, :], eq[:, :, :], over_tiles(ramp[:, :]), ALU.mult))
                link(dve.tensor_reduce(top[:, :], cand[:, :, :], AX.X, ALU.max))
                link(dve.tensor_tensor(oh[k][:, :, :], cand[:, :, :], over_experts(top[:, :]), ALU.is_equal))
                link(dve.tensor_tensor(prod[:, :, :], lg[:, :, :], oh[k][:, :, :], ALU.mult))
                link(dve.tensor_reduce(sel[:, k, :], prod[:, :, :], AX.X, ALU.add))
                if k == 0:
                    link(dve.scalar_tensor_tensor(bg[:, :, :], oh[0][:, :, :], -3.0e38, bg[:, :, :], ALU.mult, ALU.add))
            dve.tensor_tensor(member[:, :, :], oh[0][:, :, :], oh[1][:, :, :], ALU.add).then_inc(s["member"], 1)
            link(dve.tensor_tensor(mx[:, :], sel[:, 0, :], sel[:, 1, :], ALU.max))
            for k in range(TOP):
                ins = dve.tensor_tensor(sel[:, k, :], sel[:, k, :], mx[:, :], ALU.subtract)
                link(ins)
            dve.tensor_copy(den[:, :], mx[:, :]).then_inc(s["exp_in"], 1)
            dve.wait_ge(s["prefix"], 1)
            link(dve.tensor_copy(within[:, :, :], psW[:, 0:NT * E].rearrange("p (n e) -> p n e", e=E)))
            link(dve.tensor_copy(tile_n[:, :, :], psN[:, 0:NT * E].rearrange("p (n e) -> p n e", e=E)))
            src, dst = tile_n, scan_a
            step = 1
            while step < NT:
                link(dve.tensor_copy(dst[:, 0:step, :], src[:, 0:step, :]))
                link(dve.tensor_tensor(dst[:, step:NT, :], src[:, step:NT, :], src[:, 0:NT - step, :], ALU.add))
                src, dst = dst, (scan_b if dst is scan_a else scan_a)
                step *= 2
            incl = src
            link(dve.tensor_scalar(base[:, :], incl[:, NT - 1, :], float(P - 1), None, ALU.add))
            link(dve.tensor_copy(cnt_i[:, :], base[:, :]))
            link(dve.tensor_scalar(cnt_i[:, :], cnt_i[:, :], 7, None, ALU.logical_shift_right))
            link(dve.tensor_copy(nblk[:, :], cnt_i[:, :]))
            src2, dst2 = nblk, cum_a
            step = 1
            while step < E:
                link(dve.tensor_copy(dst2[:, 0:step], src2[:, 0:step]))
                link(dve.tensor_tensor(dst2[:, step:E], src2[:, step:E], src2[:, 0:E - step], ALU.add))
                src2, dst2 = dst2, (cum_b if dst2 is cum_a else cum_a)
                step *= 2
            cum = src2
            link(dve.tensor_tensor(base[:, :], cum[:, :], nblk[:, :], ALU.subtract))
            link(dve.tensor_tensor(place[:, :, :], within[:, :, :], incl[:, :, :], ALU.add))
            link(dve.tensor_tensor(place[:, :, :], place[:, :, :], tile_n[:, :, :], ALU.subtract))
            link(dve.scalar_tensor_tensor(place[:, :, :], over_tiles(base[:, :]), float(P), place[:, :, :], ALU.mult, ALU.add))
            for k in range(TOP):
                link(dve.tensor_tensor(prod[:, :, :], place[:, :, :], oh[k][:, :, :], ALU.mult))
                link(dve.tensor_reduce(slot_f[:, k, :], prod[:, :, :], AX.X, ALU.add))
            dve.tensor_copy(slot[:, :, :], slot_f[:, :, :]).then_inc(s["slots"], 1)
            link(dve.tensor_tensor(cmpb[:, :, :], bidx[:, :].unsqueeze(2).broadcast_to([P, NBLK, E - 1]),
                                   cum[:, 0:E - 1].unsqueeze(1).broadcast_to([P, NBLK, E - 1]), ALU.is_ge))
            link(dve.tensor_reduce(blk_f[:, :], cmpb[:, :, :], AX.X, ALU.add))
            link(dve.tensor_copy(blk_e[:, :], blk_f[:, :]))
            dve.wait_ge(s["exp"], 1)
            link(dve.tensor_tensor(den[:, :], ex[:, 0, :], ex[:, 1, :], ALU.add))
            link(dve.reciprocal(den[:, :], den[:, :]))
            for k in range(TOP):
                link(dve.tensor_tensor(prob[:, k, :], ex[:, k, :], den[:, :], ALU.mult))
            link(dve.tensor_tensor(eq[:, :, :], oh[0][:, :, :], over_experts(prob[:, 0, :]), ALU.mult))
            link(dve.tensor_tensor(cand[:, :, :], oh[1][:, :, :], over_experts(prob[:, 1, :]), ALU.mult))
            link(dve.tensor_tensor(pmat[:, :, 1, 0:E], eq[:, :, :], cand[:, :, :], ALU.add))
            link(dve.memset(pmat[:, :, 1, E:E + 1], 1.0))
            link(dve.tensor_copy(ph16[:, :, :], pmat[:, :, 1, :]))
            link(dve.tensor_copy(pmat[:, :, 0, :], ph16[:, :, :]))
            link(dve.tensor_copy(pmat[:, :, 2, :], ph16[:, :, :]))
            link(dve.tensor_tensor(pmat[:, :, 1, :], pmat[:, :, 1, :], ph16[:, :, :], ALU.subtract))


def feed_forward(nc, t, sem, g_, shared, out):
    ident, w_exp, blk_e, slot, prob, pmat = (g_[k] for k in ("ident", "w_exp", "blk_e", "slot", "prob", "pmat"))
    tag = "s_" if shared else "e_"
    N = NT if shared else NBLK
    ROW0 = NSLOT if shared else 0
    sb = Map(nc, SBUF_LO + (1 if shared else E) * g_["PER_E"], SBUF_HI - g_["CONST"])
    NB = 1 if shared else E
    bias_u = sb(tag + "bias_u", [P, NB, KD], F32)
    bias_g = sb(tag + "bias_g", [P, NB, KD], F32)
    x_in = sb(tag + "x", [P, 2, D], F32)
    xT = sb(tag + "xT", [P, 2, 2, KD, P], F16)
    u = sb(tag + "u", [P, 2, KD, P], F32)
    uT = sb(tag + "uT", [P, 2, KD, P], F16)
    h = sb(tag + "h", [P, KD, P], F32)
    sl = sb(tag + "silu", [P, KD, P], F32)
    gf = sb(tag + "g", [P, KD, P], F32)
    gT = sb(tag + "gT", [P, 2, 2, KD, P], F16)
    y = sb(tag + "y", [P, 2, D], F32)
    if shared:
        x1 = sb("s_x1", [P, 2, D], F32)
        ya = sb("s_ya", [P, 2, TOP, D], F32)
        acc = sb("s_acc", [P, 2, D], F32)
        K3 = 3 * (E + 1)
        bd_raw = sb("bd_raw", [K3, D], F32)
        bd_16 = sb("bd_16", [K3, D], F32)
        bd_hi = sb("bd_hi", [K3, D], F16)
        bd = sb("bd", [K3, D], F16)
        low = sb("low", [K3, 1], F32)
        pT = sb("pT", [K3, NT, P], F16)
    else:
        raw = sb("e_raw", [P, 2, 2, D], F32)
    names = """b_loaded xT_t xT_h xT_l u_mm u_r u_h u_l g_mm h_r silu g_r g_h g_l y_mm y_r
        acc0 acc1 bd0 bd1 low pT_t pT_c"""
    s = {n: sem(tag + n) for n in names.split()}
    x_ld = [sem(tag + "x_loaded0"), sem(tag + "x_loaded1")]
    raw_ld = [sem(tag + "raw_loaded0"), sem(tag + "raw_loaded1")]
    x1_ld = [sem(tag + "x1_loaded0"), sem(tag + "x1_loaded1")]
    ga = [sem(tag + "gathered0"), sem(tag + "gathered1")]
    y_st = [sem(tag + "y_stored0"), sem(tag + "y_stored1")]

    def live(n, lag):
        return not isinstance(n, int) or 0 <= n - lag < N

    def run(eng, step, extra=0):
        step(0, 0, 0)
        step(1, 1, 0)
        with eng.Fori(1, N // 2 - 1) as i:
            step(i * 2, 0, i)
            step(i * 2 + 1, 1, i)
        step(N - 2, 0, N // 2 - 1)
        step(N - 1, 1, N // 2 - 1)
        for j in range(extra):
            step(N + j, j, N // 2)

    def before(i, j):
        return i - 1 if j == 0 else i

    def after(i, j):
        return i if j == 0 else i + 1

    with ExitStack() as ps:
        def bank(name):
            return ps.enter_context(nc.psum_tensor(tag + name, [P, 512], F32))
        psX, psU, psG, psY, psP = (bank(n) for n in ("psX", "psU", "psG", "psY", "psP"))
        block = ps.enter_context(nc.Block())

        @block.sync
        def _(sp):
            def load(n, j):
                at_least(sp, s["xT_t"], n - 1)
                sp.dma_start(x_in[:, j % 2], g_["xs_dram"][ds(n * P + ROW0, P), :]).then_inc(x_ld[j % 2], 16)
                if shared:
                    at_least(sp, s["acc0"], n - 1)
                    sp.dma_start(x1[:, j % 2], g_["x1_dram"][ds(n * P, P), :]).then_inc(x1_ld[j % 2], 16)

            dst = out.rearrange("b s d -> (b s) d") if shared else g_["ys_dram"]

            def step(n, j, i):
                if isinstance(n, int):
                    if n + 2 < N:
                        load(n + 2, j)
                else:
                    load(n + 2, j)
                if live(n, 1):
                    sp.wait_ge(s["y_r"], n)
                    sp.dma_start(dst[ds((n - 1) * P, P), :], y[:, (j - 1) % 2]).then_inc(y_st[(j - 1) % 2], 16)
            load(0, 0)
            load(1, 1)
            run(sp, step, 1)
            for q in y_st:
                sp.wait_ge(q, 8 * N)

        @block.gpsimd
        def _(pool):
            if shared:
                pool.memset(low[:, :], -1.0).then_inc(s["low"], 1)
                pool.wait_ge(s["low"], 1)
                pool.affine_select(out=low[:, :], in_=low[:, :], compare_op=ALU.is_ge, fill=0.0, base=-2 * (E + 1),
                                   pattern=[[0, 1]], channel_multiplier=1).then_inc(s["low"], 1)
                for n in range(NT):
                    at_least(pool, s["acc1"], n - 1)
                    for k in range(TOP):
                        pool.indirect_dma_start(ya[:, n % 2, k, :], None, g_["ys_dram"],
                                                bass.IndirectOffsetOnAxis(ap=slot[:, k, n:n + 1], axis=0)).then_inc(ga[n % 2], 16)
            else:
                load, split = g_["load_matrix"], g_["split_matrix"]

                def matrix(e, m, n, following):
                    for hf in range(2):
                        split(pool, raw, raw_ld, E_EARLY * NM, e, m, n, hf)
                        if following:
                            load(pool, raw, raw_ld, *following, n + 1, hf)

                for hf in range(2):
                    load(pool, raw, raw_ld, E_EARLY, 0, E_EARLY * NM, hf)
                with pool.Fori(E_EARLY, E - 1) as e:
                    for m in range(NM):
                        matrix(e, m, e * NM + m, (e, m + 1) if m < NM - 1 else (e + 1, 0))
                for m in range(NM):
                    matrix(E - 1, m, (E - 1) * NM + m, (E - 1, m + 1) if m < NM - 1 else (None, 0))
                pool.wait_ge(s["y_mm"], B * S // P)
                for m in range(NM):
                    matrix(None, m, E * NM + m, (None, m + 1) if m < NM - 1 else None)

        @block.scalar
        def _(act):
            names_b = ("L0_ffn_bsu", "L0_ffn_bsg") if shared else ("L0_ffn_bup", "L0_ffn_bgate")
            with nc.allow_non_contiguous_dma(reason="biases by feature, once"):
                for dst, name in zip((bias_u, bias_g), names_b):
                    for e in range(NB):
                        src = t[name] if shared else t[name][e]
                        act.dma_start(dst[:, e, :], src.rearrange("(k p) -> p k", p=P)).then_inc(s["b_loaded"], 16)
            if shared:
                for r in range(3):
                    act.dma_start(bd_raw[r * (E + 1):r * (E + 1) + E, :], t["L0_ffn_bdown"]).then_inc(s["b_loaded"], 16)
                    act.dma_start(bd_raw[r * (E + 1) + E:(r + 1) * (E + 1), :],
                                  t["L0_ffn_bsd"].rearrange("(o n) -> o n", o=1)).then_inc(s["b_loaded"], 16)

            def step(n, j, i):
                if live(n, -1):
                    act.wait_ge(s["xT_t"], n + 2)
                    at_least(act, s["u_mm"], n)
                    act.activation(xT[:, (j + 1) % 2, 0], psX[:, :].rearrange("p (k n) -> p k n", n=P), ACT.Copy).then_inc(s["xT_h"], 1)
                if live(n, 0):
                    act.wait_ge(s["u_r"], n + 1)
                    at_least(act, s["g_mm"], n)
                    act.activation(uT[:, 0], u[:, j % 2], ACT.Copy).then_inc(s["u_h"], 1)
                if live(n, 1) and not shared:
                    act.wait_ge(s["y_mm"], n)
                    at_least(act, y_st[(j - 1) % 2], before(i, j) * 16)
                    act.activation(y[:, (j - 1) % 2], psY[:, :], ACT.Copy, scale=1.0 / WS).then_inc(s["y_r"], 1)
                if live(n, 0):
                    act.wait_ge(s["h_r"], n + 1)
                    at_least(act, s["g_r"], n)
                    act.activation(sl[:, :, :], h[:, :, :], ACT.Silu).then_inc(s["silu"], 1)
                    act.wait_ge(s["g_r"], n + 1)
                    at_least(act, s["y_mm"], n - 1)
                    act.activation(gT[:, j % 2, 0], gf[:, :, :], ACT.Copy).then_inc(s["g_h"], 1)
            step(-1, 1, -1)
            run(act, step, 1)

        @block.vector
        def _(dve):
            if shared:
                dve.wait_ge(s["b_loaded"], 16 * 8)
                dve.tensor_scalar(bd_hi[:, :], bd_raw[:, :], WS, None, ALU.mult).then_inc(s["bd0"], 1)
                dve.tensor_scalar(bd_16[:, :], bd_raw[:, :], WS, None, ALU.mult).then_inc(s["bd0"], 1)
                dve.wait_ge(s["bd0"], 2)
                dve.wait_ge(s["low"], 2)
                dve.scalar_tensor_tensor(bd[:, :], bd_hi[:, :], low[:, :], bd_16[:, :], ALU.mult, ALU.add).then_inc(s["bd1"], 1)
                for q in range(NT // 4):
                    dve.wait_ge(s["pT_t"], q + 1)
                    dve.tensor_copy(pT[:, 4 * q:4 * q + 4, :].rearrange("p n t -> p (n t)"), psP[0:K3, :]).then_inc(s["pT_c"], 1)
            else:
                dve.wait_ge(s["b_loaded"], 16 * 2 * NB)

            def expert(n):
                if shared:
                    return 0
                return dve.value_load(blk_e[0:1, ds(n, 1)], min_val=0, max_val=E - 1)

            def biased(dst, ps_, bias, e):
                b = bias[:, ds(e, 1), :].rearrange("p o k -> p (o k)").unsqueeze(2).broadcast_to([P, KD, P])
                return dve.scalar_tensor_tensor(dst, ps_[:, :].rearrange("p (k n) -> p k n", n=P), 1.0 / WS, b, ALU.mult, ALU.add)

            def step(n, j, i):
                if live(n, -1):
                    dve.wait_ge(s["xT_h"], n + 2)
                    dve.tensor_tensor(xT[:, (j + 1) % 2, 1], psX[:, :].rearrange("p (k n) -> p k n", n=P), xT[:, (j + 1) % 2, 0],
                                      ALU.subtract).then_inc(s["xT_l"], 1)
                if live(n, 0):
                    e = expert(n)
                    dve.wait_ge(s["u_mm"], n + 1)
                    biased(u[:, j % 2], psU, bias_u, e).then_inc(s["u_r"], 1)
                    dve.wait_ge(s["u_h"], n + 1)
                    dve.tensor_tensor(uT[:, 1], u[:, j % 2], uT[:, 0], ALU.subtract).then_inc(s["u_l"], 1)
                if shared and live(n, 1):
                    total(n - 1, (j - 1) % 2, before(i, j))
                if live(n, 0):
                    dve.wait_ge(s["g_mm"], n + 1)
                    at_least(dve, s["silu"], n)
                    biased(h[:, :, :], psG, bias_g, e).then_inc(s["h_r"], 1)
                    dve.wait_ge(s["silu"], n + 1)
                    at_least(dve, s["g_l"], n)
                    dve.tensor_tensor(gf[:, :, :], sl[:, :, :], u[:, j % 2], ALU.mult).then_inc(s["g_r"], 1)
                    dve.wait_ge(s["g_h"], n + 1)
                    dve.tensor_tensor(gT[:, j % 2, 1], gf[:, :, :], gT[:, j % 2, 0], ALU.subtract).then_inc(s["g_l"], 1)

            def total(m, jj, before):
                dve.wait_ge(ga[jj], before * 32 + 32)
                dve.wait_ge(x1_ld[jj], before * 16 + 16)
                dve.scalar_tensor_tensor(acc[:, 0], ya[:, jj, 0, :], prob[:, 0, ds(m, 1)], x1[:, jj], ALU.mult, ALU.add).then_inc(s["acc0"], 1)
                dve.wait_ge(s["acc0"], m + 1)
                dve.scalar_tensor_tensor(acc[:, 1], ya[:, jj, 1, :], prob[:, 1, ds(m, 1)], acc[:, 0], ALU.mult, ALU.add).then_inc(s["acc1"], 1)
                dve.wait_ge(s["acc1"], m + 1)
                dve.wait_ge(s["y_mm"], m + 1)
                at_least(dve, y_st[jj], before * 16)
                dve.scalar_tensor_tensor(y[:, jj], psY[:, :], 1.0 / WS, acc[:, 1], ALU.mult, ALU.add).then_inc(s["y_r"], 1)

            step(-1, 1, -1)
            run(dve, step, 1)

        @block.tensor
        def _(pe):
            def transpose(n, slot_, loads):
                pe.wait_ge(x_ld[slot_], loads * 16 + 16)
                at_least(pe, s["xT_l"], n)
                for c in range(KD):
                    ins = pe.transpose(psX[:, c * P:(c + 1) * P], x_in[:, slot_, c * P:(c + 1) * P], ident[:, :])
                ins.then_inc(s["xT_t"], 1)

            def weights(e, m, part, c, cols):
                return w_exp[:, ds(e, 1), m, part, c, cols].rearrange("p o n -> p (o n)")

            def features(dst, e, m, act_hi, act_lo):
                for f in range(KD):
                    cols = slice(f * P, (f + 1) * P)
                    i = 0
                    for c in range(KD):
                        for part, a in ((0, act_hi), (0, act_lo), (1, act_hi)):
                            ins = pe.matmul(dst[:, cols], weights(e, m, part, c, cols), a[:, c, :], start=(i == 0), stop=(i == 3 * KD - 1))
                            i += 1
                return ins

            def down(m, jj, e):
                pe.wait_ge(s["g_l"], m + 1)
                at_least(pe, s["y_r"], m)
                terms = [(gT[:, jj, x, c, :], weights(e, 2, y_, c, slice(0, D))) for c in range(KD) for x, y_ in ((0, 0), (1, 0), (0, 1))]
                if shared:
                    terms.insert(0, (pT[:, ds(m, 1), :].rearrange("p o n -> p (o n)"), bd[:, :]))
                for i, (a, w) in enumerate(terms):
                    ins = pe.matmul(psY[:, :], a, w, start=(i == 0), stop=(i == len(terms) - 1))
                ins.then_inc(s["y_mm"], 1)

            def expert(n):
                if shared:
                    return 0
                return pe.value_load(blk_e[0:1, ds(n, 1)], min_val=0, max_val=E - 1)

            def step(n, j, i):
                if live(n, -1):
                    transpose(n + 1, (j + 1) % 2, after(i, j))
                if live(n, 0):
                    e = expert(n)
                    if not shared:
                        pe.wait_ge(g_["raw_free"], e * (2 * NM) + 2 * NM + 2)
                    pe.wait_ge(s["xT_l"], n + 1)
                    at_least(pe, s["u_r"], n)
                    features(psU, e, 0, xT[:, j % 2, 0], xT[:, j % 2, 1]).then_inc(s["u_mm"], 1)
                if live(n, 1):
                    down(n - 1, (j - 1) % 2, expert(n - 1))
                if live(n, 0):
                    pe.wait_ge(s["u_l"], n + 1)
                    at_least(pe, s["h_r"], n)
                    features(psG, e, 1, uT[:, 0], uT[:, 1]).then_inc(s["g_mm"], 1)
            if shared:
                pe.wait_ge(s["bd1"], 1)
                for q in range(NT // 4):
                    at_least(pe, s["pT_c"], q)
                    for i in range(4):
                        ins = pe.transpose(psP[0:K3, i * P:(i + 1) * P], pmat[:, 4 * q + i, :, :].rearrange("p a e -> p (a e)"), ident[:, :])
                    ins.then_inc(s["pT_t"], 1)
                pe.wait_ge(s["pT_c"], NT // 4)
            step(-1, 1, -1)
            run(pe, step, 1)


def kernel(**inputs):
    import concourse.bacc as bacc
    from concourse.bass_utils import run_bass_kernel_spmd

    nc = bacc.Bacc("TRN2", target_bir_lowering=False, num_devices=1)
    arrays = {f"in_{name}_dram": np.ascontiguousarray(a) for name, a in inputs.items()}
    t = {name: nc.dram_tensor(f"in_{name}_dram", a.shape, mybir.dt.from_np(np.asarray(a).dtype), kind="ExternalInput").ap()
         for name, a in inputs.items()}
    out = nc.dram_tensor("out_0_dram", (B, S, D), F32, kind="ExternalOutput").ap()
    build(nc, t, out)
    r = run_bass_kernel_spmd(nc, [arrays], core_ids=[0])
    return r.results[0]["out_0_dram"]
```

```python
from contextlib import ExitStack

import numpy as np

import concourse.bass as bass
from concourse import mybir

F32 = mybir.dt.float32
F16 = mybir.dt.float16
I32 = mybir.dt.int32
U32 = mybir.dt.uint32
ALU = mybir.AluOpType
ACT = mybir.ActivationFunctionType
AX = mybir.AxisListType
ds = bass.ds

P = 128
B = 4
S = 512
D = 512
C = 256
H = 16
HD = D // H
NDCA = 16
NMAIN = S - NDCA
TB = S // P
NT = B * TB
KD = D // P
KC = C // P
CH = D // P
E = 7
NM = 3
TOP = 2
NBLK = (B * S * TOP + E * (P - 1)) // P
NSLOT = NBLK * P
NPAD = NBLK - TOP * NT
WS = 16.0
QS = 32.0
LN_EPS = 1e-5
HEAD_EPS = 1e-6
VSEG = 5
VW = 2 * HD + 1
PAIR = 2
SBUF_LO, SBUF_HI = 16512, 229344


def at_least(eng, sem, value):
    if isinstance(value, int) and value <= 0:
        return
    eng.wait_ge(sem, value)


class Map:

    def __init__(self, nc, base, limit):
        self.nc, self.at, self.limit = nc, base, limit

    def __call__(self, name, shape, dt):
        size = int(np.prod(shape[1:])) * (2 if dt == F16 else 4)
        t = self.nc.alloc_sbuf_tensor_at(name, shape, dt, offset=self.at)
        self.at += -(-size // 32) * 32
        assert self.at <= self.limit, (name, self.at, self.limit)
        return t


def build(nc, t, out, upto=99, dbg=None):
    ctx = ExitStack()

    mine = []

    def sem(name):
        mine.append(nc.alloc_semaphore(name=name))
        return mine[-1]

    def end_stage():
        nc.clear_and_free_semaphores(mine)
        nc.all_engine_barrier()
        mine.clear()

    def dram(name, shape, dt):
        return nc.dram_tensor(name, shape, dt, kind="Internal").ap()

    with ctx:
        q_dram = dram("q_dram", (3, B * D, S), F16)
        k_dram = dram("k_dram", (3, B * D, S), F16)
        x1_dram = dram("x1_dram", (B * S, D), F32)
        xs_dram = dram("xs_dram", (NSLOT + B * S, D), F32)
        ys_dram = dram("ys_dram", (NSLOT, D), F32)

        W_BYTES = E * NM * 2 * KD * D * 2
        PER_E = W_BYTES // E
        w_exp = nc.alloc_sbuf_tensor_at("w_exp", [P, 2 * E, NM, 2, KD // 2, D], F16, offset=SBUF_LO)
        V_BYTES = B * H * VSEG * VW * 2
        O_BYTES = B * H * TB * HD * 4
        CONST = 2624
        const = Map(nc, SBUF_HI - CONST, SBUF_HI)
        ident = const("ident", [P, P], F32)
        m_main = const("m_main", [P, 1], F32)
        m_dca = const("m_dca", [P, 1], F32)
        slot = const("slot", [P, TOP, NT], I32)
        prob = const("prob", [P, TOP, NT], F32)
        pmat = const("pmat", [P, NT, 3, E + 1], F32)
        blk_e = const("blk_e", [P, NBLK], I32)
        ws_tile = const("ws_tile", [P, 1], F32)
        seen = const("seen", [P, 1], F32)
        V_AT = (SBUF_HI - CONST - V_BYTES) // 32 * 32
        v_all = nc.alloc_sbuf_tensor_at("v_all", [P, B * H, VSEG, VW], F16, offset=V_AT)
        O_AT = V_AT - O_BYTES
        o_all = nc.alloc_sbuf_tensor_at("o_all", [P, TB, B * H, HD], F32, offset=O_AT)
        w_names = ("L0_ffn_Wup", "L0_ffn_Wgate", "L0_ffn_Wdown")
        s_dram = [t[n].rearrange("(k p) n -> p k n", p=P) for n in ("L0_ffn_Wsu", "L0_ffn_Wsg", "L0_ffn_Wsd")]
        w_dram = [t[n].rearrange("e (k p) n -> p (e k) n", p=P) for n in w_names]
        split_done = sem("w_split_done")
        w_scaled = sem("w_scaled")
        mine.clear()

        def load_half(eng, raw, loaded, x, m):
            if isinstance(x, int) and x >= 2 * E:
                src = s_dram[m][:, 2 * (x - 2 * E):2 * (x - 2 * E) + 2, :]
            else:
                src = w_dram[m][:, ds(x * 2, 2), :]
            eng.dma_start(raw, src).then_inc(loaded, 16)

        def split_half(pool, raw, loaded, arrived, x, m, n, piece):
            if isinstance(x, int) and x >= 2 * E:
                x -= 2 * E
            hi, lo = (w_exp[:, ds(x, 1), m, y, :, :].rearrange("p o k n -> p (o k n)") for y in range(2))
            w = raw.rearrange("p k n -> p (k n)")
            ws = ws_tile[:, :].broadcast_to([P, KD // 2 * D])
            if piece == 0:
                pool.wait_ge(loaded, 16 * arrived)
                pool.tensor_tensor(hi, w, ws, ALU.mult).then_inc(w_scaled, 1)
            elif piece == 1:
                pool.wait_ge(w_scaled, 2 * n + 1)
                pool.tensor_tensor(w, w, ws, ALU.mult).then_inc(w_scaled, 1)
            else:
                pool.wait_ge(w_scaled, 2 * n + 2)
                pool.tensor_tensor(lo, w, hi, ALU.subtract).then_inc(split_done, 1)

        plan = dict(locals())
        project(nc, t, sem, plan)
        end_stage()
        if upto > 1:
            attend(nc, t, sem, plan)
        if upto > 2:
            output(nc, t, sem, plan)
            route(nc, t, sem, plan)
        if upto > 3:
            feed_forward(nc, t, sem, plan, False, out)
            feed_forward(nc, t, sem, plan, True, out)
        if dbg is not None:
            dbg(nc, plan, sem)


def project(nc, t, sem, g_):
    ident, v_all, m_main, m_dca = (g_[k] for k in ("ident", "v_all", "m_main", "m_dca"))
    q_dram, k_dram = g_["q_dram"], g_["k_dram"]
    sb = Map(nc, SBUF_LO, g_["V_AT"])
    wq_raw = sb("wq_raw", [P, KD, D], F32)
    wkv_raw = sb("wkv_raw", [P, KC, 2 * D], F32)
    wdca_raw = sb("wdca_raw", [P, KC, 2 * D], F32)
    wq = sb("wq", [P, 2, KD, D], F16)
    wkv = sb("wkv", [P, 2, KC, 2 * D], F16)
    wdca = sb("wdca", [P, 2, KC, 2 * D], F16)
    bq = sb("bq", [P, D], F32)
    bkv = sb("bkv", [P, 2, 2 * D], F32)
    wsum = sb("wsum", [P, KD + 2 * KC + 3, H], F32)
    affine = sb("affine", [6, P], F32)
    affine_s = sb("affine_s", [P, 6], F32)
    x_in = sb("x_in", [P, 2, D], F32)
    c_in = sb("c_in", [P, 2, C], F32)
    st = sb("st", [P, 2, 6], F32)
    st_seen = sb("st_seen", [P, 1], F32)
    mv = sb("mv", [P, 2, 2], F32)
    ve = sb("ve", [P, 2, 1], F32)
    sd = sb("sd", [P, 2, 1], F32)
    rs = sb("rs", [P, 2, 1], F32)
    xn = sb("xn", [P, 2, D], F32)
    xT = sb("xT", [P, 2, 2, KD, P], F16)
    cT = sb("cT", [P, 2, 2, KC, P], F16)
    cTm = sb("cTm", [P, 2, KC, P], F16)
    cTd = sb("cTd", [P, 2, KC, P], F16)
    qf = sb("qf", [P, 2, D], F32)
    kf = sb("kf", [P, 2, D], F32)
    vf = sb("vf", [P, 2, D], F32)
    vm = sb("vm", [P, 2, D], F32)
    sq = sb("sq", [P, 2, D], F32)
    hv = sb("hv", [P, 2, 2 * H], F32)
    hs_ = sb("hs_", [P, 2, 2 * H], F32)
    hr = sb("hr", [P, 2, 2 * H], F32)
    qn = sb("qn", [P, D], F32)
    kn = sb("kn", [P, D], F32)
    qa = sb("qa", [P, CH, P], F32)
    ka = sb("ka", [P, CH, P], F32)
    q_st = sb("q_st", [P, 2, 2, CH, PAIR * P], F16)
    k_st = sb("k_st", [P, 2, 2, CH, PAIR * P], F16)

    names = """consts masks wq_ld wkv_ld wdca_ld b_loaded a_loaded w_sum w_cent b_cent w_16 w_hi wq_lo w_lo aff_t aff
        stats aggr veps sd_r rs_r xn_r xT_t cT_t xT_h cT_h xT_l cT_l q_mm k_mm v_mm q_ev k_ev v_ev
        sq_r hv_s hv_r hs_r hr_r qn_r kn_r vm_r v_h v_l qT_t kT_t qa_r ka_r q_h k_h q_l k_l"""
    s = {n: sem("p_" + n) for n in names.split()}
    x_ld = [sem("p_x_loaded0"), sem("p_x_loaded1")]
    c_ld = [sem("p_c_loaded0"), sem("p_c_loaded1")]
    st_q = [sem("p_q_stored0"), sem("p_q_stored1")]
    st_k = [sem("p_k_stored0"), sem("p_k_stored1")]

    with ExitStack() as ps:
        def bank(name):
            return ps.enter_context(nc.psum_tensor(name, [P, 512], F32))
        psX, psC, psQ, psK, psV, psQT, psKT = (bank("p_" + n) for n in ("psX", "psC", "psQ", "psK", "psV", "psQT", "psKT"))
        block = ps.enter_context(nc.Block())

        def g_of(b, j):
            return b * TB + j

        def load(sp, b, j):
            if isinstance(b, int):
                b, j = b + j // TB, j % TB
            else:
                b, j = (b + 1, j - TB) if j >= TB else (b, j)
            g = g_of(b, j)
            at_least(sp, s["xn_r"], g - 1)
            sp.dma_start(x_in[:, j % 2], t["x"][b, j * P:(j + 1) * P, :] if isinstance(b, int)
                         else t["x"].rearrange("b s d -> (b s) d")[ds(g * P, P), :]).then_inc(x_ld[j % 2], 16)
            at_least(sp, s["cT_t"], g - 1)
            sp.dma_start(c_in[:, j % 2], t["ctx_1024"].rearrange("b s d -> (b s) d")[ds(g * P, P), :]).then_inc(c_ld[j % 2], 16)

        def store(sp, b, j):
            if j < 0:
                b, j = b - 1, j + TB
            g = g_of(b, j)
            slot = j // PAIR
            for buf, dst, hi, lo, done in ((q_st, q_dram, "q_h", "q_l", st_q), (k_st, k_dram, "k_h", "k_l", st_k)):
                sp.wait_ge(s[hi], g + 1)
                sp.wait_ge(s[lo], g + 1)
                for r, part in enumerate((0, 0, 1) if dst is q_dram else (0, 1, 0)):
                    d = dst[r, ds(b * D, D), slot * PAIR * P:(slot + 1) * PAIR * P]
                    sp.dma_start(d.rearrange("(c p) t -> p c t", p=P), buf[:, slot, part]).then_inc(done[slot], 16)

        def later(b, j, n):
            return (b, j + n) if j + n < TB else (b + 1, j + n - TB)

        def earlier(b, j, n):
            return (b, j - n) if j >= n else (b - 1, j - n + TB)

        def w_view(w, natural):
            return w.rearrange("p (h two d) -> p h two d" if natural else "p (two h d) -> p h two d", two=2, d=HD)

        def k_cols(w):
            return w_view(w, True)[:, :, 0, :]

        def v_cols(w):
            return w_view(w, True)[:, :, 1, :]

        def v_view(b, seg):
            return v_all[:, ds(b * H, H), seg, :]

        @block.sync
        def _(sp):
            def rows(name):
                return t[name].rearrange("(k p) n -> p k n", p=P)
            load(sp, 0, 0)
            sp.dma_start(wq_raw[:, :, :], rows("L0_xattn_Wq")).then_inc(s["wq_ld"], 16)
            load(sp, 0, 1)
            sp.dma_start(wkv_raw[:, :, 0:D], rows("L0_xattn_Wk")).then_inc(s["wkv_ld"], 16)
            sp.dma_start(wkv_raw[:, :, D:2 * D], rows("L0_xattn_Wv")).then_inc(s["wkv_ld"], 16)
            sp.dma_start(wdca_raw[:, :, :], rows("L0_xattn_Wkv_dca")).then_inc(s["wdca_ld"], 16)
            load(sp, 0, 2)

            def steps(b, last):
                for j in range(TB):
                    if not (last and j >= TB - 3):
                        load(sp, b, j + 3)
                    if j % PAIR and not (isinstance(b, int) and b == 0 and j == 1):
                        store(sp, b, j - 2)
            steps(0, False)
            with sp.Fori(1, B - 1) as b:
                steps(b, False)
            steps(B - 1, True)
            store(sp, B - 1, TB - 1)
            for q in st_q + st_k:
                sp.wait_ge(q, 3 * 16 * NT // PAIR // 2)

        @block.gpsimd
        def _(pool):
            pool.memset(ident[:, :], 0.0).then_inc(s["consts"], 1)
            pool.memset(m_dca[:, :], 0.0).then_inc(s["consts"], 1)
            pool.memset(m_main[:, :], 1.0).then_inc(s["consts"], 1)
            pool.wait_ge(s["consts"], 3)
            pool.affine_select(out=ident[:, :], in_=ident[:, :], compare_op=ALU.not_equal, fill=1.0, base=0,
                               pattern=[[-1, P]], channel_multiplier=1).then_inc(s["masks"], 1)
            pool.affine_select(out=m_main[:, :], in_=m_main[:, :], compare_op=ALU.is_ge, fill=0.0, base=P - NDCA - 1,
                               pattern=[[0, 1]], channel_multiplier=-1).then_inc(s["masks"], 1)
            pool.affine_select(out=m_dca[:, :], in_=m_dca[:, :], compare_op=ALU.is_ge, fill=1.0, base=P - NDCA - 1,
                               pattern=[[0, 1]], channel_multiplier=-1).then_inc(s["masks"], 1)
            pool.memset(v_all[:, :, 0:3, HD:HD + 1], 1.0).then_inc(s["masks"], 1)
            pool.memset(cTm[:, :, :, :], 0.0).then_inc(s["masks"], 1)
            pool.memset(cTd[:, :, :, :], 0.0).then_inc(s["masks"], 1)

            for n, (src, dst) in enumerate(((wkv_raw, wkv), (wdca_raw, wdca))):
                for c in range(KC):
                    pool.wait_ge(s["w_hi"], KC * n + c + 2)
                    pool.tensor_tensor(w_view(dst[:, 1, c, :], False), w_view(src[:, c, :], n == 0), w_view(dst[:, 0, c, :], False),
                                       ALU.subtract).then_inc(s["w_lo"], 1)

            def mid(b, j):
                g = g_of(b, j)
                pool.wait_ge(s["hr_r"], g + 1)
                for n, (src, dst, dn, free) in enumerate(((qf, qn, "qn_r", "qT_t"), (kf, kn, "kn_r", "kT_t"))):
                    at_least(pool, s[free], g)
                    r = hr[:, j % 2, n * H:(n + 1) * H].unsqueeze(2).broadcast_to([P, H, HD])
                    pool.tensor_tensor(dst[:, :].rearrange("p (h d) -> p h d", d=HD),
                                       src[:, j % 2].rearrange("p (h d) -> p h d", d=HD), r, ALU.mult).then_inc(s[dn], 1)
                if j < TB - 1:
                    pool.wait_ge(s["v_h"], b * (TB + 1) + j + 1)
                    v = v_view(b, j)
                    pool.tensor_tensor(v[:, :, HD + 1:], vf[:, j % 2].rearrange("p (h d) -> p h d", d=HD),
                                       v[:, :, 0:HD], ALU.subtract).then_inc(s["v_l"], 1)
                else:
                    for n in range(2):
                        pool.wait_ge(s["v_h"], b * (TB + 1) + j + 1 + n)
                        v = v_view(b, j + n)
                        pool.tensor_tensor(v[:, :, HD + 1:], vm[:, n].rearrange("p (h d) -> p h d", d=HD),
                                           v[:, :, 0:HD], ALU.subtract).then_inc(s["v_l"], 1)

            def back(b, j):
                g = g_of(b, j)
                for buf, src, hi, dn in ((q_st, qa, "q_h", "q_l"), (k_st, ka, "k_h", "k_l")):
                    pool.wait_ge(s[hi], g + 1)
                    c = (j % PAIR) * P
                    pool.tensor_tensor(buf[:, j // PAIR, 1, :, c:c + P], src[:, :, :],
                                       buf[:, j // PAIR, 0, :, c:c + P], ALU.subtract).then_inc(s[dn], 1)

            def steps(b, first):
                for j in range(TB):
                    if not (first and j < 2):
                        back(*earlier(b, j, 2))
                    mid(b, j)
            steps(0, True)
            with pool.Fori(1, B) as b:
                steps(b, False)
            back(B - 1, TB - 2)
            back(B - 1, TB - 1)

        @block.scalar
        def _(act):
            act.dma_start(bq[:, :], t["L0_xattn_bq"].partition_broadcast(P)).then_inc(s["b_loaded"], 16)
            for n, name in enumerate(("qn_w", "qn_b", "kn_w", "kn_b", "kn_dca_w", "kn_dca_b")):
                act.dma_start(affine[n:n + 1, :].rearrange("o (q d) -> o q d", d=HD),
                              t["L0_xattn_" + name].rearrange("(o r d) -> o r d", o=1, r=1).broadcast_to([1, P // HD, HD])
                              ).then_inc(s["a_loaded"], 16)
            for v, n in ((0, P), (1, P - NDCA)):
                for half, name in ((0, "L0_xattn_bk"), (1, "L0_xattn_bv")):
                    act.dma_start(bkv[0:n, v, half * D:(half + 1) * D], t[name].partition_broadcast(n)).then_inc(s["b_loaded"], 16)
            for kv in range(2):
                dst = w_view(bkv[P - NDCA:P, 1, :], True)[:, :, kv, :]
                src = t["L0_xattn_bkv_dca"][kv * D:(kv + 1) * D].rearrange("(h d) -> h d", d=HD)
                act.dma_start(dst, src.partition_broadcast(NDCA)).then_inc(s["b_loaded"], 16)

            def sqrt(b, j):
                act.wait_ge(s["veps"], g_of(b, j) + 1)
                act.activation(sd[:, j % 2], ve[:, j % 2], ACT.Sqrt).then_inc(s["sd_r"], 1)

            def front(b, j):
                g = g_of(b, j)
                act.wait_ge(s["xT_t"], g + 1)
                at_least(act, s["q_mm"], g - 1)
                act.activation(xT[:, j % 2, 0], psX[:, :].rearrange("p (k n) -> p k n", n=P), ACT.Copy).then_inc(s["xT_h"], 1)
                act.wait_ge(s["cT_t"], g + 1)
                pc = psC[:, 0:C].rearrange("p (k n) -> p k n", n=P)
                if j < TB - 1:
                    at_least(act, s["v_mm"], g - 1)
                    act.activation(cT[:, j % 2, 0], pc, ACT.Copy).then_inc(s["cT_h"], 1)
                else:
                    at_least(act, s["v_mm"], g - TB + 1)
                    m = P - NDCA
                    act.activation(cTm[:, 0, :, 0:m], pc[:, :, 0:m], ACT.Copy)
                    act.activation(cTd[:, 0, :, m:P], pc[:, :, m:P], ACT.Copy).then_inc(s["cT_h"], 1)

            def mid(b, j):
                g = g_of(b, j)
                at_least(act, s["hv_s"], g)
                act.wait_ge(s["q_ev"], g + 1)
                act.activation(sq[:, 0], qf[:, j % 2], ACT.Square)
                act.wait_ge(s["k_ev"], g + 1)
                act.activation(sq[:, 1], kf[:, j % 2], ACT.Square).then_inc(s["sq_r"], 1)
                if j < TB - 1:
                    act.wait_ge(s["v_ev"], g + 1)
                    act.activation(v_view(b, j)[:, :, 0:HD], vf[:, j % 2].rearrange("p (h d) -> p h d", d=HD),
                                   ACT.Copy).then_inc(s["v_h"], 1)
                else:
                    for n in range(2):
                        act.wait_ge(s["vm_r"], 2 * b + n + 1)
                        act.activation(v_view(b, j + n)[:, :, 0:HD], vm[:, n].rearrange("p (h d) -> p h d", d=HD),
                                       ACT.Copy).then_inc(s["v_h"], 1)
                act.wait_ge(s["hv_r"], g + 1)
                act.activation(hs_[:, j % 2], hv[:, j % 2], ACT.Sqrt).then_inc(s["hs_r"], 1)

            def back(b, j):
                g = g_of(b, j)
                act.wait_ge(s["aff"], 1)
                gp = b * (TB // PAIR) + j // PAIR
                for buf, a, p_t, tt, dn, hi, lo, stored, w in (
                        (q_st, qa, psQT, "qT_t", "qa_r", "q_h", "q_l", st_q, 0),
                        (k_st, ka, psKT, "kT_t", "ka_r", "k_h", "k_l", st_k, 2)):
                    act.wait_ge(s[tt], g + 1)
                    at_least(act, s[lo], g)
                    pt = p_t[:, :].rearrange("p (c n) -> p c n", n=P)
                    m = P - NDCA if (w == 2 and j == TB - 1) else P
                    ins = act.activation(a[:, :, 0:m], pt[:, :, 0:m], ACT.Identity,
                                         scale=affine_s[:, w:w + 1], bias=affine_s[:, w + 1:w + 2])
                    if m < P:
                        ins = act.activation(a[:, :, m:P], pt[:, :, m:P], ACT.Identity,
                                             scale=affine_s[:, 4:5], bias=affine_s[:, 5:6])
                    ins.then_inc(s[dn], 1)
                    act.wait_ge(s[dn], g + 1)
                    if j % PAIR == 0:
                        at_least(act, stored[j // PAIR], 3 * 16 * b)
                    c = (j % PAIR) * P
                    act.activation(buf[:, j // PAIR, 0, :, c:c + P], a[:, :, :], ACT.Copy).then_inc(s[hi], 1)

            def steps(b, first, last):
                for j in range(TB):
                    if not (last and j >= TB - 2):
                        sqrt(*later(b, j, 2))
                    if not (last and j == TB - 1):
                        front(*later(b, j, 1))
                    if not (first and j < 2):
                        back(*earlier(b, j, 2))
                    mid(b, j)
            sqrt(0, 0)
            sqrt(0, 1)
            act.wait_ge(s["w_cent"], 1)
            act.activation(wq[:, 0], wq_raw[:, :, :], ACT.Copy, scale=WS).then_inc(s["w_hi"], 1)
            front(0, 0)
            act.wait_ge(s["aff_t"], 1)
            act.activation(affine_s[:, :], psKT[:, 0:6], ACT.Copy, scale=QS).then_inc(s["aff"], 1)
            for n, (src, dst) in enumerate(((wkv_raw, wkv), (wdca_raw, wdca))):
                for c in range(KC):
                    act.wait_ge(s["w_cent"], 2 + KC * n + c)
                    act.activation(src[:, c, :], src[:, c, :], ACT.Copy, scale=WS).then_inc(s["w_16"], 1)
                    act.wait_ge(s["w_16"], KC * n + c + 1)
                    act.activation(w_view(dst[:, 0, c, :], False), w_view(src[:, c, :], n == 0), ACT.Copy).then_inc(s["w_hi"], 1)
            steps(0, True, False)
            with act.Fori(1, B - 1) as b:
                steps(b, False, False)
            steps(B - 1, False, True)
            back(B - 1, TB - 2)
            back(B - 1, TB - 1)

        @block.vector
        def _(dve):
            sums = [0]

            def centre(views, done):
                first = sums[0]
                for i, v in enumerate(views):
                    dve.tensor_reduce(wsum[:, first + i, :], v, AX.X, ALU.add).then_inc(s["w_sum"], 1)
                sums[0] += len(views)
                dve.wait_ge(s["w_sum"], sums[0])
                for i, v in enumerate(views):
                    dve.scalar_tensor_tensor(v, wsum[:, first + i, :].unsqueeze(2).broadcast_to([P, H, HD]), -1.0 / HD, v,
                                             ALU.mult, ALU.add).then_inc(s[done], 1)

            def heads(v):
                return v.rearrange("p (h d) -> p h d", d=HD)

            def front_a(b, j):
                g = g_of(b, j)
                dve.wait_ge(x_ld[j % 2], 16 * (b * (TB // 2) + j // 2 + 1))
                dve.bn_stats(st[:, j % 2], x_in[:, j % 2]).then_inc(s["stats"], 1)
                dve.wait_ge(s["stats"], g + 1)
                dve.tensor_copy(st_seen[:, :], st[:, j % 2, 0:1])
                dve.bn_aggr(mv[:, j % 2], st[:, j % 2]).then_inc(s["aggr"], 1)
                dve.wait_ge(s["aggr"], g + 1)
                dve.tensor_scalar(ve[:, j % 2], mv[:, j % 2, 1:2], LN_EPS, None, ALU.add).then_inc(s["veps"], 1)

            def front_b(b, j):
                g = g_of(b, j)
                dve.wait_ge(s["sd_r"], g + 1)
                dve.reciprocal(rs[:, j % 2], sd[:, j % 2]).then_inc(s["rs_r"], 1)
                dve.wait_ge(s["rs_r"], g + 1)
                at_least(dve, s["xT_t"], g - 1)
                dve.tensor_scalar(xn[:, j % 2], x_in[:, j % 2], mv[:, j % 2, 0:1], rs[:, j % 2],
                                  ALU.subtract, ALU.mult).then_inc(s["xn_r"], 1)

            def front_c(b, j):
                g = g_of(b, j)
                dve.wait_ge(s["xT_h"], g + 1)
                dve.tensor_tensor(xT[:, j % 2, 1], psX[:, :].rearrange("p (k n) -> p k n", n=P), xT[:, j % 2, 0],
                                  ALU.subtract).then_inc(s["xT_l"], 1)
                dve.wait_ge(s["cT_h"], g + 1)
                pc = psC[:, 0:C].rearrange("p (k n) -> p k n", n=P)
                if j < TB - 1:
                    dve.tensor_tensor(cT[:, j % 2, 1], pc, cT[:, j % 2, 0], ALU.subtract).then_inc(s["cT_l"], 1)
                else:
                    m = P - NDCA
                    dve.wait_ge(s["masks"], 6)
                    dve.tensor_tensor(cTm[:, 1, :, 0:m], pc[:, :, 0:m], cTm[:, 0, :, 0:m], ALU.subtract)
                    dve.tensor_tensor(cTd[:, 1, :, m:P], pc[:, :, m:P], cTd[:, 0, :, m:P], ALU.subtract).then_inc(s["cT_l"], 1)

            def mid(b, j):
                g = g_of(b, j)
                dve.wait_ge(s["q_mm"], g + 1)
                at_least(dve, s["qn_r"], g - 1)
                dve.scalar_tensor_tensor(qf[:, j % 2], psQ[:, :], 1.0 / WS, bq[:, :], ALU.mult, ALU.add).then_inc(s["q_ev"], 1)
                var = 1 if j == TB - 1 else 0
                dve.wait_ge(s["k_mm"], g + 1)
                at_least(dve, s["kn_r"], g - 1)
                dve.scalar_tensor_tensor(heads(kf[:, j % 2]), heads(psK[:, :]), 1.0 / WS, k_cols(bkv[:, var, :]), ALU.mult, ALU.add).then_inc(s["k_ev"], 1)
                dve.wait_ge(s["v_mm"], g + 1)
                at_least(dve, s["v_l"], b * (TB + 1) + j - 1)
                dve.scalar_tensor_tensor(heads(vf[:, j % 2]), heads(psV[:, :]), 1.0 / WS, v_cols(bkv[:, var, :]), ALU.mult, ALU.add).then_inc(s["v_ev"], 1)
                if var:
                    dve.wait_ge(s["v_ev"], g + 1)
                    at_least(dve, s["v_l"], b * (TB + 1))
                    dve.tensor_scalar(vm[:, 0], vf[:, j % 2], m_main[:, :], None, ALU.mult).then_inc(s["vm_r"], 1)
                    dve.tensor_scalar(vm[:, 1], vf[:, j % 2], m_dca[:, :], None, ALU.mult).then_inc(s["vm_r"], 1)
                dve.wait_ge(s["sq_r"], g + 1)
                dve.tensor_reduce(hv[:, j % 2], sq[:, :, :].rearrange("p n (h d) -> p (n h) d", d=HD), AX.X, ALU.add).then_inc(s["hv_s"], 1)
                dve.wait_ge(s["hv_s"], g + 1)
                dve.tensor_scalar(hv[:, j % 2], hv[:, j % 2], 1.0 / HD, HEAD_EPS, ALU.mult, ALU.add).then_inc(s["hv_r"], 1)

            def mid_b(b, j):
                g = g_of(b, j)
                dve.wait_ge(s["hs_r"], g + 1)
                at_least(dve, s["kn_r"], g - 1)
                dve.reciprocal(hr[:, j % 2], hs_[:, j % 2]).then_inc(s["hr_r"], 1)

            def steps(b, first, last):
                for j in range(TB):
                    if not (last and j >= TB - 2):
                        front_a(*later(b, j, 2))
                    if not (last and j == TB - 1):
                        front_c(*later(b, j, 1))
                    if not (last and j >= TB - 2):
                        front_b(*later(b, j, 2))
                    mid(b, j)
                    mid_b(b, j)
            front_a(0, 0)
            front_a(0, 1)
            front_b(0, 0)
            front_b(0, 1)
            dve.wait_ge(s["wq_ld"], 16)
            for c in range(KD):
                dve.tensor_reduce(wsum[:, c, :], heads(wq_raw[:, c, :]), AX.X, ALU.add).then_inc(s["w_sum"], 1)
            sums[0] = KD
            dve.wait_ge(s["w_sum"], KD)
            for c in range(KD):
                ins = dve.scalar_tensor_tensor(heads(wq_raw[:, c, :]), wsum[:, c, :].unsqueeze(2).broadcast_to([P, H, HD]), -1.0 / HD,
                                               heads(wq_raw[:, c, :]), ALU.mult, ALU.add)
            ins.then_inc(s["w_cent"], 1)
            dve.wait_ge(s["w_hi"], 1)
            dve.scalar_tensor_tensor(wq[:, 1].rearrange("p k n -> p (k n)"), wq_raw[:, :, :].rearrange("p k n -> p (k n)"),
                                     WS, wq[:, 0].rearrange("p k n -> p (k n)"), ALU.mult, ALU.subtract).then_inc(s["wq_lo"], 1)
            dve.wait_ge(s["wkv_ld"], 32)
            centre([k_cols(wkv_raw[:, c, :]) for c in range(KC)], "w_cent")
            front_c(0, 0)
            dve.wait_ge(s["b_loaded"], 16 * 7)
            centre([heads(bq[:, :]), k_cols(bkv[:, 0, :]), k_cols(bkv[:, 1, :])], "b_cent")
            dve.wait_ge(s["wdca_ld"], 16)
            centre([heads(wdca_raw[:, c, 0:D]) for c in range(KC)], "w_cent")
            dve.wait_ge(s["masks"], 4)
            dve.tensor_copy(v_all[:, :, 3, HD:HD + 1], m_main[:, :].unsqueeze(1).broadcast_to([P, B * H, 1]))
            dve.tensor_copy(v_all[:, :, 4, HD:HD + 1], m_dca[:, :].unsqueeze(1).broadcast_to([P, B * H, 1]))
            dve.wait_ge(s["b_cent"], 3)
            steps(0, True, False)
            with dve.Fori(1, B - 1) as b:
                steps(b, False, False)
            steps(B - 1, False, True)

        @block.tensor
        def _(pe):
            pe.wait_ge(s["masks"], 1)

            def front(b, j):
                g = g_of(b, j)
                pe.wait_ge(s["xn_r"], g + 1)
                at_least(pe, s["xT_l"], g)
                for c in range(KD):
                    ins = pe.transpose(psX[:, c * P:(c + 1) * P], xn[:, j % 2, c * P:(c + 1) * P], ident[:, :])
                ins.then_inc(s["xT_t"], 1)
                pe.wait_ge(c_ld[j % 2], 16 * (b * (TB // 2) + j // 2 + 1))
                at_least(pe, s["cT_l"], g)
                for c in range(KC):
                    ins = pe.transpose(psC[:, c * P:(c + 1) * P], c_in[:, j % 2, c * P:(c + 1) * P], ident[:, :])
                ins.then_inc(s["cT_t"], 1)

            def product(dst, terms):
                for n, (a, w) in enumerate(terms):
                    ins = pe.matmul(dst, a, w, start=(n == 0), stop=(n == len(terms) - 1))
                return ins

            def passes(a, w, cols, chunks):
                return [(a[:, x, c, :], w[:, y, c, cols]) for c in range(chunks) for x, y in ((0, 0), (1, 0), (0, 1))]

            def mid(b, j):
                g = g_of(b, j)
                pe.wait_ge(s["xT_l"], g + 1)
                pe.wait_ge(s["wq_lo"], 1)
                at_least(pe, s["q_ev"], g)
                product(psQ[:, :], passes(xT[:, j % 2], wq, slice(0, D), KD)).then_inc(s["q_mm"], 1)
                pe.wait_ge(s["cT_l"], g + 1)
                pe.wait_ge(s["w_lo"], KC if j < TB - 1 else 2 * KC)
                for dst, ev, mm, cols in ((psK, "k_ev", "k_mm", slice(0, D)), (psV, "v_ev", "v_mm", slice(D, 2 * D))):
                    at_least(pe, s[ev], g)
                    if j < TB - 1:
                        terms = passes(cT[:, j % 2], wkv, cols, KC)
                    else:
                        terms = passes(cTm, wkv, cols, KC) + passes(cTd, wdca, cols, KC)
                    product(dst[:, :], terms).then_inc(s[mm], 1)

            def back(b, j):
                g = g_of(b, j)
                for src, dst, rdy, used, dn in ((qn, psQT, "qn_r", "qa_r", "qT_t"), (kn, psKT, "kn_r", "ka_r", "kT_t")):
                    pe.wait_ge(s[rdy], g + 1)
                    at_least(pe, s[used], g)
                    if isinstance(g, int) and g == 0:
                        pe.wait_ge(s["aff"], 1)
                    for c in range(CH):
                        ins = pe.transpose(dst[:, c * P:(c + 1) * P], src[:, c * P:(c + 1) * P], ident[:, :])
                    ins.then_inc(s[dn], 1)

            def steps(b, first, last):
                for j in range(TB):
                    nxt = (b, j + 1) if j < TB - 1 else (b + 1, 0)
                    if not (last and j == TB - 1):
                        front(*nxt)
                    mid(b, j)
                    if j:
                        back(b, j - 1)
                    elif not first:
                        back(b - 1, TB - 1)
            front(0, 0)
            pe.wait_ge(s["a_loaded"], 16 * 6)
            pe.transpose(psKT[:, 0:6], affine[:, :], ident[0:6, 0:6]).then_inc(s["aff_t"], 1)
            steps(0, True, False)
            with pe.Fori(1, B - 1) as b:
                steps(b, False, False)
            steps(B - 1, False, True)
            back(B - 1, TB - 1)


E_EARLY = 2
SCALE = float(HD) ** -0.5


def attend(nc, t, sem, g_):
    ident, v_all, o_all = g_["ident"], g_["v_all"], g_["o_all"]
    q_dram, k_dram = g_["q_dram"], g_["k_dram"]
    N = B * H
    G = 4
    SLOTS = G
    PEEL = 2
    K3 = 3 * HD
    KR = K3 + 2
    sb = Map(nc, SBUF_LO + E_EARLY * g_["PER_E"], g_["O_AT"])
    raw = sb("a_raw", [P, 2, D], F32)
    q_stk = sb("q_stk", [P, SLOTS, S], F16)
    k_stk = sb("k_stk", [P, SLOTS, S], F16)
    nm = sb("nm", [P, 2, TB, 2], F32)
    pf = sb("pf", [P, TB, S], F32)
    ph = sb("ph", [P, 2, TB, S], F16)
    pl = sb("pl", [P, 2, TB, S], F16)
    oe = sb("oe", [P, 2, TB, 2, VW], F32)
    on = sb("on", [P, 2, TB, 2, HD], F32)
    orc = sb("orc", [P, 2, TB, 2, 1], F32)
    om = sb("om", [P, 2, TB, 2, HD], F32)
    HI_ACT, LO_DVE = (0, 2), (0, 1)

    names = """sel max m_mm mrow s_mm t_mm exp o_mm o_ev h_act h_dve l_dve l_pool num rec mul out"""
    s = {n: sem("a_" + n) for n in names.split()}
    raw_ld = sem("a_raw_loaded")
    loaded = [sem(f"a_stack_loaded{n}") for n in range(SLOTS)]

    with ExitStack() as ps:
        psS = ps.enter_context(nc.psum_tensor("a_psS", [P, 2, 512], F32))
        psT = ps.enter_context(nc.psum_tensor("a_psT", [P, 2, 512], F32))
        psO = ps.enter_context(nc.psum_tensor("a_psO", [P, 2, 512], F32))
        psM = ps.enter_context(nc.psum_tensor("a_psM", [P, 512], F32))
        block = ps.enter_context(nc.Block())

        def live(u, lag, end=N):
            return not isinstance(u, int) or lag <= u < end + lag

        def run(eng, step, tail, between=None):
            for u in range(PEEL * G):
                step(u, u % G)
            at = PEEL
            if between:
                for m in range(NM):
                    with eng.Fori(at, at + 2 * E_EARLY) as g:
                        for j in range(G):
                            step(g * G + j, j)
                            between(m, g - at, j)
                    at += 2 * E_EARLY
            with eng.Fori(at, N // G) as g:
                for j in range(G):
                    step(g * G + j, j)
            for j in range(tail):
                step(N + j, j % G)

        def half_of(m, x):
            return x + 2 * E_EARLY * m

        @block.sync
        def _(sp):
            def step(u, j):
                if live(u, 0):
                    at_least(sp, s["t_mm"], TB * (u - 3))
                    for stk, dr in ((q_stk, q_dram), (k_stk, k_dram)):
                        sp.dma_start(stk[0:K3, j, :], dr[:, ds(u * HD, HD), :]).then_inc(loaded[j], 16)

            def between(m, x, j):
                if j == 0:
                    sp.wait_ge(g_["split_done"], half_of(m, x) + 1)
                    g_["load_half"](sp, raw[:, :, :], raw_ld, x, m)
            run(sp, step, 0, between)

        @block.gpsimd
        def _(pool):
            pool.memset(k_stk[K3:KR, :, :], QS).then_inc(s["sel"], 1)
            pool.wait_ge(s["sel"], 1)
            pool.memset(g_["ws_tile"][:, :], WS).then_inc(g_["split_done"], 1)
            pool.wait_ge(g_["split_done"], 1)
            sel = k_stk[K3:KR, :, :]
            pool.affine_select(out=sel, in_=sel, compare_op=ALU.is_ge, fill=0.0, base=NMAIN - 1,
                               pattern=[[0, SLOTS], [-1, S]], channel_multiplier=1000).then_inc(s["sel"], 1)
            pool.wait_ge(s["sel"], 2)
            pool.affine_select(out=sel, in_=sel, compare_op=ALU.is_ge, fill=0.0, base=1000 - NMAIN,
                               pattern=[[0, SLOTS], [1, S]], channel_multiplier=-1000).then_inc(s["sel"], 1)

            def step(u, j):
                if live(u, 4):
                    w = u - 4
                    sl = j % 2
                    pool.wait_ge(s["rec"], w + 1)
                    pool.tensor_tensor(om[:, sl].rearrange("p q s d -> p (q s) d"), on[:, sl].rearrange("p q s d -> p (q s) d"),
                                       orc[:, sl].rearrange("p q s o -> p (q s) o").broadcast_to([P, TB * 2, HD]), ALU.mult).then_inc(s["mul"], 1)
                    pool.wait_ge(s["mul"], w + 1)
                    pool.tensor_tensor(o_all[:, :, ds(w, 1), :].rearrange("p q o d -> p (q o) d"), om[:, sl, :, 0, :], om[:, sl, :, 1, :], ALU.add).then_inc(s["out"], 1)
                if live(u, 2):
                    w = u - 2
                    sl = j % 2
                    for n, k in enumerate(k for k in range(TB) if k not in LO_DVE):
                        if k in HI_ACT:
                            pool.wait_ge(s["h_act"], len(HI_ACT) * w + HI_ACT.index(k) + 1)
                        else:
                            pool.wait_ge(s["h_dve"], (TB - len(HI_ACT)) * w + [x for x in range(TB) if x not in HI_ACT].index(k) + 1)
                        pool.tensor_tensor(pl[:, sl, k], pf[:, k], ph[:, sl, k], ALU.subtract).then_inc(s["l_pool"], 1)

            def between(m, x, j):
                if j < 3:
                    n = half_of(m, x)
                    g_["split_half"](pool, raw[:, :, :], raw_ld, n + 1, x, m, n, j)
            run(pool, step, 4, between)

        @block.scalar
        def _(act):
            def exps(w, sl, k):
                act.wait_ge(s["t_mm"], TB * w + k + 1)
                if k in LO_DVE:
                    at_least(act, s["l_dve"], len(LO_DVE) * (w - 1) + LO_DVE.index(k) + 1)
                else:
                    at_least(act, s["l_pool"], 2 * (w - 1) + (k - 2) + 1)
                act.activation(pf[:, k], psT[:, k % 2], ACT.Exp, scale=SCALE / (QS * QS)).then_inc(s["exp"], 1)
                if k in HI_ACT:
                    act.wait_ge(s["exp"], TB * w + k + 1)
                    at_least(act, s["o_mm"], 2 * (w - 1))
                    act.activation(ph[:, sl, k], pf[:, k], ACT.Copy).then_inc(s["h_act"], 1)

            def evac(w, sl, p):
                act.wait_ge(s["o_mm"], 2 * w + p + 1)
                if p == 0:
                    at_least(act, s["rec"], w - 1)
                act.activation(oe[:, sl, 2 * p:2 * p + 2].rearrange("p q s v -> p (q s v)"), psO[:, p, 0:4 * VW], ACT.Copy).then_inc(s["o_ev"], 1)

            def step(u, j):
                if live(u, 4):
                    evac(u - 4, j % 2, 1)
                if live(u, 2):
                    exps(u - 2, j % 2, 0)
                    exps(u - 2, j % 2, 1)
                if live(u, 1):
                    w = u - 1
                    act.wait_ge(s["m_mm"], w + 1)
                    act.activation(q_stk[K3:KR, (j - 1) % SLOTS, :], psM[0:2, :], ACT.Copy, scale=1.0 / QS).then_inc(s["mrow"], 1)
                if live(u, 2):
                    exps(u - 2, j % 2, 2)
                if live(u, 3):
                    evac(u - 3, (j - 3) % 2, 0)
                if live(u, 2):
                    exps(u - 2, j % 2, 3)
            run(act, step, 5)

        @block.vector
        def _(dve):
            def maxima(u, j, p):
                sl = j % 2
                dve.wait_ge(s["s_mm"], 2 * u + p + 1)
                at_least(dve, s["m_mm"], u - 1)
                dve.tensor_reduce(nm[:, sl, 2 * p:2 * p + 2, 0:1].rearrange("p q o -> p (q o)"), psS[:, :, 0:NMAIN], AX.X, ALU.max, negate=True)
                dve.tensor_reduce(nm[:, sl, 2 * p:2 * p + 2, 1:2].rearrange("p q o -> p (q o)"), psS[:, :, NMAIN:S], AX.X, ALU.max, negate=True).then_inc(s["max"], 1)

            def hi(w, sl, k):
                dve.wait_ge(s["exp"], TB * w + k + 1)
                at_least(dve, s["o_mm"], 2 * (w - 1))
                dve.tensor_copy(ph[:, sl, k], pf[:, k]).then_inc(s["h_dve"], 1)

            def lo(w, sl, k):
                if k in HI_ACT:
                    dve.wait_ge(s["h_act"], len(HI_ACT) * w + HI_ACT.index(k) + 1)
                else:
                    dve.wait_ge(s["h_dve"], 2 * w + k // 2 + 1)
                dve.tensor_tensor(pl[:, sl, k], pf[:, k], ph[:, sl, k], ALU.subtract).then_inc(s["l_dve"], 1)

            def norm(w, sl):
                dve.wait_ge(s["o_ev"], 2 * w + 2)
                at_least(dve, s["mul"], w - 1)
                e = oe[:, sl].rearrange("p q s v -> p (q s) v")
                dve.tensor_tensor(on[:, sl].rearrange("p q s d -> p (q s) d"), e[:, :, 0:HD], e[:, :, HD + 1:], ALU.add)
                dve.reciprocal(orc[:, sl].rearrange("p q s o -> p (q s) o"), e[:, :, HD:HD + 1]).then_inc(s["rec"], 1)

            def step(u, j):
                if live(u, 0):
                    maxima(u, j, 0)
                if live(u, 4):
                    norm(u - 4, j % 2)
                if live(u, 2):
                    w, sl = u - 2, j % 2
                    lo(w, sl, 0)
                    hi(w, sl, 1)
                    lo(w, sl, 1)
                if live(u, 0):
                    maxima(u, j, 1)
                if live(u, 2):
                    hi(u - 2, j % 2, 3)
            run(dve, step, 5)

        @block.tensor
        def _(pe):
            def scores(u, j, q):
                if q == 0:
                    pe.wait_ge(loaded[j], (u - j) * (2 * 16 // G) + 2 * 16)
                if q % 2 == 0:
                    at_least(pe, s["max"], 2 * u + q // 2)
                ins = pe.matmul(psS[:, q % 2], q_stk[0:K3, j, q * P:(q + 1) * P], k_stk[0:K3, j, :], start=True, stop=True)
                if q % 2:
                    ins.then_inc(s["s_mm"], 1)

            def max_rows(w, sl):
                pe.wait_ge(s["max"], 2 * w + 2)
                at_least(pe, s["mrow"], w)
                for q in range(TB):
                    ins = pe.transpose(psM[0:2, q * P:(q + 1) * P], nm[:, sl, q, :], ident[:, :])
                ins.then_inc(s["m_mm"], 1)

            def scores_t(w, j, k):
                if k == 0:
                    pe.wait_ge(s["mrow"], w + 1)
                    if isinstance(w, int) and w == 0:
                        pe.wait_ge(s["sel"], 3)
                at_least(pe, s["exp"], TB * w + k - 1)
                pe.matmul(psT[:, k % 2], k_stk[0:KR, j, k * P:(k + 1) * P], q_stk[0:KR, j, :], start=True, stop=True).then_inc(s["t_mm"], 1)

            def values(w, sl, q):
                if q == 0:
                    pe.wait_ge(s["h_act"], 2 * w + 2)
                    pe.wait_ge(s["h_dve"], 2 * w + 2)
                    pe.wait_ge(s["l_dve"], 2 * w + 2)
                    pe.wait_ge(s["l_pool"], 2 * w + 2)
                if q % 2 == 0:
                    at_least(pe, s["o_ev"], 2 * (w - 1) + q // 2 + 1)
                at = (q % 2) * 2 * VW
                c = slice(q * P, (q + 1) * P)
                for seg, keys in ((1, [TB - 1]), (0, range(TB))):
                    keys = list(keys)
                    dst = psO[:, q // 2, at + seg * VW:at + (seg + 1) * VW]
                    for k in keys:
                        v = v_all[:, ds(w, 1), k + seg, :].rearrange("p o v -> p (o v)")
                        pe.matmul(dst, ph[:, sl, k, c], v, start=(k == keys[0]), stop=False)
                        ins = pe.matmul(dst[:, 0:HD + 1], pl[:, sl, k, c], v[:, 0:HD + 1], start=False, stop=(k == keys[-1]))
                if q % 2:
                    ins.then_inc(s["o_mm"], 1)

            def step(u, j):
                if live(u, 0):
                    scores(u, j, 0)
                    scores(u, j, 1)
                if live(u, 2):
                    scores_t(u - 2, (j - 2) % SLOTS, 0)
                    scores_t(u - 2, (j - 2) % SLOTS, 1)
                if live(u, 1):
                    max_rows(u - 1, (j - 1) % 2)
                if live(u, 3):
                    values(u - 3, (j - 3) % 2, 0)
                    values(u - 3, (j - 3) % 2, 1)
                if live(u, 2):
                    scores_t(u - 2, (j - 2) % SLOTS, 2)
                if live(u, 0):
                    scores(u, j, 2)
                    scores(u, j, 3)
                if live(u, 3):
                    values(u - 3, (j - 3) % 2, 2)
                if live(u, 2):
                    scores_t(u - 2, (j - 2) % SLOTS, 3)
                if live(u, 3):
                    values(u - 3, (j - 3) % 2, 3)
            run(pe, step, 3)


def output(nc, t, sem, g_):
    ident, o_all = g_["ident"], g_["o_all"]
    sb = Map(nc, SBUF_LO + E_EARLY * g_["PER_E"], g_["O_AT"])
    xn2 = g_["xn2"] = sb("xn2", [P, NT, D], F32)
    logits = g_["logits"] = sb("logits", [P, NT, E + 1], F32)
    low, sb = sb, Map(nc, g_["V_AT"], SBUF_HI - g_["CONST"])
    wo_raw = sb("wo_raw", [P, KD, D], F32)
    wo = sb("wo", [P, 2, KD, D], F16)
    wr = sb("wr", [P, KD, E], F32)
    bo = sb("bo", [P, D], F32)
    x_in = low("o_x", [P, 2, D], F32)
    xb = low("o_xb", [P, 2, D], F32)
    x1 = low("o_x1", [P, 2, D], F32)
    o_in = low("o_in", [P, 2, D], F32)
    xn = low("o_xn", [P, 2, D], F32)
    oT = sb("oT", [P, 2, 2, KD, P], F16)
    nT = sb("nT", [P, KD, P], F32)
    st = sb("o_st", [P, 2, 6], F32)
    st_seen = sb("o_st_seen", [P, 1], F32)
    mv = sb("o_mv", [P, 2, 2], F32)
    ve = sb("o_ve", [P, 2, 1], F32)
    sd = sb("o_sd", [P, 2, 1], F32)
    rs = sb("o_rs", [P, 2, 1], F32)
    names = """w_loaded w_hi w_lo b_loaded xb_r oT_t oT_h oT_l y_mm x1_r stats aggr veps sd_r rs_r xn_r nT_t nT_c r_mm logit"""
    s = {n: sem("o_" + n) for n in names.split()}
    x_ld = [sem("o_x_loaded0"), sem("o_x_loaded1")]
    o_ld = [sem("o_o_copied0"), sem("o_o_copied1")]
    x1_st = [sem("o_x1_stored0"), sem("o_x1_stored1")]
    xn_st = [sem("o_xn_stored0"), sem("o_xn_stored1")]

    with ExitStack() as ps:
        def bank(name):
            return ps.enter_context(nc.psum_tensor(name, [P, 512], F32))
        psX, psY, psN, psR = (bank("o_" + n) for n in ("psX", "psY", "psN", "psR"))
        block = ps.enter_context(nc.Block())

        def g_of(b, j):
            return b * TB + j

        def loop(eng, step):
            for j in range(TB):
                step(0, j, True, False)
            with eng.Fori(1, B - 1) as b:
                for j in range(TB):
                    step(b, j, False, False)
            for j in range(TB):
                step(B - 1, j, False, True)

        @block.sync
        def _(sp):
            sp.dma_start(wo_raw[:, :, :], t["L0_xattn_Wo"].rearrange("(k p) n -> p k n", p=P)).then_inc(s["w_loaded"], 16)
            sp.dma_start(wr[:, :, :], t["L0_ffn_Wr"].rearrange("(k p) n -> p k n", p=P)).then_inc(s["b_loaded"], 16)
            sp.dma_start(bo[:, :], t["L0_xattn_bo"].partition_broadcast(P)).then_inc(s["b_loaded"], 16)
            x_rows = t["x"].rearrange("b s d -> (b s) d")

            def load(b, j):
                b, j = (b + 1, j - TB) if j >= TB else (b, j)
                g = g_of(b, j)
                at_least(sp, s["xb_r"], g - 1)
                sp.dma_start(x_in[:, j % 2], x_rows[ds(g * P, P), :]).then_inc(x_ld[j % 2], 16)
                at_least(sp, s["oT_t"], g - 1)
                sp.dma_start(o_in[:, j % 2], o_all[:, j % TB, ds(b * H, H), :].rearrange("p h d -> p (h d)")).then_inc(o_ld[j % 2], 16)
            load(0, 0)
            load(0, 1)

            def step(b, j, first, last):
                g = g_of(b, j)
                if not (last and j >= TB - 2):
                    load(b, j + 2)
                sp.wait_ge(s["x1_r"], g + 1)
                sp.dma_start(g_["x1_dram"][ds(g * P, P), :], x1[:, j % 2]).then_inc(x1_st[j % 2], 16)
                sp.wait_ge(s["xn_r"], g + 1)
                sp.dma_start(g_["xs_dram"][ds(NSLOT + g * P, P), :], xn[:, j % 2]).then_inc(xn_st[j % 2], 16)
                sp.dma_start(xn2[:, ds(g, 1), :].rearrange("p o d -> p (o d)"), xn[:, j % 2]).then_inc(xn_st[j % 2], 16)
            loop(sp, step)
            for q in x1_st:
                sp.wait_ge(q, 8 * NT)
            for q in xn_st:
                sp.wait_ge(q, 16 * NT)

        @block.gpsimd
        def _(pool):
            pool.wait_ge(s["b_loaded"], 32)

            def step(b, j, first, last):
                g = g_of(b, j)
                pool.wait_ge(x_ld[j % 2], 16 * (b * (TB // 2) + j // 2 + 1))
                at_least(pool, s["x1_r"], g - 1)
                pool.tensor_tensor(xb[:, j % 2], x_in[:, j % 2], bo[:, :], ALU.add).then_inc(s["xb_r"], 1)
            loop(pool, step)

        @block.scalar
        def _(act):
            act.wait_ge(s["w_loaded"], 16)
            act.activation(wo[:, 0], wo_raw[:, :, :], ACT.Copy, scale=WS).then_inc(s["w_hi"], 1)

            def front(b, j):
                g = g_of(b, j)
                act.wait_ge(s["oT_t"], g + 1)
                at_least(act, s["y_mm"], g - 1)
                act.activation(oT[:, j % 2, 0], psX[:, :].rearrange("p (k n) -> p k n", n=P), ACT.Copy).then_inc(s["oT_h"], 1)

            def back(b, j):
                g = g_of(b, j)
                act.wait_ge(s["nT_t"], g + 1)
                at_least(act, s["r_mm"], g)
                act.activation(nT[:, :, :], psN[:, :].rearrange("p (k n) -> p k n", n=P), ACT.Copy).then_inc(s["nT_c"], 1)

            def step(b, j, first, last):
                g = g_of(b, j)
                if not (last and j == TB - 1):
                    front(*((b, j + 1) if j < TB - 1 else (b + 1, 0)))
                act.wait_ge(s["veps"], g + 1)
                act.activation(sd[:, j % 2], ve[:, j % 2], ACT.Sqrt).then_inc(s["sd_r"], 1)
                if not (first and j == 0):
                    back(*((b, j - 1) if j else (b - 1, TB - 1)))
            front(0, 0)
            loop(act, step)
            back(B - 1, TB - 1)

        @block.vector
        def _(dve):
            dve.wait_ge(s["w_hi"], 1)
            dve.scalar_tensor_tensor(wo[:, 1].rearrange("p k n -> p (k n)"), wo_raw[:, :, :].rearrange("p k n -> p (k n)"),
                                     WS, wo[:, 0].rearrange("p k n -> p (k n)"), ALU.mult, ALU.subtract).then_inc(s["w_lo"], 1)

            def front(b, j):
                g = g_of(b, j)
                dve.wait_ge(s["oT_h"], g + 1)
                dve.tensor_tensor(oT[:, j % 2, 1], psX[:, :].rearrange("p (k n) -> p k n", n=P), oT[:, j % 2, 0],
                                  ALU.subtract).then_inc(s["oT_l"], 1)

            def step(b, j, first, last):
                g = g_of(b, j)
                if not (last and j == TB - 1):
                    front(*((b, j + 1) if j < TB - 1 else (b + 1, 0)))
                dve.wait_ge(s["y_mm"], g + 1)
                dve.wait_ge(s["xb_r"], g + 1)
                at_least(dve, x1_st[j % 2], (b * (TB // 2) + j // 2) * 16)
                dve.scalar_tensor_tensor(x1[:, j % 2], psY[:, :], 1.0 / WS, xb[:, j % 2], ALU.mult, ALU.add).then_inc(s["x1_r"], 1)
                dve.wait_ge(s["x1_r"], g + 1)
                dve.bn_stats(st[:, j % 2], x1[:, j % 2]).then_inc(s["stats"], 1)
                dve.wait_ge(s["stats"], g + 1)
                dve.tensor_copy(st_seen[:, :], st[:, j % 2, 0:1])
                dve.bn_aggr(mv[:, j % 2], st[:, j % 2]).then_inc(s["aggr"], 1)
                dve.wait_ge(s["aggr"], g + 1)
                dve.tensor_scalar(ve[:, j % 2], mv[:, j % 2, 1:2], LN_EPS, None, ALU.add).then_inc(s["veps"], 1)
                dve.wait_ge(s["sd_r"], g + 1)
                dve.reciprocal(rs[:, j % 2], sd[:, j % 2]).then_inc(s["rs_r"], 1)
                dve.wait_ge(s["rs_r"], g + 1)
                at_least(dve, xn_st[j % 2], (b * (TB // 2) + j // 2) * 32)
                at_least(dve, s["nT_t"], g - 1)
                dve.tensor_scalar(xn[:, j % 2], x1[:, j % 2], mv[:, j % 2, 0:1], rs[:, j % 2],
                                  ALU.subtract, ALU.mult).then_inc(s["xn_r"], 1)
            front(0, 0)
            loop(dve, step)
            dve.wait_ge(s["r_mm"], NT)
            dve.tensor_copy(logits[:, :, 0:E], psR[:, 0:NT * (E + 1)].rearrange("p (n e) -> p n e", e=E + 1)[:, :, 0:E]).then_inc(s["logit"], 1)

        @block.tensor
        def _(pe):
            def front(b, j):
                g = g_of(b, j)
                pe.wait_ge(o_ld[j % 2], 16 * (b * (TB // 2) + j // 2 + 1))
                at_least(pe, s["oT_l"], g)
                for c in range(KD):
                    ins = pe.transpose(psX[:, c * P:(c + 1) * P], o_in[:, j % 2, c * P:(c + 1) * P], ident[:, :])
                ins.then_inc(s["oT_t"], 1)

            def back(b, j):
                g = g_of(b, j)
                pe.wait_ge(s["xn_r"], g + 1)
                at_least(pe, s["nT_c"], g)
                for c in range(KD):
                    ins = pe.transpose(psN[:, c * P:(c + 1) * P], xn[:, j % 2, c * P:(c + 1) * P], ident[:, :])
                ins.then_inc(s["nT_t"], 1)

            def router(b, j):
                g = g_of(b, j)
                pe.wait_ge(s["nT_c"], g + 1)
                for c in range(KD):
                    ins = pe.matmul(psR[:, ds(g * (E + 1), E)], nT[:, c, :], wr[:, c, :], start=(c == 0), stop=(c == KD - 1))
                ins.then_inc(s["r_mm"], 1)

            pe.wait_ge(s["w_lo"], 1)
            pe.wait_ge(s["b_loaded"], 32)

            def step(b, j, first, last):
                g = g_of(b, j)
                before = None if first and j == 0 else ((b, j - 1) if j else (b - 1, TB - 1))
                if not (last and j == TB - 1):
                    front(*((b, j + 1) if j < TB - 1 else (b + 1, 0)))
                if before:
                    back(*before)
                pe.wait_ge(s["oT_l"], g + 1)
                at_least(pe, s["x1_r"], g)
                n = 0
                for c in range(KD):
                    for x, y in ((0, 0), (1, 0), (0, 1)):
                        ins = pe.matmul(psY[:, :], oT[:, j % 2, x, c, :], wo[:, y, c, :], start=(n == 0), stop=(n == 3 * KD - 1))
                        n += 1
                ins.then_inc(s["y_mm"], 1)
                if before:
                    router(*before)
            front(0, 0)
            loop(pe, step)
            back(B - 1, TB - 1)
            router(B - 1, TB - 1)


def route(nc, t, sem, g_):
    xn2, logits, slot, prob, pmat, blk_e = (g_[k] for k in ("xn2", "logits", "slot", "prob", "pmat", "blk_e"))
    sb = Map(nc, SBUF_LO + E_EARLY * g_["PER_E"] + (NT * D + NT * (E + 1)) * 4, g_["V_AT"])
    R = [P, NT, E]
    br = sb("br", [P, E], F32)
    gb = sb("gb", [P, E], F32)
    tri = sb("tri", [P, P], F32)
    ones = sb("ones", [P, P], F32)
    ramp_i = sb("ramp_i", [P, E], I32)
    ramp = sb("ramp", [P, E], F32)
    bidx_i = sb("bidx_i", [P, NBLK], I32)
    bidx = sb("bidx", [P, NBLK], F32)
    lg, bg, eq, cand, prod, member, within, tile_n, scan_a, scan_b, place = (
        sb("r_" + n, R, F32) for n in "lg bg eq cand prod member within tile_n scan_a scan_b place".split())
    oh = [sb(f"oh{k}", R, F32) for k in range(TOP)]
    top = sb("top", [P, NT], F32)
    sel = sb("sel_l", [P, TOP, NT], F32)
    mx = sb("r_mx", [P, NT], F32)
    ex = sb("r_ex", [P, TOP, NT], F32)
    den = sb("r_den", [P, NT], F32)
    ph16 = sb("ph16", [P, NT, E + 1], F16)
    cnt_i = sb("cnt_i", [P, E], I32)
    nblk = sb("nblk", [P, E], F32)
    cum_a = sb("cum_a", [P, E], F32)
    cum_b = sb("cum_b", [P, E], F32)
    base = sb("base", [P, E], F32)
    cum2_a = sb("cum2_a", [P, E], F32)
    cum2_b = sb("cum2_b", [P, E], F32)
    slot_f = sb("slot_f", [P, TOP, NT], F32)
    cmpb = sb("cmpb", [P, NBLK, E - 1], F32)
    blk_f = sb("blk_f", [P, NBLK], F32)
    zero = sb("zero", [P, D], F32)
    pad_i = sb("pad_i", [P, NPAD], I32)
    pad_n = sb("pad_n", [P, NPAD], F32)
    pad_c = sb("pad_c", [P, E], F32)
    pad_w = sb("pad_w", [P, NPAD, E], F32)
    pad_f = sb("pad_f", [P, NPAD], F32)
    pad = sb("pad", [P, NPAD], I32)
    names = "loaded const0 const1 iota member prefix exp_in exp slots pads scattered"
    s = {n: sem("r_" + n) for n in names.split()}
    dve_step = sem("r_dve_step")

    def over_tiles(x):
        return x.unsqueeze(1).broadcast_to(R)

    def over_experts(x):
        return x.unsqueeze(2).broadcast_to(R)

    with ExitStack() as ps:
        psW = ps.enter_context(nc.psum_tensor("r_psW", [P, 512], F32))
        psN = ps.enter_context(nc.psum_tensor("r_psN", [P, 512], F32))
        block = ps.enter_context(nc.Block())

        @block.sync
        def _(sp):
            sp.dma_start(br[:, :], t["L0_ffn_br"].partition_broadcast(P)).then_inc(s["loaded"], 16)
            sp.dma_start(gb[:, :], t["L0_ffn_gate_bias"].partition_broadcast(P)).then_inc(s["loaded"], 16)

        @block.gpsimd
        def _(pool):
            pool.memset(tri[:, :], 1.0).then_inc(s["const0"], 1)
            pool.memset(ones[:, :], 1.0).then_inc(s["const1"], 1)
            pool.iota(ramp_i[:, :], pattern=[[-1, E]], base=E, channel_multiplier=0).then_inc(s["iota"], 1)
            pool.iota(bidx_i[:, :], pattern=[[1, NBLK]], base=0, channel_multiplier=0).then_inc(s["iota"], 1)
            pool.iota(pad_i[:, :], pattern=[[P, NPAD]], base=0, channel_multiplier=1).then_inc(s["iota"], 1)
            pool.wait_ge(s["const0"], 1)
            pool.affine_select(out=tri[:, :], in_=tri[:, :], compare_op=ALU.is_ge, fill=0.0, base=-1,
                               pattern=[[1, P]], channel_multiplier=-1).then_inc(s["const1"], 1)
            pool.wait_ge(s["const1"], 2)
            pool.memset(zero[:, :], 0.0).then_inc(s["const0"], 1)
            pool.wait_ge(s["const0"], 2)
            pool.wait_ge(s["slots"], 1)
            for k in range(TOP):
                for g in range(NT):
                    pool.indirect_dma_start(g_["xs_dram"][0:NSLOT, :], bass.IndirectOffsetOnAxis(ap=slot[:, k, g:g + 1], axis=0),
                                            xn2[:, g, :], None).then_inc(s["scattered"], 16)
            pool.wait_ge(s["pads"], 1)
            for q in range(NPAD):
                pool.indirect_dma_start(g_["xs_dram"][0:NSLOT, :], bass.IndirectOffsetOnAxis(ap=pad[:, q:q + 1], axis=0),
                                        zero[:, :], None).then_inc(s["scattered"], 16)
            pool.wait_ge(s["scattered"], 16 * (TOP * NT + NPAD))

        @block.tensor
        def _(pe):
            pe.wait_ge(s["const1"], 2)
            pe.wait_ge(s["member"], 1)
            m = member[:, :, :].rearrange("p n e -> p (n e)")
            pe.matmul(psW[:, 0:NT * E], tri[:, :], m, start=True, stop=True)
            pe.matmul(psN[:, 0:NT * E], ones[:, :], m, start=True, stop=True).then_inc(s["prefix"], 1)

        @block.scalar
        def _(act):
            act.wait_ge(s["exp_in"], 1)
            act.activation(ex[:, :, :], sel[:, :, :], ACT.Exp).then_inc(s["exp"], 1)

        @block.vector
        def _(dve):
            n = [0]

            def link(ins):
                n[0] += 1
                ins.then_inc(dve_step, 1)
                dve.wait_ge(dve_step, n[0])

            dve.wait_ge(s["iota"], 3)
            link(dve.tensor_copy(ramp[:, :], ramp_i[:, :]))
            link(dve.tensor_copy(bidx[:, :], bidx_i[:, :]))
            dve.wait_ge(s["loaded"], 32)
            link(dve.tensor_tensor(lg[:, :, :], logits[:, :, 0:E], over_tiles(br[:, :]), ALU.add))
            link(dve.tensor_tensor(bg[:, :, :], lg[:, :, :], over_tiles(gb[:, :]), ALU.add))
            for k in range(TOP):
                link(dve.tensor_reduce(top[:, :], bg[:, :, :], AX.X, ALU.max))
                link(dve.tensor_tensor(eq[:, :, :], bg[:, :, :], over_experts(top[:, :]), ALU.is_equal))
                link(dve.tensor_tensor(cand[:, :, :], eq[:, :, :], over_tiles(ramp[:, :]), ALU.mult))
                link(dve.tensor_reduce(top[:, :], cand[:, :, :], AX.X, ALU.max))
                link(dve.tensor_tensor(oh[k][:, :, :], cand[:, :, :], over_experts(top[:, :]), ALU.is_equal))
                link(dve.tensor_tensor(prod[:, :, :], lg[:, :, :], oh[k][:, :, :], ALU.mult))
                link(dve.tensor_reduce(sel[:, k, :], prod[:, :, :], AX.X, ALU.add))
                if k == 0:
                    link(dve.scalar_tensor_tensor(bg[:, :, :], oh[0][:, :, :], -3.0e38, bg[:, :, :], ALU.mult, ALU.add))
            dve.tensor_tensor(member[:, :, :], oh[0][:, :, :], oh[1][:, :, :], ALU.add).then_inc(s["member"], 1)
            link(dve.tensor_tensor(mx[:, :], sel[:, 0, :], sel[:, 1, :], ALU.max))
            for k in range(TOP):
                ins = dve.tensor_tensor(sel[:, k, :], sel[:, k, :], mx[:, :], ALU.subtract)
                link(ins)
            dve.tensor_copy(den[:, :], mx[:, :]).then_inc(s["exp_in"], 1)
            dve.wait_ge(s["prefix"], 1)
            link(dve.tensor_copy(within[:, :, :], psW[:, 0:NT * E].rearrange("p (n e) -> p n e", e=E)))
            link(dve.tensor_copy(tile_n[:, :, :], psN[:, 0:NT * E].rearrange("p (n e) -> p n e", e=E)))
            src, dst = tile_n, scan_a
            step = 1
            while step < NT:
                link(dve.tensor_copy(dst[:, 0:step, :], src[:, 0:step, :]))
                link(dve.tensor_tensor(dst[:, step:NT, :], src[:, step:NT, :], src[:, 0:NT - step, :], ALU.add))
                src, dst = dst, (scan_b if dst is scan_a else scan_a)
                step *= 2
            incl = src
            link(dve.tensor_scalar(base[:, :], incl[:, NT - 1, :], float(P - 1), None, ALU.add))
            link(dve.tensor_copy(cnt_i[:, :], base[:, :]))
            link(dve.tensor_scalar(cnt_i[:, :], cnt_i[:, :], 7, None, ALU.logical_shift_right))
            link(dve.tensor_copy(nblk[:, :], cnt_i[:, :]))
            src2, dst2 = nblk, cum_a
            step = 1
            while step < E:
                link(dve.tensor_copy(dst2[:, 0:step], src2[:, 0:step]))
                link(dve.tensor_tensor(dst2[:, step:E], src2[:, step:E], src2[:, 0:E - step], ALU.add))
                src2, dst2 = dst2, (cum_b if dst2 is cum_a else cum_a)
                step *= 2
            cum = src2
            link(dve.tensor_tensor(base[:, :], cum[:, :], nblk[:, :], ALU.subtract))
            link(dve.tensor_tensor(place[:, :, :], within[:, :, :], incl[:, :, :], ALU.add))
            link(dve.tensor_tensor(place[:, :, :], place[:, :, :], tile_n[:, :, :], ALU.subtract))
            link(dve.scalar_tensor_tensor(place[:, :, :], over_tiles(base[:, :]), float(P), place[:, :, :], ALU.mult, ALU.add))
            for k in range(TOP):
                link(dve.tensor_tensor(prod[:, :, :], place[:, :, :], oh[k][:, :, :], ALU.mult))
                link(dve.tensor_reduce(slot_f[:, k, :], prod[:, :, :], AX.X, ALU.add))
            dve.tensor_copy(slot[:, :, :], slot_f[:, :, :]).then_inc(s["slots"], 1)
            link(dve.tensor_copy(pad_n[:, :], pad_i[:, :]))
            link(dve.scalar_tensor_tensor(pad_c[:, :], nblk[:, :], float(P), incl[:, NT - 1, :], ALU.mult, ALU.subtract))
            src3, dst3 = pad_c, cum2_a
            step = 1
            while step < E:
                link(dve.tensor_copy(dst3[:, 0:step], src3[:, 0:step]))
                link(dve.tensor_tensor(dst3[:, step:E], src3[:, step:E], src3[:, 0:E - step], ALU.add))
                src3, dst3 = dst3, (cum2_b if dst3 is cum2_a else cum2_a)
                step *= 2
            link(dve.tensor_tensor(pad_c[:, :], src3[:, :], pad_c[:, :], ALU.subtract))
            shape = [P, NPAD, E]
            link(dve.tensor_tensor(pad_w[:, :, :], pad_n[:, :].unsqueeze(2).broadcast_to(shape),
                                   pad_c[:, :].unsqueeze(1).broadcast_to(shape), ALU.is_ge))
            link(dve.tensor_tensor(pad_w[:, :, :], pad_w[:, :, :], incl[:, NT - 1, :].unsqueeze(1).broadcast_to(shape), ALU.mult))
            link(dve.tensor_reduce(pad_f[:, :], pad_w[:, :, :], AX.X, ALU.add))
            dve.tensor_tensor(pad[:, :], pad_f[:, :], pad_n[:, :], ALU.add).then_inc(s["pads"], 1)
            link(dve.tensor_tensor(cmpb[:, :, :], bidx[:, :].unsqueeze(2).broadcast_to([P, NBLK, E - 1]),
                                   cum[:, 0:E - 1].unsqueeze(1).broadcast_to([P, NBLK, E - 1]), ALU.is_ge))
            link(dve.tensor_reduce(blk_f[:, :], cmpb[:, :, :], AX.X, ALU.add))
            link(dve.tensor_copy(blk_e[:, :], blk_f[:, :]))
            dve.wait_ge(s["exp"], 1)
            link(dve.tensor_tensor(den[:, :], ex[:, 0, :], ex[:, 1, :], ALU.add))
            link(dve.reciprocal(den[:, :], den[:, :]))
            for k in range(TOP):
                link(dve.tensor_tensor(prob[:, k, :], ex[:, k, :], den[:, :], ALU.mult))
            link(dve.tensor_tensor(eq[:, :, :], oh[0][:, :, :], over_experts(prob[:, 0, :]), ALU.mult))
            link(dve.tensor_tensor(cand[:, :, :], oh[1][:, :, :], over_experts(prob[:, 1, :]), ALU.mult))
            link(dve.tensor_tensor(pmat[:, :, 1, 0:E], eq[:, :, :], cand[:, :, :], ALU.add))
            link(dve.memset(pmat[:, :, 1, E:E + 1], 1.0))
            link(dve.tensor_copy(ph16[:, :, :], pmat[:, :, 1, :]))
            link(dve.tensor_copy(pmat[:, :, 0, :], ph16[:, :, :]))
            link(dve.tensor_copy(pmat[:, :, 2, :], ph16[:, :, :]))
            link(dve.tensor_tensor(pmat[:, :, 1, :], pmat[:, :, 1, :], ph16[:, :, :], ALU.subtract))


def feed_forward(nc, t, sem, g_, shared, out):
    ident, w_exp, blk_e, slot, prob, pmat = (g_[k] for k in ("ident", "w_exp", "blk_e", "slot", "prob", "pmat"))
    seen, ws_tile = g_["seen"], g_["ws_tile"]
    tag = "s_" if shared else "e_"
    N = NT if shared else NBLK
    ROW0 = NSLOT if shared else 0
    sb = Map(nc, SBUF_LO + (1 if shared else E) * g_["PER_E"], SBUF_HI - g_["CONST"])
    NB = 1 if shared else E
    bias_u = sb(tag + "bias_u", [P, NB, KD], F32)
    bias_g = sb(tag + "bias_g", [P, NB, KD], F32)
    x_in = sb(tag + "x", [P, 2, D], F32)
    xT = sb(tag + "xT", [P, 2, 2, KD, P], F16)
    u = sb(tag + "u", [P, 2, KD, P], F32)
    uT = sb(tag + "uT", [P, 2, KD, P], F16)
    h = sb(tag + "h", [P, KD, P], F32)
    sl = sb(tag + "silu", [P, KD, P], F32)
    gf = sb(tag + "g", [P, KD, P], F32)
    gT = sb(tag + "gT", [P, 2, 2, KD, P], F16)
    y = sb(tag + "y", [P, 2, D], F32)
    if shared:
        x1 = sb("s_x1", [P, 2, D], F32)
        ya = sb("s_ya", [P, 2, TOP, D], F32)
        acc = sb("s_acc", [P, 2, D], F32)
        K3 = 3 * (E + 1)
        bd_raw = sb("bd_raw", [K3, D], F32)
        bd_16 = sb("bd_16", [K3, D], F32)
        bd_hi = sb("bd_hi", [K3, D], F16)
        bd = sb("bd", [K3, D], F16)
        low = sb("low", [K3, 1], F32)
        pT = sb("pT", [K3, NT, P], F16)
    else:
        raw = sb("e_raw", [P, 2, 2, D], F32)
    names = """b_loaded xT_t xT_h xT_l u_mm u_r u_h u_l g_mm h_r silu g_r g_h g_l y_mm y_r
        acc0 acc1 bd0 bd1 low pT_t pT_c"""
    s = {n: sem(tag + n) for n in names.split()}
    x_ld = [sem(tag + "x_loaded0"), sem(tag + "x_loaded1")]
    raw_ld = [sem(tag + "raw_loaded0"), sem(tag + "raw_loaded1")]
    x1_ld = [sem(tag + "x1_loaded0"), sem(tag + "x1_loaded1")]
    ga = [sem(tag + "gathered0"), sem(tag + "gathered1")]
    y_st = [sem(tag + "y_stored0"), sem(tag + "y_stored1")]

    def live(n, lag):
        return not isinstance(n, int) or 0 <= n - lag < N

    def run(eng, step, extra=0):
        for n in range(4):
            step(n, n % 2, n // 2)
        with eng.Fori(2, N // 2 - 1) as i:
            step(i * 2, 0, i)
            step(i * 2 + 1, 1, i)
        step(N - 2, 0, N // 2 - 1)
        step(N - 1, 1, N // 2 - 1)
        for j in range(extra):
            step(N + j, j, N // 2)

    def before(i, j):
        return i - 1 if j == 0 else i

    def after(i, j):
        return i if j == 0 else i + 1

    with ExitStack() as ps:
        def bank(name):
            return ps.enter_context(nc.psum_tensor(tag + name, [P, 512], F32))
        psX, psU, psG, psY, psP = (bank(n) for n in ("psX", "psU", "psG", "psY", "psP"))
        block = ps.enter_context(nc.Block())

        @block.sync
        def _(sp):
            def load(n, j):
                at_least(sp, s["xT_t"], n - 1)
                sp.dma_start(x_in[:, j % 2], g_["xs_dram"][ds(n * P + ROW0, P), :]).then_inc(x_ld[j % 2], 16)
                if shared:
                    at_least(sp, s["acc0"], n - 1)
                    sp.dma_start(x1[:, j % 2], g_["x1_dram"][ds(n * P, P), :]).then_inc(x1_ld[j % 2], 16)

            dst = out.rearrange("b s d -> (b s) d") if shared else g_["ys_dram"]

            def step(n, j, i):
                if isinstance(n, int):
                    if n + 2 < N:
                        load(n + 2, j)
                else:
                    load(n + 2, j)
                if live(n, 1):
                    sp.wait_ge(s["y_r"], n)
                    sp.dma_start(dst[ds((n - 1) * P, P), :], y[:, (j - 1) % 2]).then_inc(y_st[(j - 1) % 2], 16)
            load(0, 0)
            load(1, 1)
            run(sp, step, 1)
            for q in y_st:
                sp.wait_ge(q, 8 * N)

        @block.gpsimd
        def _(pool):
            if shared:
                pool.memset(low[:, :], -1.0).then_inc(s["low"], 1)
                pool.wait_ge(s["low"], 1)
                pool.affine_select(out=low[:, :], in_=low[:, :], compare_op=ALU.is_ge, fill=0.0, base=-2 * (E + 1),
                                   pattern=[[0, 1]], channel_multiplier=1).then_inc(s["low"], 1)
                for n in range(NT):
                    at_least(pool, s["acc1"], n - 1)
                    for k in range(TOP):
                        pool.indirect_dma_start(ya[:, n % 2, k, :], None, g_["ys_dram"],
                                                bass.IndirectOffsetOnAxis(ap=slot[:, k, n:n + 1], axis=0)).then_inc(ga[n % 2], 16)
            else:
                def load(x, m, half):
                    g_["load_half"](pool, raw[:, half], raw_ld[half], x, m)

                def expert_halves(e, last):
                    for m in range(NM):
                        for half in range(2):
                            n = e * (2 * NM) + 2 * m + half
                            for piece in range(3):
                                g_["split_half"](pool, raw[:, half], raw_ld[half], (e - E_EARLY) * NM + m + 1, e * 2 + half, m, n, piece)
                            if last and m == NM - 1:
                                continue
                            pool.wait_ge(g_["split_done"], n + 2)
                            if not isinstance(e, int):
                                pool.tensor_tensor(seen[:, :], ws_tile[:, :], ws_tile[:, :], ALU.add)
                            load(*((e * 2 + half, m + 1) if m < NM - 1 else ((e + 1) * 2 + half, 0)), half)
                for half in range(2):
                    load(2 * E_EARLY + half, 0, half)
                with pool.Fori(E_EARLY, E - 1) as e:
                    expert_halves(e, False)
                expert_halves(E - 1, False)
                pool.wait_ge(s["y_mm"], B * S // P)
                expert_halves(E, True)

        @block.scalar
        def _(act):
            names_b = ("L0_ffn_bsu", "L0_ffn_bsg") if shared else ("L0_ffn_bup", "L0_ffn_bgate")
            with nc.allow_non_contiguous_dma(reason="biases by feature, once"):
                for dst, name in zip((bias_u, bias_g), names_b):
                    for e in range(NB):
                        src = t[name] if shared else t[name][e]
                        act.dma_start(dst[:, e, :], src.rearrange("(k p) -> p k", p=P)).then_inc(s["b_loaded"], 16)
            if shared:
                for r in range(3):
                    act.dma_start(bd_raw[r * (E + 1):r * (E + 1) + E, :], t["L0_ffn_bdown"]).then_inc(s["b_loaded"], 16)
                    act.dma_start(bd_raw[r * (E + 1) + E:(r + 1) * (E + 1), :],
                                  t["L0_ffn_bsd"].rearrange("(o n) -> o n", o=1)).then_inc(s["b_loaded"], 16)

            def step(n, j, i):
                if live(n, -1):
                    act.wait_ge(s["xT_t"], n + 2)
                    at_least(act, s["u_mm"], n)
                    act.activation(xT[:, (j + 1) % 2, 0], psX[:, :].rearrange("p (k n) -> p k n", n=P), ACT.Copy).then_inc(s["xT_h"], 1)
                if live(n, 0):
                    act.wait_ge(s["u_r"], n + 1)
                    at_least(act, s["g_mm"], n)
                    act.activation(uT[:, 0], u[:, j % 2], ACT.Copy).then_inc(s["u_h"], 1)
                if live(n, 1) and not shared:
                    act.wait_ge(s["y_mm"], n)
                    at_least(act, y_st[(j - 1) % 2], before(i, j) * 16)
                    act.activation(y[:, (j - 1) % 2], psY[:, :], ACT.Copy, scale=1.0 / WS).then_inc(s["y_r"], 1)
                if live(n, 0):
                    act.wait_ge(s["h_r"], n + 1)
                    at_least(act, s["g_r"], n)
                    act.activation(sl[:, :, :], h[:, :, :], ACT.Silu).then_inc(s["silu"], 1)
                    act.wait_ge(s["g_r"], n + 1)
                    at_least(act, s["y_mm"], n - 1)
                    act.activation(gT[:, j % 2, 0], gf[:, :, :], ACT.Copy).then_inc(s["g_h"], 1)
            step(-1, 1, -1)
            run(act, step, 1)

        @block.vector
        def _(dve):
            if shared:
                dve.wait_ge(s["b_loaded"], 16 * 8)
                dve.tensor_scalar(bd_hi[:, :], bd_raw[:, :], WS, None, ALU.mult).then_inc(s["bd0"], 1)
                dve.tensor_scalar(bd_16[:, :], bd_raw[:, :], WS, None, ALU.mult).then_inc(s["bd0"], 1)
                dve.wait_ge(s["bd0"], 2)
                dve.wait_ge(s["low"], 2)
                dve.scalar_tensor_tensor(bd[:, :], bd_hi[:, :], low[:, :], bd_16[:, :], ALU.mult, ALU.add).then_inc(s["bd1"], 1)
                for q in range(NT // 4):
                    dve.wait_ge(s["pT_t"], q + 1)
                    dve.tensor_copy(pT[:, 4 * q:4 * q + 4, :].rearrange("p n t -> p (n t)"), psP[0:K3, :]).then_inc(s["pT_c"], 1)
            else:
                dve.wait_ge(s["b_loaded"], 16 * 2 * NB)

            def expert(n):
                if shared:
                    return 0
                return dve.value_load(blk_e[0:1, ds(n, 1)], min_val=0, max_val=E - 1)

            def biased(dst, ps_, bias, e):
                b = bias[:, ds(e, 1), :].rearrange("p o k -> p (o k)").unsqueeze(2).broadcast_to([P, KD, P])
                return dve.scalar_tensor_tensor(dst, ps_[:, :].rearrange("p (k n) -> p k n", n=P), 1.0 / WS, b, ALU.mult, ALU.add)

            def step(n, j, i):
                if live(n, -1):
                    dve.wait_ge(s["xT_h"], n + 2)
                    dve.tensor_tensor(xT[:, (j + 1) % 2, 1], psX[:, :].rearrange("p (k n) -> p k n", n=P), xT[:, (j + 1) % 2, 0],
                                      ALU.subtract).then_inc(s["xT_l"], 1)
                if live(n, 0):
                    e = expert(n)
                    dve.wait_ge(s["u_mm"], n + 1)
                    biased(u[:, j % 2], psU, bias_u, e).then_inc(s["u_r"], 1)
                    dve.wait_ge(s["u_h"], n + 1)
                    dve.tensor_tensor(uT[:, 1], u[:, j % 2], uT[:, 0], ALU.subtract).then_inc(s["u_l"], 1)
                if shared and live(n, 1):
                    total(n - 1, (j - 1) % 2, before(i, j))
                if live(n, 0):
                    dve.wait_ge(s["g_mm"], n + 1)
                    at_least(dve, s["silu"], n)
                    biased(h[:, :, :], psG, bias_g, e).then_inc(s["h_r"], 1)
                    dve.wait_ge(s["silu"], n + 1)
                    at_least(dve, s["g_l"], n)
                    dve.tensor_tensor(gf[:, :, :], sl[:, :, :], u[:, j % 2], ALU.mult).then_inc(s["g_r"], 1)
                    dve.wait_ge(s["g_h"], n + 1)
                    dve.tensor_tensor(gT[:, j % 2, 1], gf[:, :, :], gT[:, j % 2, 0], ALU.subtract).then_inc(s["g_l"], 1)

            def total(m, jj, before):
                dve.wait_ge(ga[jj], before * 32 + 32)
                dve.wait_ge(x1_ld[jj], before * 16 + 16)
                dve.scalar_tensor_tensor(acc[:, 0], ya[:, jj, 0, :], prob[:, 0, ds(m, 1)], x1[:, jj], ALU.mult, ALU.add).then_inc(s["acc0"], 1)
                dve.wait_ge(s["acc0"], m + 1)
                dve.scalar_tensor_tensor(acc[:, 1], ya[:, jj, 1, :], prob[:, 1, ds(m, 1)], acc[:, 0], ALU.mult, ALU.add).then_inc(s["acc1"], 1)
                dve.wait_ge(s["acc1"], m + 1)
                dve.wait_ge(s["y_mm"], m + 1)
                at_least(dve, y_st[jj], before * 16)
                dve.scalar_tensor_tensor(y[:, jj], psY[:, :], 1.0 / WS, acc[:, 1], ALU.mult, ALU.add).then_inc(s["y_r"], 1)

            step(-1, 1, -1)
            run(dve, step, 1)

        @block.tensor
        def _(pe):
            def transpose(n, slot_, loads):
                pe.wait_ge(x_ld[slot_], loads * 16 + 16)
                at_least(pe, s["xT_l"], n)
                for c in range(KD):
                    ins = pe.transpose(psX[:, c * P:(c + 1) * P], x_in[:, slot_, c * P:(c + 1) * P], ident[:, :])
                ins.then_inc(s["xT_t"], 1)

            def weights(e, m, part, c, cols):
                return w_exp[:, ds(e * 2 + c // 2, 1), m, part, c % 2, cols].rearrange("p o n -> p (o n)")

            def features(dst, e, m, act_hi, act_lo):
                for f in range(KD):
                    cols = slice(f * P, (f + 1) * P)
                    i = 0
                    for c in range(KD):
                        for part, a in ((0, act_hi), (0, act_lo), (1, act_hi)):
                            ins = pe.matmul(dst[:, cols], weights(e, m, part, c, cols), a[:, c, :], start=(i == 0), stop=(i == 3 * KD - 1))
                            i += 1
                return ins

            def down(m, jj, e):
                pe.wait_ge(s["g_l"], m + 1)
                at_least(pe, s["y_r"], m)
                terms = [(gT[:, jj, x, c, :], weights(e, 2, y_, c, slice(0, D))) for c in range(KD) for x, y_ in ((0, 0), (1, 0), (0, 1))]
                if shared:
                    terms.insert(0, (pT[:, ds(m, 1), :].rearrange("p o n -> p (o n)"), bd[:, :]))
                for i, (a, w) in enumerate(terms):
                    ins = pe.matmul(psY[:, :], a, w, start=(i == 0), stop=(i == len(terms) - 1))
                ins.then_inc(s["y_mm"], 1)

            def expert(n):
                if shared:
                    return 0
                return pe.value_load(blk_e[0:1, ds(n, 1)], min_val=0, max_val=E - 1)

            def step(n, j, i):
                if live(n, -1):
                    transpose(n + 1, (j + 1) % 2, after(i, j))
                if live(n, 0):
                    e = expert(n)
                    if not shared:
                        pe.wait_ge(g_["split_done"], e * (2 * NM) + 2 * NM + 1)
                    pe.wait_ge(s["xT_l"], n + 1)
                    at_least(pe, s["u_r"], n)
                    features(psU, e, 0, xT[:, j % 2, 0], xT[:, j % 2, 1]).then_inc(s["u_mm"], 1)
                if live(n, 1):
                    down(n - 1, (j - 1) % 2, expert(n - 1))
                if live(n, 0):
                    pe.wait_ge(s["u_l"], n + 1)
                    at_least(pe, s["h_r"], n)
                    features(psG, e, 1, uT[:, 0], uT[:, 1]).then_inc(s["g_mm"], 1)
            if shared:
                pe.wait_ge(s["bd1"], 1)
                for q in range(NT // 4):
                    at_least(pe, s["pT_c"], q)
                    for i in range(4):
                        ins = pe.transpose(psP[0:K3, i * P:(i + 1) * P], pmat[:, 4 * q + i, :, :].rearrange("p a e -> p (a e)"), ident[:, :])
                    ins.then_inc(s["pT_t"], 1)
                pe.wait_ge(s["pT_c"], NT // 4)
            step(-1, 1, -1)
            run(pe, step, 1)


def kernel(**inputs):
    import concourse.bacc as bacc
    from concourse.bass_utils import run_bass_kernel_spmd

    nc = bacc.Bacc("TRN2", target_bir_lowering=False, num_devices=1)
    arrays = {f"in_{name}_dram": np.ascontiguousarray(a) for name, a in inputs.items()}
    t = {name: nc.dram_tensor(f"in_{name}_dram", a.shape, mybir.dt.from_np(np.asarray(a).dtype), kind="ExternalInput").ap()
         for name, a in inputs.items()}
    out = nc.dram_tensor("out_0_dram", (B, S, D), F32, kind="ExternalOutput").ap()
    build(nc, t, out)
    r = run_bass_kernel_spmd(nc, [arrays], core_ids=[0])
    return r.results[0]["out_0_dram"]
```

```python
from contextlib import ExitStack

import numpy as np

import concourse.bass as bass
from concourse import mybir

F32 = mybir.dt.float32
F16 = mybir.dt.float16
I32 = mybir.dt.int32
U32 = mybir.dt.uint32
ALU = mybir.AluOpType
ACT = mybir.ActivationFunctionType
AX = mybir.AxisListType
ds = bass.ds

P = 128
B = 4
S = 512
D = 512
C = 256
H = 16
HD = D // H
NDCA = 16
NMAIN = S - NDCA
TB = S // P
NT = B * TB
KD = D // P
KC = C // P
CH = D // P
E = 7
NM = 3
TOP = 2
NBLK = (B * S * TOP + E * (P - 1)) // P
NSLOT = NBLK * P
NFIRST = 6
NPAD = NBLK - TOP * NT
WS = 16.0
QS = 32.0
LN_EPS = 1e-5
HEAD_EPS = 1e-6
VSEG = 5
VW = 2 * HD + 1
PAIR = 2
SBUF_LO, SBUF_HI = 16512, 229344


def at_least(eng, sem, value):
    if isinstance(value, int) and value <= 0:
        return
    eng.wait_ge(sem, value)


class Map:

    def __init__(self, nc, base, limit):
        self.nc, self.at, self.limit = nc, base, limit

    def __call__(self, name, shape, dt):
        size = int(np.prod(shape[1:])) * (2 if dt == F16 else 4)
        t = self.nc.alloc_sbuf_tensor_at(name, shape, dt, offset=self.at)
        self.at += -(-size // 32) * 32
        assert self.at <= self.limit, (name, self.at, self.limit)
        return t


def build(nc, t, out, upto=99, dbg=None):
    ctx = ExitStack()

    mine = []

    def sem(name):
        mine.append(nc.alloc_semaphore(name=name))
        return mine[-1]

    def end_stage():
        nc.clear_and_free_semaphores(mine)
        nc.all_engine_barrier()
        mine.clear()

    def dram(name, shape, dt):
        return nc.dram_tensor(name, shape, dt, kind="Internal").ap()

    with ctx:
        q_dram = dram("q_dram", (3, B * D, S), F16)
        k_dram = dram("k_dram", (3, B * D, S), F16)
        x1_dram = dram("x1_dram", (B * S, D), F32)
        xn_dram = dram("xn_dram", (B * S, D), F32)
        xs_dram = dram("xs_dram", (NSLOT, D), F32)
        ys_dram = dram("ys_dram", (NSLOT, D), F32)
        yf_dram = dram("yf_dram", (NFIRST * P, D), F32)

        W_BYTES = E * NM * 2 * KD * D * 2
        PER_E = W_BYTES // E
        w_exp = nc.alloc_sbuf_tensor_at("w_exp", [P, 2 * E, NM, 2, KD // 2, D], F16, offset=SBUF_LO)
        V_BYTES = B * H * VSEG * VW * 2
        O_BYTES = B * H * TB * HD * 4
        CONST = 2848
        const = Map(nc, SBUF_HI - CONST, SBUF_HI)
        ident = const("ident", [P, P], F32)
        m_main = const("m_main", [P, 1], F32)
        m_dca = const("m_dca", [P, 1], F32)
        slot = const("slot", [P, TOP, NT], I32)
        prob = const("prob", [P, TOP, NT], F32)
        pmat = const("pmat", [P, NT, 3, E + 1], F32)
        blk_k = const("blk_k", [P, NFIRST + NBLK], I32)
        blk_w = const("blk_w", [P, NFIRST + NBLK], I32)
        ws_tile = const("ws_tile", [P, 1], F32)
        seen = const("seen", [P, 1], F32)
        KB = 2 * (E + 1)
        AUX_AT = SBUF_HI - CONST - 4096
        bias = nc.alloc_sbuf_tensor_at("bias", [KB, 2, D], F16, offset=AUX_AT)
        pick = nc.alloc_sbuf_tensor_at("pick", [KB, E + 1, P], F16, offset=AUX_AT + 2048)
        WO_AT = SBUF_HI - CONST - 2 * KD * D * 2
        wo = nc.alloc_sbuf_tensor_at("wo", [P, 2, KD, D], F16, offset=WO_AT)
        V_AT = (WO_AT - V_BYTES) // 32 * 32
        v_all = nc.alloc_sbuf_tensor_at("v_all", [P, B * H, VSEG, VW], F16, offset=V_AT)
        O_AT = V_AT - O_BYTES
        o_all = nc.alloc_sbuf_tensor_at("o_all", [P, TB, B * H, HD], F32, offset=O_AT)
        w_names = ("L0_ffn_Wup", "L0_ffn_Wgate", "L0_ffn_Wdown")
        s_dram = [t[n].rearrange("(k p) n -> p k n", p=P) for n in ("L0_ffn_Wsu", "L0_ffn_Wsg", "L0_ffn_Wsd")]
        w_dram = [t[n].rearrange("e (k p) n -> p (e k) n", p=P) for n in w_names]
        qk_stored = [[sem(f"{x}_stored{k}") for k in range(2)] for x in "qk"]
        split_done = sem("w_split_done")
        w_scaled = sem("w_scaled")
        mine.clear()

        def load_half(eng, raw, loaded, k, half, m):
            shared = isinstance(k, int) and k in (0, E + 1)
            src = s_dram[m][:, ds(half * 2, 2), :] if shared else w_dram[m][:, ds((k - 1) * KD + half * 2, 2), :]
            eng.dma_start(raw, src).then_inc(loaded, 16)

        def split_half(pool, raw, loaded, arrived, k, half, m, n, piece):
            x = (k % E if isinstance(k, int) else k) * 2 + half
            hi, lo = (w_exp[:, ds(x, 1), m, y, :, :].rearrange("p o k n -> p (o k n)") for y in range(2))
            w = raw.rearrange("p k n -> p (k n)")
            ws = ws_tile[:, :].broadcast_to([P, KD // 2 * D])
            if piece == 0:
                pool.wait_ge(loaded, 16 * arrived)
                pool.tensor_tensor(hi, w, ws, ALU.mult).then_inc(w_scaled, 1)
            elif piece == 1:
                pool.wait_ge(w_scaled, 2 * n + 1)
                pool.tensor_tensor(seen[:, :], ws_tile[:, :], ws_tile[:, :], ALU.add)
                pool.tensor_scalar(w, w, WS, 0.0, ALU.mult, ALU.add).then_inc(w_scaled, 1)
            else:
                pool.wait_ge(w_scaled, 2 * n + 2)
                pool.tensor_tensor(lo, w, hi, ALU.subtract).then_inc(split_done, 1)

        plan = dict(locals())
        project(nc, t, sem, plan)
        end_stage()
        if upto > 1:
            attend(nc, t, sem, plan)
        if upto > 2:
            output(nc, t, sem, plan)
            route(nc, t, sem, plan)
        if upto > 3:
            feed_forward(nc, t, sem, plan, False, out)
            feed_forward(nc, t, sem, plan, True, out)
        if dbg is not None:
            dbg(nc, plan, sem)


def project(nc, t, sem, g_):
    ident, v_all, m_main, m_dca = (g_[k] for k in ("ident", "v_all", "m_main", "m_dca"))
    q_dram, k_dram = g_["q_dram"], g_["k_dram"]
    sb = Map(nc, SBUF_LO, g_["V_AT"])
    wq_raw = sb("wq_raw", [P, KD, D], F32)
    wkv_raw = sb("wkv_raw", [P, KC, 2 * D], F32)
    wdca_raw = sb("wdca_raw", [P, KC, 2 * D], F32)
    wq = sb("wq", [P, 2, KD, D], F16)
    wkv = sb("wkv", [P, 2, KC, 2 * D], F16)
    wdca = sb("wdca", [P, 2, KC, 2 * D], F16)
    bq = sb("bq", [P, D], F32)
    bkv = sb("bkv", [P, 2, 2 * D], F32)
    wsum = sb("wsum", [P, KD + 2 * KC + 3, H], F32)
    affine = sb("affine", [6, P], F32)
    affine_s = sb("affine_s", [P, 6], F32)
    x_in = sb("x_in", [P, 2, D], F32)
    c_in = sb("c_in", [P, 2, C], F32)
    st = sb("st", [P, 2, 6], F32)
    st_seen = sb("st_seen", [P, 1], F32)
    mv = sb("mv", [P, 2, 2], F32)
    ve = sb("ve", [P, 2, 1], F32)
    sd = sb("sd", [P, 2, 1], F32)
    rs = sb("rs", [P, 2, 1], F32)
    xn = sb("xn", [P, 2, D], F32)
    xT = sb("xT", [P, 2, 2, KD, P], F16)
    cT = sb("cT", [P, 2, 2, KC, P], F16)
    cTm = sb("cTm", [P, 2, KC, P], F16)
    cTd = sb("cTd", [P, 2, KC, P], F16)
    qf = sb("qf", [P, 2, D], F32)
    kf = sb("kf", [P, 2, D], F32)
    vf = sb("vf", [P, 2, D], F32)
    vm = sb("vm", [P, 2, D], F32)
    sq = sb("sq", [P, 2, D], F32)
    hv = sb("hv", [P, 2, 2 * H], F32)
    hs_ = sb("hs_", [P, 2, 2 * H], F32)
    hr = sb("hr", [P, 2, 2 * H], F32)
    qn = sb("qn", [P, D], F32)
    kn = sb("kn", [P, D], F32)
    qa = sb("qa", [P, CH, P], F32)
    ka = sb("ka", [P, CH, P], F32)
    q_st = sb("q_st", [P, 2, 2, CH, PAIR * P], F16)
    k_st = sb("k_st", [P, 2, 2, CH, PAIR * P], F16)

    names = """consts masks wq_ld wkv_ld wdca_ld b_loaded a_loaded w_sum w_cent b_cent w_16 w_hi wq_lo w_lo aff_t aff
        stats aggr veps sd_r rs_r xn_r xT_t cT_t xT_h cT_h xT_l cT_l q_mm k_mm v_mm q_ev k_ev v_ev
        sq_r hv_s hv_r hs_r hr_r qn_r kn_r vm_r v_h v_l qT_t kT_t qa_r ka_r q_h k_h q_l k_l"""
    s = {n: sem("p_" + n) for n in names.split()}
    x_ld = [sem("p_x_loaded0"), sem("p_x_loaded1")]
    c_ld = [sem("p_c_loaded0"), sem("p_c_loaded1")]
    st_q, st_k = g_["qk_stored"]

    with ExitStack() as ps:
        def bank(name):
            return ps.enter_context(nc.psum_tensor(name, [P, 512], F32))
        psX, psC, psQ, psK, psV, psQT, psKT = (bank("p_" + n) for n in ("psX", "psC", "psQ", "psK", "psV", "psQT", "psKT"))
        block = ps.enter_context(nc.Block())

        def g_of(b, j):
            return b * TB + j

        def load(sp, b, j):
            if isinstance(b, int):
                b, j = b + j // TB, j % TB
            else:
                b, j = (b + 1, j - TB) if j >= TB else (b, j)
            g = g_of(b, j)
            at_least(sp, s["xn_r"], g - 1)
            sp.dma_start(x_in[:, j % 2], t["x"][b, j * P:(j + 1) * P, :] if isinstance(b, int)
                         else t["x"].rearrange("b s d -> (b s) d")[ds(g * P, P), :]).then_inc(x_ld[j % 2], 16)
            at_least(sp, s["cT_t"], g - 1)
            sp.dma_start(c_in[:, j % 2], t["ctx_1024"].rearrange("b s d -> (b s) d")[ds(g * P, P), :]).then_inc(c_ld[j % 2], 16)

        def store(sp, b, j):
            if j < 0:
                b, j = b - 1, j + TB
            g = g_of(b, j)
            slot = j // PAIR
            for buf, dst, hi, lo, done in ((q_st, q_dram, "q_h", "q_l", st_q), (k_st, k_dram, "k_h", "k_l", st_k)):
                sp.wait_ge(s[hi], g + 1)
                sp.wait_ge(s[lo], g + 1)
                for r, part in enumerate((0, 0, 1) if dst is q_dram else (0, 1, 0)):
                    d = dst[r, ds(b * D, D), slot * PAIR * P:(slot + 1) * PAIR * P]
                    sp.dma_start(d.rearrange("(c p) t -> p c t", p=P), buf[:, slot, part]).then_inc(done[slot], 16)

        def later(b, j, n):
            return (b, j + n) if j + n < TB else (b + 1, j + n - TB)

        def earlier(b, j, n):
            return (b, j - n) if j >= n else (b - 1, j - n + TB)

        def w_view(w, natural):
            return w.rearrange("p (h two d) -> p h two d" if natural else "p (two h d) -> p h two d", two=2, d=HD)

        def k_cols(w):
            return w_view(w, True)[:, :, 0, :]

        def v_cols(w):
            return w_view(w, True)[:, :, 1, :]

        def v_view(b, seg):
            return v_all[:, ds(b * H, H), seg, :]

        @block.sync
        def _(sp):
            def rows(name):
                return t[name].rearrange("(k p) n -> p k n", p=P)
            load(sp, 0, 0)
            sp.dma_start(wq_raw[:, :, :], rows("L0_xattn_Wq")).then_inc(s["wq_ld"], 16)
            load(sp, 0, 1)
            sp.dma_start(wkv_raw[:, :, 0:D], rows("L0_xattn_Wk")).then_inc(s["wkv_ld"], 16)
            sp.dma_start(wkv_raw[:, :, D:2 * D], rows("L0_xattn_Wv")).then_inc(s["wkv_ld"], 16)
            sp.dma_start(wdca_raw[:, :, :], rows("L0_xattn_Wkv_dca")).then_inc(s["wdca_ld"], 16)
            load(sp, 0, 2)

            def steps(b, last):
                for j in range(TB):
                    if not (last and j >= TB - 3):
                        load(sp, b, j + 3)
                    if j % PAIR and not (isinstance(b, int) and b == 0 and j == 1):
                        store(sp, b, j - 2)
            steps(0, False)
            with sp.Fori(1, B - 1) as b:
                steps(b, False)
            steps(B - 1, True)
            store(sp, B - 1, TB - 1)

        @block.gpsimd
        def _(pool):
            pool.memset(ident[:, :], 0.0).then_inc(s["consts"], 1)
            pool.memset(m_dca[:, :], 0.0).then_inc(s["consts"], 1)
            pool.memset(m_main[:, :], 1.0).then_inc(s["consts"], 1)
            pool.wait_ge(s["consts"], 3)
            pool.affine_select(out=ident[:, :], in_=ident[:, :], compare_op=ALU.not_equal, fill=1.0, base=0,
                               pattern=[[-1, P]], channel_multiplier=1).then_inc(s["masks"], 1)
            pool.affine_select(out=m_main[:, :], in_=m_main[:, :], compare_op=ALU.is_ge, fill=0.0, base=P - NDCA - 1,
                               pattern=[[0, 1]], channel_multiplier=-1).then_inc(s["masks"], 1)
            pool.affine_select(out=m_dca[:, :], in_=m_dca[:, :], compare_op=ALU.is_ge, fill=1.0, base=P - NDCA - 1,
                               pattern=[[0, 1]], channel_multiplier=-1).then_inc(s["masks"], 1)
            pool.memset(v_all[:, :, 0:3, HD:HD + 1], 1.0).then_inc(s["masks"], 1)
            pool.memset(cTm[:, :, :, :], 0.0).then_inc(s["masks"], 1)
            pool.memset(cTd[:, :, :, :], 0.0).then_inc(s["masks"], 1)

            for n, (src, dst) in enumerate(((wkv_raw, wkv), (wdca_raw, wdca))):
                for c in range(KC):
                    pool.wait_ge(s["w_hi"], KC * n + c + 2)
                    pool.tensor_tensor(w_view(dst[:, 1, c, :], False), w_view(src[:, c, :], n == 0), w_view(dst[:, 0, c, :], False),
                                       ALU.subtract).then_inc(s["w_lo"], 1)

            def mid(b, j):
                g = g_of(b, j)
                pool.wait_ge(s["hr_r"], g + 1)
                for n, (src, dst, dn, free) in enumerate(((qf, qn, "qn_r", "qT_t"), (kf, kn, "kn_r", "kT_t"))):
                    at_least(pool, s[free], g)
                    r = hr[:, j % 2, n * H:(n + 1) * H].unsqueeze(2).broadcast_to([P, H, HD])
                    pool.tensor_tensor(dst[:, :].rearrange("p (h d) -> p h d", d=HD),
                                       src[:, j % 2].rearrange("p (h d) -> p h d", d=HD), r, ALU.mult).then_inc(s[dn], 1)
                if j < TB - 1:
                    pool.wait_ge(s["v_h"], b * (TB + 1) + j + 1)
                    v = v_view(b, j)
                    pool.tensor_tensor(v[:, :, HD + 1:], vf[:, j % 2].rearrange("p (h d) -> p h d", d=HD),
                                       v[:, :, 0:HD], ALU.subtract).then_inc(s["v_l"], 1)
                else:
                    for n in range(2):
                        pool.wait_ge(s["v_h"], b * (TB + 1) + j + 1 + n)
                        v = v_view(b, j + n)
                        pool.tensor_tensor(v[:, :, HD + 1:], vm[:, n].rearrange("p (h d) -> p h d", d=HD),
                                           v[:, :, 0:HD], ALU.subtract).then_inc(s["v_l"], 1)

            def back(b, j):
                g = g_of(b, j)
                for buf, src, hi, dn in ((q_st, qa, "q_h", "q_l"), (k_st, ka, "k_h", "k_l")):
                    pool.wait_ge(s[hi], g + 1)
                    c = (j % PAIR) * P
                    pool.tensor_tensor(buf[:, j // PAIR, 1, :, c:c + P], src[:, :, :],
                                       buf[:, j // PAIR, 0, :, c:c + P], ALU.subtract).then_inc(s[dn], 1)

            def steps(b, first):
                for j in range(TB):
                    if not (first and j < 2):
                        back(*earlier(b, j, 2))
                    mid(b, j)
            steps(0, True)
            with pool.Fori(1, B) as b:
                steps(b, False)
            back(B - 1, TB - 2)
            back(B - 1, TB - 1)

        @block.scalar
        def _(act):
            act.dma_start(bq[:, :], t["L0_xattn_bq"].partition_broadcast(P)).then_inc(s["b_loaded"], 16)
            for n, name in enumerate(("qn_w", "qn_b", "kn_w", "kn_b", "kn_dca_w", "kn_dca_b")):
                act.dma_start(affine[n:n + 1, :].rearrange("o (q d) -> o q d", d=HD),
                              t["L0_xattn_" + name].rearrange("(o r d) -> o r d", o=1, r=1).broadcast_to([1, P // HD, HD])
                              ).then_inc(s["a_loaded"], 16)
            for v, n in ((0, P), (1, P - NDCA)):
                for half, name in ((0, "L0_xattn_bk"), (1, "L0_xattn_bv")):
                    act.dma_start(bkv[0:n, v, half * D:(half + 1) * D], t[name].partition_broadcast(n)).then_inc(s["b_loaded"], 16)
            for kv in range(2):
                dst = w_view(bkv[P - NDCA:P, 1, :], True)[:, :, kv, :]
                src = t["L0_xattn_bkv_dca"][kv * D:(kv + 1) * D].rearrange("(h d) -> h d", d=HD)
                act.dma_start(dst, src.partition_broadcast(NDCA)).then_inc(s["b_loaded"], 16)

            def sqrt(b, j):
                act.wait_ge(s["veps"], g_of(b, j) + 1)
                act.activation(sd[:, j % 2], ve[:, j % 2], ACT.Sqrt).then_inc(s["sd_r"], 1)

            def front(b, j):
                g = g_of(b, j)
                act.wait_ge(s["xT_t"], g + 1)
                at_least(act, s["q_mm"], g - 1)
                act.activation(xT[:, j % 2, 0], psX[:, :].rearrange("p (k n) -> p k n", n=P), ACT.Copy).then_inc(s["xT_h"], 1)
                act.wait_ge(s["cT_t"], g + 1)
                pc = psC[:, 0:C].rearrange("p (k n) -> p k n", n=P)
                if j < TB - 1:
                    at_least(act, s["v_mm"], g - 1)
                    act.activation(cT[:, j % 2, 0], pc, ACT.Copy).then_inc(s["cT_h"], 1)
                else:
                    at_least(act, s["v_mm"], g - TB + 1)
                    m = P - NDCA
                    act.activation(cTm[:, 0, :, 0:m], pc[:, :, 0:m], ACT.Copy)
                    act.activation(cTd[:, 0, :, m:P], pc[:, :, m:P], ACT.Copy).then_inc(s["cT_h"], 1)

            def mid(b, j):
                g = g_of(b, j)
                at_least(act, s["hv_s"], g)
                act.wait_ge(s["q_ev"], g + 1)
                act.activation(sq[:, 0], qf[:, j % 2], ACT.Square)
                act.wait_ge(s["k_ev"], g + 1)
                act.activation(sq[:, 1], kf[:, j % 2], ACT.Square).then_inc(s["sq_r"], 1)
                if j < TB - 1:
                    act.wait_ge(s["v_ev"], g + 1)
                    act.activation(v_view(b, j)[:, :, 0:HD], vf[:, j % 2].rearrange("p (h d) -> p h d", d=HD),
                                   ACT.Copy).then_inc(s["v_h"], 1)
                else:
                    for n in range(2):
                        act.wait_ge(s["vm_r"], 2 * b + n + 1)
                        act.activation(v_view(b, j + n)[:, :, 0:HD], vm[:, n].rearrange("p (h d) -> p h d", d=HD),
                                       ACT.Copy).then_inc(s["v_h"], 1)
                act.wait_ge(s["hv_r"], g + 1)
                act.activation(hs_[:, j % 2], hv[:, j % 2], ACT.Sqrt).then_inc(s["hs_r"], 1)

            def back(b, j):
                g = g_of(b, j)
                act.wait_ge(s["aff"], 1)
                gp = b * (TB // PAIR) + j // PAIR
                for buf, a, p_t, tt, dn, hi, lo, stored, w in (
                        (q_st, qa, psQT, "qT_t", "qa_r", "q_h", "q_l", st_q, 0),
                        (k_st, ka, psKT, "kT_t", "ka_r", "k_h", "k_l", st_k, 2)):
                    act.wait_ge(s[tt], g + 1)
                    at_least(act, s[lo], g)
                    pt = p_t[:, :].rearrange("p (c n) -> p c n", n=P)
                    m = P - NDCA if (w == 2 and j == TB - 1) else P
                    ins = act.activation(a[:, :, 0:m], pt[:, :, 0:m], ACT.Identity,
                                         scale=affine_s[:, w:w + 1], bias=affine_s[:, w + 1:w + 2])
                    if m < P:
                        ins = act.activation(a[:, :, m:P], pt[:, :, m:P], ACT.Identity,
                                             scale=affine_s[:, 4:5], bias=affine_s[:, 5:6])
                    ins.then_inc(s[dn], 1)
                    act.wait_ge(s[dn], g + 1)
                    if j % PAIR == 0:
                        at_least(act, stored[j // PAIR], 3 * 16 * b)
                    c = (j % PAIR) * P
                    act.activation(buf[:, j // PAIR, 0, :, c:c + P], a[:, :, :], ACT.Copy).then_inc(s[hi], 1)

            def steps(b, first, last):
                for j in range(TB):
                    if not (last and j >= TB - 2):
                        sqrt(*later(b, j, 2))
                    if not (last and j == TB - 1):
                        front(*later(b, j, 1))
                    if not (first and j < 2):
                        back(*earlier(b, j, 2))
                    mid(b, j)
            sqrt(0, 0)
            sqrt(0, 1)
            act.wait_ge(s["w_cent"], 1)
            act.activation(wq[:, 0], wq_raw[:, :, :], ACT.Copy, scale=WS).then_inc(s["w_hi"], 1)
            front(0, 0)
            act.wait_ge(s["aff_t"], 1)
            act.activation(affine_s[:, :], psKT[:, 0:6], ACT.Copy, scale=QS).then_inc(s["aff"], 1)
            for n, (src, dst) in enumerate(((wkv_raw, wkv), (wdca_raw, wdca))):
                for c in range(KC):
                    act.wait_ge(s["w_cent"], 2 + KC * n + c)
                    act.activation(src[:, c, :], src[:, c, :], ACT.Copy, scale=WS).then_inc(s["w_16"], 1)
                    act.wait_ge(s["w_16"], KC * n + c + 1)
                    act.activation(w_view(dst[:, 0, c, :], False), w_view(src[:, c, :], n == 0), ACT.Copy).then_inc(s["w_hi"], 1)
            steps(0, True, False)
            with act.Fori(1, B - 1) as b:
                steps(b, False, False)
            steps(B - 1, False, True)
            back(B - 1, TB - 2)
            back(B - 1, TB - 1)

        @block.vector
        def _(dve):
            sums = [0]

            def centre(views, done):
                first = sums[0]
                for i, v in enumerate(views):
                    dve.tensor_reduce(wsum[:, first + i, :], v, AX.X, ALU.add).then_inc(s["w_sum"], 1)
                sums[0] += len(views)
                dve.wait_ge(s["w_sum"], sums[0])
                for i, v in enumerate(views):
                    dve.scalar_tensor_tensor(v, wsum[:, first + i, :].unsqueeze(2).broadcast_to([P, H, HD]), -1.0 / HD, v,
                                             ALU.mult, ALU.add).then_inc(s[done], 1)

            def heads(v):
                return v.rearrange("p (h d) -> p h d", d=HD)

            def front_a(b, j):
                g = g_of(b, j)
                dve.wait_ge(x_ld[j % 2], 16 * (b * (TB // 2) + j // 2 + 1))
                dve.bn_stats(st[:, j % 2], x_in[:, j % 2]).then_inc(s["stats"], 1)
                dve.wait_ge(s["stats"], g + 1)
                dve.tensor_copy(st_seen[:, :], st[:, j % 2, 0:1])
                dve.bn_aggr(mv[:, j % 2], st[:, j % 2]).then_inc(s["aggr"], 1)
                dve.wait_ge(s["aggr"], g + 1)
                dve.tensor_scalar(ve[:, j % 2], mv[:, j % 2, 1:2], LN_EPS, None, ALU.add).then_inc(s["veps"], 1)

            def front_b(b, j):
                g = g_of(b, j)
                dve.wait_ge(s["sd_r"], g + 1)
                dve.reciprocal(rs[:, j % 2], sd[:, j % 2]).then_inc(s["rs_r"], 1)
                dve.wait_ge(s["rs_r"], g + 1)
                at_least(dve, s["xT_t"], g - 1)
                dve.tensor_scalar(xn[:, j % 2], x_in[:, j % 2], mv[:, j % 2, 0:1], rs[:, j % 2],
                                  ALU.subtract, ALU.mult).then_inc(s["xn_r"], 1)

            def front_c(b, j):
                g = g_of(b, j)
                dve.wait_ge(s["xT_h"], g + 1)
                dve.tensor_tensor(xT[:, j % 2, 1], psX[:, :].rearrange("p (k n) -> p k n", n=P), xT[:, j % 2, 0],
                                  ALU.subtract).then_inc(s["xT_l"], 1)
                dve.wait_ge(s["cT_h"], g + 1)
                pc = psC[:, 0:C].rearrange("p (k n) -> p k n", n=P)
                if j < TB - 1:
                    dve.tensor_tensor(cT[:, j % 2, 1], pc, cT[:, j % 2, 0], ALU.subtract).then_inc(s["cT_l"], 1)
                else:
                    m = P - NDCA
                    dve.wait_ge(s["masks"], 6)
                    dve.tensor_tensor(cTm[:, 1, :, 0:m], pc[:, :, 0:m], cTm[:, 0, :, 0:m], ALU.subtract)
                    dve.tensor_tensor(cTd[:, 1, :, m:P], pc[:, :, m:P], cTd[:, 0, :, m:P], ALU.subtract).then_inc(s["cT_l"], 1)

            def mid(b, j):
                g = g_of(b, j)
                dve.wait_ge(s["q_mm"], g + 1)
                at_least(dve, s["qn_r"], g - 1)
                dve.scalar_tensor_tensor(qf[:, j % 2], psQ[:, :], 1.0 / WS, bq[:, :], ALU.mult, ALU.add).then_inc(s["q_ev"], 1)
                var = 1 if j == TB - 1 else 0
                dve.wait_ge(s["k_mm"], g + 1)
                at_least(dve, s["kn_r"], g - 1)
                dve.scalar_tensor_tensor(heads(kf[:, j % 2]), heads(psK[:, :]), 1.0 / WS, k_cols(bkv[:, var, :]), ALU.mult, ALU.add).then_inc(s["k_ev"], 1)
                dve.wait_ge(s["v_mm"], g + 1)
                at_least(dve, s["v_l"], b * (TB + 1) + j - (1 if j else 2))
                dve.scalar_tensor_tensor(heads(vf[:, j % 2]), heads(psV[:, :]), 1.0 / WS, v_cols(bkv[:, var, :]), ALU.mult, ALU.add).then_inc(s["v_ev"], 1)
                if var:
                    dve.wait_ge(s["v_ev"], g + 1)
                    at_least(dve, s["v_l"], b * (TB + 1))
                    dve.tensor_scalar(vm[:, 0], vf[:, j % 2], m_main[:, :], None, ALU.mult).then_inc(s["vm_r"], 1)
                    dve.tensor_scalar(vm[:, 1], vf[:, j % 2], m_dca[:, :], None, ALU.mult).then_inc(s["vm_r"], 1)
                dve.wait_ge(s["sq_r"], g + 1)
                dve.tensor_reduce(hv[:, j % 2], sq[:, :, :].rearrange("p n (h d) -> p (n h) d", d=HD), AX.X, ALU.add).then_inc(s["hv_s"], 1)
                dve.wait_ge(s["hv_s"], g + 1)
                dve.tensor_scalar(hv[:, j % 2], hv[:, j % 2], 1.0 / HD, HEAD_EPS, ALU.mult, ALU.add).then_inc(s["hv_r"], 1)

            def mid_b(b, j):
                g = g_of(b, j)
                dve.wait_ge(s["hs_r"], g + 1)
                at_least(dve, s["kn_r"], g - 1)
                dve.reciprocal(hr[:, j % 2], hs_[:, j % 2]).then_inc(s["hr_r"], 1)

            def steps(b, first, last):
                for j in range(TB):
                    if not (last and j >= TB - 2):
                        front_a(*later(b, j, 2))
                    if not (last and j == TB - 1):
                        front_c(*later(b, j, 1))
                    if not (last and j >= TB - 2):
                        front_b(*later(b, j, 2))
                    mid(b, j)
                    mid_b(b, j)
            front_a(0, 0)
            front_a(0, 1)
            front_b(0, 0)
            front_b(0, 1)
            dve.wait_ge(s["wq_ld"], 16)
            for c in range(KD):
                dve.tensor_reduce(wsum[:, c, :], heads(wq_raw[:, c, :]), AX.X, ALU.add).then_inc(s["w_sum"], 1)
            sums[0] = KD
            dve.wait_ge(s["w_sum"], KD)
            for c in range(KD):
                ins = dve.scalar_tensor_tensor(heads(wq_raw[:, c, :]), wsum[:, c, :].unsqueeze(2).broadcast_to([P, H, HD]), -1.0 / HD,
                                               heads(wq_raw[:, c, :]), ALU.mult, ALU.add)
            ins.then_inc(s["w_cent"], 1)
            dve.wait_ge(s["w_hi"], 1)
            dve.scalar_tensor_tensor(wq[:, 1].rearrange("p k n -> p (k n)"), wq_raw[:, :, :].rearrange("p k n -> p (k n)"),
                                     WS, wq[:, 0].rearrange("p k n -> p (k n)"), ALU.mult, ALU.subtract).then_inc(s["wq_lo"], 1)
            dve.wait_ge(s["wkv_ld"], 32)
            centre([k_cols(wkv_raw[:, c, :]) for c in range(KC)], "w_cent")
            front_c(0, 0)
            dve.wait_ge(s["b_loaded"], 16 * 7)
            centre([heads(bq[:, :]), k_cols(bkv[:, 0, :]), k_cols(bkv[:, 1, :])], "b_cent")
            dve.wait_ge(s["wdca_ld"], 16)
            centre([heads(wdca_raw[:, c, 0:D]) for c in range(KC)], "w_cent")
            dve.wait_ge(s["masks"], 4)
            dve.tensor_copy(v_all[:, :, 3, HD:HD + 1], m_main[:, :].unsqueeze(1).broadcast_to([P, B * H, 1]))
            dve.tensor_copy(v_all[:, :, 4, HD:HD + 1], m_dca[:, :].unsqueeze(1).broadcast_to([P, B * H, 1]))
            dve.wait_ge(s["b_cent"], 3)
            steps(0, True, False)
            with dve.Fori(1, B - 1) as b:
                steps(b, False, False)
            steps(B - 1, False, True)

        @block.tensor
        def _(pe):
            pe.wait_ge(s["masks"], 1)

            def front(b, j):
                g = g_of(b, j)
                pe.wait_ge(s["xn_r"], g + 1)
                at_least(pe, s["xT_l"], g)
                for c in range(KD):
                    ins = pe.transpose(psX[:, c * P:(c + 1) * P], xn[:, j % 2, c * P:(c + 1) * P], ident[:, :])
                ins.then_inc(s["xT_t"], 1)
                pe.wait_ge(c_ld[j % 2], 16 * (b * (TB // 2) + j // 2 + 1))
                at_least(pe, s["cT_l"], g)
                for c in range(KC):
                    ins = pe.transpose(psC[:, c * P:(c + 1) * P], c_in[:, j % 2, c * P:(c + 1) * P], ident[:, :])
                ins.then_inc(s["cT_t"], 1)

            def product(dst, terms):
                for n, (a, w) in enumerate(terms):
                    ins = pe.matmul(dst, a, w, start=(n == 0), stop=(n == len(terms) - 1))
                return ins

            def passes(a, w, cols, chunks):
                return [(a[:, x, c, :], w[:, y, c, cols]) for c in range(chunks) for x, y in ((0, 0), (1, 0), (0, 1))]

            def mid(b, j):
                g = g_of(b, j)
                pe.wait_ge(s["xT_l"], g + 1)
                pe.wait_ge(s["wq_lo"], 1)
                at_least(pe, s["q_ev"], g)
                product(psQ[:, :], passes(xT[:, j % 2], wq, slice(0, D), KD)).then_inc(s["q_mm"], 1)
                pe.wait_ge(s["cT_l"], g + 1)
                pe.wait_ge(s["w_lo"], KC if j < TB - 1 else 2 * KC)
                for dst, ev, mm, cols in ((psK, "k_ev", "k_mm", slice(0, D)), (psV, "v_ev", "v_mm", slice(D, 2 * D))):
                    at_least(pe, s[ev], g)
                    if j < TB - 1:
                        terms = passes(cT[:, j % 2], wkv, cols, KC)
                    else:
                        terms = passes(cTm, wkv, cols, KC) + passes(cTd, wdca, cols, KC)
                    product(dst[:, :], terms).then_inc(s[mm], 1)

            def back(b, j):
                g = g_of(b, j)
                for src, dst, rdy, used, dn in ((qn, psQT, "qn_r", "qa_r", "qT_t"), (kn, psKT, "kn_r", "ka_r", "kT_t")):
                    pe.wait_ge(s[rdy], g + 1)
                    at_least(pe, s[used], g)
                    if isinstance(g, int) and g == 0:
                        pe.wait_ge(s["aff"], 1)
                    for c in range(CH):
                        ins = pe.transpose(dst[:, c * P:(c + 1) * P], src[:, c * P:(c + 1) * P], ident[:, :])
                    ins.then_inc(s[dn], 1)

            def steps(b, first, last):
                for j in range(TB):
                    nxt = (b, j + 1) if j < TB - 1 else (b + 1, 0)
                    if not (last and j == TB - 1):
                        front(*nxt)
                    mid(b, j)
                    if j:
                        back(b, j - 1)
                    elif not first:
                        back(b - 1, TB - 1)
            front(0, 0)
            pe.wait_ge(s["a_loaded"], 16 * 6)
            pe.transpose(psKT[:, 0:6], affine[:, :], ident[0:6, 0:6]).then_inc(s["aff_t"], 1)
            steps(0, True, False)
            with pe.Fori(1, B - 1) as b:
                steps(b, False, False)
            steps(B - 1, False, True)
            back(B - 1, TB - 1)


E_EARLY = 2
SCALE = float(HD) ** -0.5


def attend(nc, t, sem, g_):
    ident, v_all, o_all = g_["ident"], g_["v_all"], g_["o_all"]
    q_dram, k_dram = g_["q_dram"], g_["k_dram"]
    N = B * H
    G = 4
    SLOTS = G
    PEEL = 2
    K3 = 3 * HD
    KR = K3 + 2
    sb = Map(nc, SBUF_LO + E_EARLY * g_["PER_E"], g_["O_AT"])
    raw = sb("a_raw", [P, 2, D], F32)
    q_stk = sb("q_stk", [P, SLOTS, S], F16)
    k_stk = sb("k_stk", [P, SLOTS, S], F16)
    nm = sb("nm", [P, 2, TB, 2], F32)
    pf = sb("pf", [P, TB, S], F32)
    ph = sb("ph", [P, 2, TB, S], F16)
    pl = sb("pl", [P, 2, TB, S], F16)
    oe = sb("oe", [P, 2, TB, 2, VW], F32)
    on = sb("on", [P, 2, TB, 2, HD], F32)
    orc = sb("orc", [P, 2, TB, 2, 1], F32)
    om = sb("om", [P, 2, TB, 2, HD], F32)
    HI_ACT, HI_DVE = (0, 2, 3), (1,)
    LO_DVE, LO_POOL = (0, 1), (2, 3)

    def wait_hi(eng, w, k):
        for name, mine in (("h_act", HI_ACT), ("h_dve", HI_DVE)):
            if k in mine:
                eng.wait_ge(s[name], len(mine) * w + mine.index(k) + 1)

    names = """wo_ld wo_hi wo_16 wo_lo sel max m_mm mrow s_mm t_mm exp o_mm o_ev h_act h_dve l_dve l_pool num rec mul out"""
    s = {n: sem("a_" + n) for n in names.split()}
    raw_ld = sem("a_raw_loaded")
    wo = g_["wo"]
    wo_raw = sb("wo_raw", [P, KD, D], F32)
    loaded = [sem(f"a_stack_loaded{n}") for n in range(SLOTS)]

    with ExitStack() as ps:
        psS = ps.enter_context(nc.psum_tensor("a_psS", [P, 2, 512], F32))
        psT = ps.enter_context(nc.psum_tensor("a_psT", [P, 2, 512], F32))
        psO = ps.enter_context(nc.psum_tensor("a_psO", [P, 2, 512], F32))
        psM = ps.enter_context(nc.psum_tensor("a_psM", [P, 512], F32))
        block = ps.enter_context(nc.Block())

        def live(u, lag, end=N):
            return not isinstance(u, int) or lag <= u < end + lag

        def run(eng, step, tail, between=None):
            for u in range(PEEL * G):
                step(u, u % G)
            at = PEEL
            if between:
                for m in range(NM):
                    for k in range(E_EARLY):
                        with eng.Fori(at, at + 2) as g:
                            for j in range(G):
                                step(g * G + j, j)
                                between(m, k, g - at, j)
                        at += 2
            with eng.Fori(at, N // G) as g:
                for j in range(G):
                    step(g * G + j, j)
            for j in range(tail):
                step(N + j, j % G)

        def half_of(m, k, half):
            return half + 2 * (E_EARLY * m + k)

        @block.sync
        def _(sp):
            def step(u, j):
                if isinstance(u, int) and u == PEEL * G - 1:
                    for q in g_["qk_stored"][0] + g_["qk_stored"][1]:
                        sp.wait_ge(q, 3 * 16 * NT // PAIR // 2)
                if isinstance(u, int) and u == 2:
                    sp.dma_start(wo_raw[:, :, :], t["L0_xattn_Wo"].rearrange("(k p) n -> p k n", p=P)).then_inc(s["wo_ld"], 16)
                if live(u, 0):
                    at_least(sp, s["t_mm"], TB * (u - 3))
                    for stk, dr in ((q_stk, q_dram), (k_stk, k_dram)):
                        sp.dma_start(stk[0:K3, j, :], dr[:, ds(u * HD, HD), :]).then_inc(loaded[j], 16)

            def between(m, k, half, j):
                if j == 0:
                    sp.wait_ge(g_["split_done"], half_of(m, k, half) + 1)
                    g_["load_half"](sp, raw[:, :, :], raw_ld, k, half, m)
            run(sp, step, 0, between)

        @block.gpsimd
        def _(pool):
            pool.memset(k_stk[K3:KR, :, :], QS).then_inc(s["sel"], 1)
            pool.wait_ge(s["sel"], 1)
            pool.memset(g_["ws_tile"][:, :], WS).then_inc(g_["split_done"], 1)
            pool.wait_ge(g_["split_done"], 1)
            sel = k_stk[K3:KR, :, :]
            pool.affine_select(out=sel, in_=sel, compare_op=ALU.is_ge, fill=0.0, base=NMAIN - 1,
                               pattern=[[0, SLOTS], [-1, S]], channel_multiplier=1000).then_inc(s["sel"], 1)
            pool.wait_ge(s["sel"], 2)
            pool.affine_select(out=sel, in_=sel, compare_op=ALU.is_ge, fill=0.0, base=1000 - NMAIN,
                               pattern=[[0, SLOTS], [1, S]], channel_multiplier=-1000).then_inc(s["sel"], 1)

            def step(u, j):
                if isinstance(u, int) and u == 4:
                    pool.wait_ge(s["wo_16"], 1)
                    pool.tensor_tensor(wo[:, 1].rearrange("p k n -> p (k n)"), wo_raw[:, :, :].rearrange("p k n -> p (k n)"),
                                       wo[:, 0].rearrange("p k n -> p (k n)"), ALU.subtract).then_inc(s["wo_lo"], 1)
                if live(u, 2):
                    w = u - 2
                    sl = j % 2
                    for k in LO_POOL:
                        wait_hi(pool, w, k)
                        pool.tensor_tensor(pl[:, sl, k], pf[:, k], ph[:, sl, k], ALU.subtract).then_inc(s["l_pool"], 1)
                if live(u, 4):
                    w = u - 4
                    sl = j % 2
                    pool.wait_ge(s["rec"], w + 1)
                    pool.tensor_tensor(om[:, sl].rearrange("p q s d -> p (q s) d"), on[:, sl].rearrange("p q s d -> p (q s) d"),
                                       orc[:, sl].rearrange("p q s o -> p (q s) o").broadcast_to([P, TB * 2, HD]), ALU.mult).then_inc(s["mul"], 1)
                    pool.wait_ge(s["mul"], w + 1)
                    pool.tensor_tensor(o_all[:, :, ds(w, 1), :].rearrange("p q o d -> p (q o) d"), om[:, sl, :, 0, :], om[:, sl, :, 1, :], ALU.add).then_inc(s["out"], 1)

            def between(m, k, half, j):
                if j < 3:
                    n = half_of(m, k, half)
                    g_["split_half"](pool, raw[:, :, :], raw_ld, n + 1, k, half, m, n, j)
            run(pool, step, 4, between)

        @block.scalar
        def _(act):
            def exps(w, k):
                act.wait_ge(s["t_mm"], TB * w + k + 1)
                for name, mine in (("l_dve", LO_DVE), ("l_pool", LO_POOL)):
                    if k in mine:
                        at_least(act, s[name], len(mine) * (w - 1) + mine.index(k) + 1)
                act.activation(pf[:, k], psT[:, k % 2], ACT.Exp, scale=SCALE / (QS * QS)).then_inc(s["exp"], 1)

            def hi(w, sl, k):
                act.wait_ge(s["exp"], TB * w + k + 1)
                at_least(act, s["o_mm"], 2 * (w - 1))
                act.activation(ph[:, sl, k], pf[:, k], ACT.Copy).then_inc(s["h_act"], 1)

            def evac(w, sl, p):
                act.wait_ge(s["o_mm"], 2 * w + p + 1)
                if p == 0:
                    at_least(act, s["rec"], w - 1)
                act.activation(oe[:, sl, 2 * p:2 * p + 2].rearrange("p q s v -> p (q s v)"), psO[:, p, 0:4 * VW], ACT.Copy).then_inc(s["o_ev"], 1)

            def step(u, j):
                if isinstance(u, int) and u == 2:
                    act.wait_ge(s["wo_ld"], 16)
                    act.activation(wo[:, 0], wo_raw[:, :, :], ACT.Copy, scale=WS).then_inc(s["wo_hi"], 1)
                    act.wait_ge(s["wo_hi"], 1)
                    act.activation(wo_raw[:, :, :], wo_raw[:, :, :], ACT.Copy, scale=WS).then_inc(s["wo_16"], 1)
                if live(u, 2):
                    exps(u - 2, 0)
                if live(u, 4):
                    evac(u - 4, j % 2, 0)
                if live(u, 2):
                    exps(u - 2, 1)
                if live(u, 4):
                    evac(u - 4, j % 2, 1)
                if live(u, 2):
                    hi(u - 2, j % 2, 0)
                    exps(u - 2, 2)
                if live(u, 1):
                    w = u - 1
                    act.wait_ge(s["m_mm"], w + 1)
                    act.activation(q_stk[K3:KR, (j - 1) % SLOTS, :], psM[0:2, :], ACT.Copy, scale=1.0 / QS).then_inc(s["mrow"], 1)
                if live(u, 2):
                    hi(u - 2, j % 2, 2)
                    exps(u - 2, 3)
                if live(u, 2):
                    hi(u - 2, j % 2, 3)
            run(act, step, 5)

        @block.vector
        def _(dve):
            def maxima(u, j, p):
                sl = j % 2
                dve.wait_ge(s["s_mm"], 2 * u + p + 1)
                at_least(dve, s["m_mm"], u - 1)
                dve.tensor_reduce(nm[:, sl, 2 * p:2 * p + 2, 0:1].rearrange("p q o -> p (q o)"), psS[:, :, 0:NMAIN], AX.X, ALU.max, negate=True)
                dve.tensor_reduce(nm[:, sl, 2 * p:2 * p + 2, 1:2].rearrange("p q o -> p (q o)"), psS[:, :, NMAIN:S], AX.X, ALU.max, negate=True).then_inc(s["max"], 1)

            def hi(w, sl, k):
                dve.wait_ge(s["exp"], TB * w + k + 1)
                at_least(dve, s["o_mm"], 2 * (w - 1))
                dve.tensor_copy(ph[:, sl, k], pf[:, k]).then_inc(s["h_dve"], 1)

            def lo(w, sl, k):
                wait_hi(dve, w, k)
                dve.tensor_tensor(pl[:, sl, k], pf[:, k], ph[:, sl, k], ALU.subtract).then_inc(s["l_dve"], 1)

            def norm(w, sl):
                dve.wait_ge(s["o_ev"], 2 * w + 2)
                at_least(dve, s["mul"], w - 1)
                e = oe[:, sl].rearrange("p q s v -> p (q s) v")
                dve.tensor_tensor(on[:, sl].rearrange("p q s d -> p (q s) d"), e[:, :, 0:HD], e[:, :, HD + 1:], ALU.add)
                dve.reciprocal(orc[:, sl].rearrange("p q s o -> p (q s) o"), e[:, :, HD:HD + 1]).then_inc(s["rec"], 1)

            def step(u, j):
                if live(u, 0):
                    maxima(u, j, 0)
                if live(u, 4):
                    norm(u - 4, j % 2)
                if live(u, 2):
                    w, sl = u - 2, j % 2
                    lo(w, sl, 0)
                    hi(w, sl, 1)
                if live(u, 0):
                    maxima(u, j, 1)
                if live(u, 2):
                    lo(w, sl, 1)
            run(dve, step, 5)

        @block.tensor
        def _(pe):
            def scores(u, j, q):
                if q == 0:
                    pe.wait_ge(loaded[j], (u - j) * (2 * 16 // G) + 2 * 16)
                if q % 2 == 0:
                    at_least(pe, s["max"], 2 * u + q // 2)
                ins = pe.matmul(psS[:, q % 2], q_stk[0:K3, j, q * P:(q + 1) * P], k_stk[0:K3, j, :], start=True, stop=True)
                if q % 2:
                    ins.then_inc(s["s_mm"], 1)

            def max_rows(w, sl):
                pe.wait_ge(s["max"], 2 * w + 2)
                at_least(pe, s["mrow"], w)
                for q in range(TB):
                    ins = pe.transpose(psM[0:2, q * P:(q + 1) * P], nm[:, sl, q, :], ident[:, :])
                ins.then_inc(s["m_mm"], 1)

            def scores_t(w, j, k):
                if k == 0:
                    pe.wait_ge(s["mrow"], w + 1)
                    if isinstance(w, int) and w == 0:
                        pe.wait_ge(s["sel"], 3)
                at_least(pe, s["exp"], TB * w + k - 1)
                pe.matmul(psT[:, k % 2], k_stk[0:KR, j, k * P:(k + 1) * P], q_stk[0:KR, j, :], start=True, stop=True).then_inc(s["t_mm"], 1)

            def values(w, sl, q):
                if q == 0:
                    pe.wait_ge(s["h_act"], len(HI_ACT) * (w + 1))
                    pe.wait_ge(s["h_dve"], len(HI_DVE) * (w + 1))
                    pe.wait_ge(s["l_dve"], 2 * w + 2)
                    pe.wait_ge(s["l_pool"], 2 * w + 2)
                if q % 2 == 0:
                    at_least(pe, s["o_ev"], 2 * (w - 1) + q // 2 + 1)
                at = (q % 2) * 2 * VW
                c = slice(q * P, (q + 1) * P)
                for seg, keys in ((1, [TB - 1]), (0, range(TB))):
                    keys = list(keys)
                    dst = psO[:, q // 2, at + seg * VW:at + (seg + 1) * VW]
                    for k in keys:
                        v = v_all[:, ds(w, 1), k + seg, :].rearrange("p o v -> p (o v)")
                        pe.matmul(dst, ph[:, sl, k, c], v, start=(k == keys[0]), stop=False)
                        ins = pe.matmul(dst[:, 0:HD + 1], pl[:, sl, k, c], v[:, 0:HD + 1], start=False, stop=(k == keys[-1]))
                if q % 2:
                    ins.then_inc(s["o_mm"], 1)

            def step(u, j):
                if live(u, 2):
                    scores_t(u - 2, (j - 2) % SLOTS, 0)
                if live(u, 0):
                    scores(u, j, 0)
                    scores(u, j, 1)
                if live(u, 2):
                    scores_t(u - 2, (j - 2) % SLOTS, 1)
                if live(u, 1):
                    max_rows(u - 1, (j - 1) % 2)
                if live(u, 2):
                    scores_t(u - 2, (j - 2) % SLOTS, 2)
                if live(u, 0):
                    scores(u, j, 2)
                    scores(u, j, 3)
                if live(u, 2):
                    scores_t(u - 2, (j - 2) % SLOTS, 3)
                if live(u, 3):
                    for q in range(TB):
                        values(u - 3, (j - 3) % 2, q)
            run(pe, step, 3)


def output(nc, t, sem, g_):
    ident, o_all, wo = g_["ident"], g_["o_all"], g_["wo"]
    low = Map(nc, SBUF_LO + E_EARLY * g_["PER_E"], g_["O_AT"])
    xn2 = g_["xn2"] = low("xn2", [P, NT, D], F32)
    logits = g_["logits"] = low("logits", [P, NT, E + 1], F32)
    sb = Map(nc, g_["V_AT"], g_["WO_AT"])
    wr = sb("wr", [P, KD, E], F32)
    bo = sb("bo", [P, D], F32)
    x_in = sb("o_x", [P, 2, D], F32)
    xb = sb("o_xb", [P, 2, D], F32)
    x1 = sb("o_x1", [P, 2, D], F32)
    o_in = sb("o_in", [P, 2, D], F32)
    xn = sb("o_xn", [P, 2, D], F32)
    oT = low("oT", [P, 2, 2, KD, P], F16)
    nT = low("nT", [P, KD, P], F32)
    st = sb("o_st", [P, 2, 6], F32)
    st_seen = sb("o_st_seen", [P, 1], F32)
    mv = sb("o_mv", [P, 2, 2], F32)
    ve = sb("o_ve", [P, 2, 1], F32)
    sd = sb("o_sd", [P, 2, 1], F32)
    rs = sb("o_rs", [P, 2, 1], F32)
    names = """r_loaded b_loaded xb_r oT_t oT_h oT_l y_mm x1_r stats aggr veps sd_r rs_r xn_r xn2_r nT_t nT_c r_mm logit"""
    s = {n: sem("o_" + n) for n in names.split()}
    x_ld = [sem("o_x_loaded0"), sem("o_x_loaded1")]
    o_ld = [sem("o_o_copied0"), sem("o_o_copied1")]
    x1_st = [sem("o_x1_stored0"), sem("o_x1_stored1")]
    xn_st = [sem("o_xn_stored0"), sem("o_xn_stored1")]

    with ExitStack() as ps:
        def bank(name):
            return ps.enter_context(nc.psum_tensor(name, [P, 512], F32))
        psX, psY, psN, psR = (bank("o_" + n) for n in ("psX", "psY", "psN", "psR"))
        block = ps.enter_context(nc.Block())

        def shift(b, j, n):
            j += n
            if j < 0:
                return b - 1, j + TB
            return (b, j) if j < TB else (b + 1, j - TB)

        def g_of(b, j):
            return b * TB + j

        def nth(b, j):
            return b * (TB // 2) + j // 2

        def there(b, j):
            return not isinstance(b, int) or 0 <= g_of(b, j) < NT

        def loop(eng, step, tail):
            for j in range(TB):
                step(0, j)
            with eng.Fori(1, B - 1) as b:
                for j in range(TB):
                    step(b, j)
            for j in range(TB):
                step(B - 1, j)
            for j in range(tail):
                step(B, j)

        @block.sync
        def _(sp):
            x_rows = t["x"].rearrange("b s d -> (b s) d")

            def load(b, j):
                g = g_of(b, j)
                at_least(sp, s["oT_t"], g - 1)
                sp.dma_start(o_in[:, j % 2], o_all[:, j, ds(b * H, H), :].rearrange("p h d -> p (h d)")).then_inc(o_ld[j % 2], 16)
                at_least(sp, s["xb_r"], g - 1)
                sp.dma_start(x_in[:, j % 2], x_rows[ds(g * P, P), :]).then_inc(x_ld[j % 2], 16)
            load(0, 0)
            sp.dma_start(bo[:, :], t["L0_xattn_bo"].partition_broadcast(P)).then_inc(s["b_loaded"], 16)
            load(0, 1)
            sp.dma_start(wr[:, :, :], t["L0_ffn_Wr"].rearrange("(k p) n -> p k n", p=P)).then_inc(s["r_loaded"], 16)

            def step(b, j):
                if there(*shift(b, j, 2)) and there(b, j):
                    load(*shift(b, j, 2))
                c, k = shift(b, j, -1)
                if there(c, k):
                    sp.wait_ge(s["x1_r"], g_of(c, k) + 1)
                    sp.dma_start(g_["x1_dram"][ds(g_of(c, k) * P, P), :], x1[:, k % 2]).then_inc(x1_st[k % 2], 16)
                c, k = shift(b, j, -2)
                if there(c, k):
                    sp.wait_ge(s["xn_r"], g_of(c, k) + 1)
                    sp.dma_start(g_["xn_dram"][ds(g_of(c, k) * P, P), :], xn[:, k % 2]).then_inc(xn_st[k % 2], 16)
            loop(sp, step, 2)
            for q in x1_st + xn_st:
                sp.wait_ge(q, 8 * NT)

        @block.gpsimd
        def _(pool):
            def residual(b, j):
                g = g_of(b, j)
                pool.wait_ge(x_ld[j % 2], 16 * nth(b, j) + 16)
                at_least(pool, s["x1_r"], g - 1)
                pool.tensor_tensor(xb[:, j % 2], x_in[:, j % 2], bo[:, :], ALU.add).then_inc(s["xb_r"], 1)

            def step(b, j):
                if there(*shift(b, j, 1)):
                    residual(*shift(b, j, 1))
            pool.wait_ge(s["b_loaded"], 16)
            residual(0, 0)
            loop(pool, step, 0)

        @block.scalar
        def _(act):
            def front(b, j):
                g = g_of(b, j)
                act.wait_ge(s["oT_t"], g + 1)
                at_least(act, s["y_mm"], g - 1)
                act.activation(oT[:, j % 2, 0], psX[:, :].rearrange("p (k n) -> p k n", n=P), ACT.Copy).then_inc(s["oT_h"], 1)

            def step(b, j):
                if there(*shift(b, j, 1)):
                    front(*shift(b, j, 1))
                c, k = shift(b, j, -1)
                if there(c, k):
                    act.wait_ge(s["xn_r"], g_of(c, k) + 1)
                    act.activation(xn2[:, ds(g_of(c, k), 1), :].rearrange("p o d -> p (o d)"), xn[:, k % 2], ACT.Copy).then_inc(s["xn2_r"], 1)
                c, k = shift(b, j, -2)
                if there(c, k):
                    act.wait_ge(s["nT_t"], g_of(c, k) + 1)
                    at_least(act, s["r_mm"], g_of(c, k))
                    act.activation(nT[:, :, :], psN[:, :].rearrange("p (k n) -> p k n", n=P), ACT.Copy).then_inc(s["nT_c"], 1)
                if there(b, j):
                    act.wait_ge(s["veps"], g_of(b, j) + 1)
                    act.activation(sd[:, j % 2], ve[:, j % 2], ACT.Sqrt).then_inc(s["sd_r"], 1)
            front(0, 0)
            loop(act, step, 2)

        @block.vector
        def _(dve):
            def front(b, j):
                g = g_of(b, j)
                dve.wait_ge(s["oT_h"], g + 1)
                dve.tensor_tensor(oT[:, j % 2, 1], psX[:, :].rearrange("p (k n) -> p k n", n=P), oT[:, j % 2, 0],
                                  ALU.subtract).then_inc(s["oT_l"], 1)

            def norm(b, j):
                g = g_of(b, j)
                dve.wait_ge(s["sd_r"], g + 1)
                dve.reciprocal(rs[:, j % 2], sd[:, j % 2]).then_inc(s["rs_r"], 1)
                dve.wait_ge(s["rs_r"], g + 1)
                at_least(dve, xn_st[j % 2], 16 * nth(b, j))
                at_least(dve, s["nT_t"], g - 1)
                at_least(dve, s["xn2_r"], g - 1)
                dve.tensor_scalar(xn[:, j % 2], x1[:, j % 2], mv[:, j % 2, 0:1], rs[:, j % 2],
                                  ALU.subtract, ALU.mult).then_inc(s["xn_r"], 1)

            def step(b, j):
                if there(*shift(b, j, -1)):
                    norm(*shift(b, j, -1))
                if there(*shift(b, j, 1)):
                    front(*shift(b, j, 1))
                if not there(b, j):
                    return
                g = g_of(b, j)
                dve.wait_ge(s["y_mm"], g + 1)
                dve.wait_ge(s["xb_r"], g + 1)
                at_least(dve, x1_st[j % 2], 16 * nth(b, j))
                dve.scalar_tensor_tensor(x1[:, j % 2], psY[:, :], 1.0 / WS, xb[:, j % 2], ALU.mult, ALU.add).then_inc(s["x1_r"], 1)
                dve.wait_ge(s["x1_r"], g + 1)
                dve.bn_stats(st[:, j % 2], x1[:, j % 2]).then_inc(s["stats"], 1)
                dve.wait_ge(s["stats"], g + 1)
                dve.tensor_copy(st_seen[:, :], st[:, j % 2, 0:1])
                dve.bn_aggr(mv[:, j % 2], st[:, j % 2]).then_inc(s["aggr"], 1)
                dve.wait_ge(s["aggr"], g + 1)
                dve.tensor_scalar(ve[:, j % 2], mv[:, j % 2, 1:2], LN_EPS, None, ALU.add).then_inc(s["veps"], 1)
            front(0, 0)
            loop(dve, step, 1)
            dve.wait_ge(s["r_mm"], NT)
            dve.tensor_copy(logits[:, :, 0:E], psR[:, 0:NT * (E + 1)].rearrange("p (n e) -> p n e", e=E + 1)[:, :, 0:E]).then_inc(s["logit"], 1)

        @block.tensor
        def _(pe):
            def transposes(dst, src, done):
                for c in range(KD):
                    ins = pe.transpose(dst[:, c * P:(c + 1) * P], src[:, c * P:(c + 1) * P], ident[:, :])
                ins.then_inc(done, 1)

            def front(b, j):
                pe.wait_ge(o_ld[j % 2], 16 * nth(b, j) + 16)
                at_least(pe, s["oT_l"], g_of(b, j))
                transposes(psX, o_in[:, j % 2], s["oT_t"])

            def step(b, j):
                if there(*shift(b, j, 1)):
                    front(*shift(b, j, 1))
                c, k = shift(b, j, -2)
                if there(c, k):
                    pe.wait_ge(s["xn_r"], g_of(c, k) + 1)
                    at_least(pe, s["nT_c"], g_of(c, k))
                    transposes(psN, xn[:, k % 2], s["nT_t"])
                if there(b, j):
                    g = g_of(b, j)
                    pe.wait_ge(s["oT_l"], g + 1)
                    at_least(pe, s["x1_r"], g)
                    n = 0
                    for q in range(KD):
                        for x, y in ((0, 0), (1, 0), (0, 1)):
                            ins = pe.matmul(psY[:, :], oT[:, j % 2, x, q, :], wo[:, y, q, :], start=(n == 0), stop=(n == 3 * KD - 1))
                            n += 1
                    ins.then_inc(s["y_mm"], 1)
                if there(c, k):
                    g = g_of(c, k)
                    pe.wait_ge(s["nT_c"], g + 1)
                    for q in range(KD):
                        ins = pe.matmul(psR[:, ds(g * (E + 1), E)], nT[:, q, :], wr[:, q, :], start=(q == 0), stop=(q == KD - 1))
                    ins.then_inc(s["r_mm"], 1)

            pe.wait_ge(s["r_loaded"], 16)
            front(0, 0)
            loop(pe, step, 2)


def route(nc, t, sem, g_):
    logits, slot, prob, pmat, blk_k, blk_w, bias, pick = (g_[k] for k in "logits slot prob pmat blk_k blk_w bias pick".split())
    KB = g_["KB"]
    sb = Map(nc, SBUF_LO + E_EARLY * g_["PER_E"] + (NT * D + NT * (E + 1)) * 4, g_["V_AT"])
    R = [P, NT, E]
    br = sb("br", [P, E], F32)
    gb = sb("gb", [P, E], F32)
    tri = sb("tri", [P, P], F32)
    ones = sb("ones", [P, P], F32)
    ramp_i = sb("ramp_i", [P, E], I32)
    ramp = sb("ramp", [P, E], F32)
    bidx_i = sb("bidx_i", [P, NBLK], I32)
    bidx = sb("bidx", [P, NBLK], F32)
    lg, bg, eq, cand, prod, member, within, tile_n, scan_a, scan_b, place = (
        sb("r_" + n, R, F32) for n in "lg bg eq cand prod member within tile_n scan_a scan_b place".split())
    oh = [sb(f"oh{k}", R, F32) for k in range(TOP)]
    top = sb("top", [P, NT], F32)
    sel = sb("sel_l", [P, TOP, NT], F32)
    mx = sb("r_mx", [P, NT], F32)
    ex = sb("r_ex", [P, TOP, NT], F32)
    den = sb("r_den", [P, NT], F32)
    ph16 = sb("ph16", [P, NT, E + 1], F16)
    cnt_i = sb("cnt_i", [P, E], I32)
    nblk = sb("nblk", [P, E], F32)
    cum_a = sb("cum_a", [P, E], F32)
    cum_b = sb("cum_b", [P, E], F32)
    base = sb("base", [P, E], F32)
    cum2_a = sb("cum2_a", [P, E], F32)
    cum2_b = sb("cum2_b", [P, E], F32)
    slot_f = sb("slot_f", [P, TOP, NT], F32)
    cmpb = sb("cmpb", [P, NBLK, E - 1], F32)
    blk_f = sb("blk_f", [P, NBLK], F32)
    wrap = sb("wrap", [P, NBLK], F32)
    zero = g_["zero"] = sb("zero", [P, D], F32)
    pad_i = sb("pad_i", [P, NPAD], I32)
    pad_n = sb("pad_n", [P, NPAD], F32)
    pad_c = sb("pad_c", [P, E], F32)
    pad_w = sb("pad_w", [P, NPAD, E], F32)
    pad_f = sb("pad_f", [P, NPAD], F32)
    pad = g_["pad"] = sb("pad", [P, NPAD], I32)
    bias_raw = sb("bias_raw", [KB, 2, D], F32)
    bias_16 = sb("bias_16", [KB, 2, D], F32)
    bias_hi = sb("bias_hi", [KB, 2, D], F16)
    bias_m = sb("bias_m", [KB, 2, D], F32)
    low = sb("low", [KB, 1], F32)
    names = "loaded const0 const1 iota member prefix exp_in exp probs b_loaded b_16 b_m low pick"
    s = {n: sem("r_" + n) for n in names.split()}
    dve_step = sem("r_dve_step")

    def over_tiles(x):
        return x.unsqueeze(1).broadcast_to(R)

    def over_experts(x):
        return x.unsqueeze(2).broadcast_to(R)

    with ExitStack() as ps:
        psW = ps.enter_context(nc.psum_tensor("r_psW", [P, 512], F32))
        psN = ps.enter_context(nc.psum_tensor("r_psN", [P, 512], F32))
        block = ps.enter_context(nc.Block())

        @block.sync
        def _(sp):
            sp.dma_start(br[:, :], t["L0_ffn_br"].partition_broadcast(P)).then_inc(s["loaded"], 16)
            sp.dma_start(gb[:, :], t["L0_ffn_gate_bias"].partition_broadcast(P)).then_inc(s["loaded"], 16)
            for m, (one, many) in enumerate((("L0_ffn_bsu", "L0_ffn_bup"), ("L0_ffn_bsg", "L0_ffn_bgate"))):
                for at in (0, E + 1):
                    sp.dma_start(bias_raw[at:at + 1, m, :], t[one].rearrange("(o n) -> o n", o=1)).then_inc(s["b_loaded"], 16)
                    sp.dma_start(bias_raw[at + 1:at + E + 1, m, :], t[many]).then_inc(s["b_loaded"], 16)

        @block.gpsimd
        def _(pool):
            pool.memset(tri[:, :], 1.0).then_inc(s["const0"], 1)
            pool.memset(ones[:, :], 1.0).then_inc(s["const1"], 1)
            pool.iota(ramp_i[:, :], pattern=[[-1, E]], base=E, channel_multiplier=0).then_inc(s["iota"], 1)
            pool.iota(bidx_i[:, :], pattern=[[1, NBLK]], base=0, channel_multiplier=0).then_inc(s["iota"], 1)
            pool.iota(pad_i[:, :], pattern=[[P, NPAD]], base=0, channel_multiplier=1).then_inc(s["iota"], 1)
            pool.wait_ge(s["const0"], 1)
            pool.affine_select(out=tri[:, :], in_=tri[:, :], compare_op=ALU.is_ge, fill=0.0, base=-1,
                               pattern=[[1, P]], channel_multiplier=-1).then_inc(s["const1"], 1)
            pool.wait_ge(s["const1"], 2)
            pool.memset(zero[:, :], 0.0).then_inc(s["const0"], 1)
            pool.wait_ge(s["const0"], 2)
            pool.memset(pick[:, :, :], 0.0).then_inc(s["pick"], 1)
            for part in range(2):
                pool.wait_ge(s["pick"], part + 1)
                pool.affine_select(out=pick[:, :, :], in_=pick[:, :, :], compare_op=ALU.not_equal, fill=1.0, base=-part * (E + 1),
                                   pattern=[[-1, E + 1], [0, P]], channel_multiplier=1).then_inc(s["pick"], 1)
            pool.wait_ge(s["pick"], 3)
            pool.memset(low[:, :], -1.0).then_inc(s["low"], 1)
            pool.wait_ge(s["low"], 1)
            pool.affine_select(out=low[:, :], in_=low[:, :], compare_op=ALU.is_ge, fill=0.0, base=-(E + 1),
                               pattern=[[0, 1]], channel_multiplier=1).then_inc(s["low"], 1)
            pool.wait_ge(s["low"], 2)
            pool.wait_ge(s["b_16"], 2)
            flat = [v[:, :, :].rearrange("p m n -> p (m n)") for v in (bias_m, bias_hi, bias, bias_16)]
            pool.tensor_tensor(flat[0], flat[1], low[:, :].broadcast_to([KB, 2 * D]), ALU.mult).then_inc(s["b_m"], 1)
            pool.wait_ge(s["b_m"], 1)
            pool.tensor_tensor(flat[2], flat[0], flat[3], ALU.add).then_inc(s["b_m"], 1)
            pool.wait_ge(s["b_m"], 2)

        @block.tensor
        def _(pe):
            pe.wait_ge(s["const1"], 2)
            pe.wait_ge(s["member"], 1)
            m = member[:, :, :].rearrange("p n e -> p (n e)")
            pe.matmul(psW[:, 0:NT * E], tri[:, :], m, start=True, stop=True)
            pe.matmul(psN[:, 0:NT * E], ones[:, :], m, start=True, stop=True).then_inc(s["prefix"], 1)

        @block.scalar
        def _(act):
            act.wait_ge(s["b_loaded"], 16 * 8)
            act.activation(bias_hi[:, :, :], bias_raw[:, :, :], ACT.Copy, scale=WS).then_inc(s["b_16"], 1)
            act.activation(bias_16[:, :, :], bias_raw[:, :, :], ACT.Copy, scale=WS).then_inc(s["b_16"], 1)
            act.wait_ge(s["exp_in"], 1)
            act.activation(ex[:, :, :], sel[:, :, :], ACT.Exp).then_inc(s["exp"], 1)

        @block.vector
        def _(dve):
            n = [0]

            def link(ins):
                n[0] += 1
                ins.then_inc(dve_step, 1)
                dve.wait_ge(dve_step, n[0])

            dve.wait_ge(s["iota"], 3)
            link(dve.tensor_copy(ramp[:, :], ramp_i[:, :]))
            link(dve.tensor_copy(bidx[:, :], bidx_i[:, :]))
            dve.wait_ge(s["loaded"], 32)
            link(dve.tensor_tensor(lg[:, :, :], logits[:, :, 0:E], over_tiles(br[:, :]), ALU.add))
            link(dve.tensor_tensor(bg[:, :, :], lg[:, :, :], over_tiles(gb[:, :]), ALU.add))
            for k in range(TOP):
                link(dve.tensor_reduce(top[:, :], bg[:, :, :], AX.X, ALU.max))
                link(dve.tensor_tensor(eq[:, :, :], bg[:, :, :], over_experts(top[:, :]), ALU.is_equal))
                link(dve.tensor_tensor(cand[:, :, :], eq[:, :, :], over_tiles(ramp[:, :]), ALU.mult))
                link(dve.tensor_reduce(top[:, :], cand[:, :, :], AX.X, ALU.max))
                link(dve.tensor_tensor(oh[k][:, :, :], cand[:, :, :], over_experts(top[:, :]), ALU.is_equal))
                link(dve.tensor_tensor(prod[:, :, :], lg[:, :, :], oh[k][:, :, :], ALU.mult))
                link(dve.tensor_reduce(sel[:, k, :], prod[:, :, :], AX.X, ALU.add))
                if k == 0:
                    link(dve.scalar_tensor_tensor(bg[:, :, :], oh[0][:, :, :], -3.0e38, bg[:, :, :], ALU.mult, ALU.add))
            dve.tensor_tensor(member[:, :, :], oh[0][:, :, :], oh[1][:, :, :], ALU.add).then_inc(s["member"], 1)
            link(dve.tensor_tensor(mx[:, :], sel[:, 0, :], sel[:, 1, :], ALU.max))
            for k in range(TOP):
                ins = dve.tensor_tensor(sel[:, k, :], sel[:, k, :], mx[:, :], ALU.subtract)
                link(ins)
            dve.tensor_copy(den[:, :], mx[:, :]).then_inc(s["exp_in"], 1)
            dve.wait_ge(s["prefix"], 1)
            link(dve.tensor_copy(within[:, :, :], psW[:, 0:NT * E].rearrange("p (n e) -> p n e", e=E)))
            link(dve.tensor_copy(tile_n[:, :, :], psN[:, 0:NT * E].rearrange("p (n e) -> p n e", e=E)))
            src, dst = tile_n, scan_a
            step = 1
            while step < NT:
                link(dve.tensor_copy(dst[:, 0:step, :], src[:, 0:step, :]))
                link(dve.tensor_tensor(dst[:, step:NT, :], src[:, step:NT, :], src[:, 0:NT - step, :], ALU.add))
                src, dst = dst, (scan_b if dst is scan_a else scan_a)
                step *= 2
            incl = src
            link(dve.tensor_scalar(base[:, :], incl[:, NT - 1, :], float(P - 1), None, ALU.add))
            link(dve.tensor_copy(cnt_i[:, :], base[:, :]))
            link(dve.tensor_scalar(cnt_i[:, :], cnt_i[:, :], 7, None, ALU.logical_shift_right))
            link(dve.tensor_copy(nblk[:, :], cnt_i[:, :]))
            src2, dst2 = nblk, cum_a
            step = 1
            while step < E:
                link(dve.tensor_copy(dst2[:, 0:step], src2[:, 0:step]))
                link(dve.tensor_tensor(dst2[:, step:E], src2[:, step:E], src2[:, 0:E - step], ALU.add))
                src2, dst2 = dst2, (cum_b if dst2 is cum_a else cum_a)
                step *= 2
            cum = src2
            link(dve.tensor_tensor(base[:, :], cum[:, :], nblk[:, :], ALU.subtract))
            link(dve.tensor_tensor(place[:, :, :], within[:, :, :], incl[:, :, :], ALU.add))
            link(dve.tensor_tensor(place[:, :, :], place[:, :, :], tile_n[:, :, :], ALU.subtract))
            link(dve.scalar_tensor_tensor(place[:, :, :], over_tiles(base[:, :]), float(P), place[:, :, :], ALU.mult, ALU.add))
            for k in range(TOP):
                link(dve.tensor_tensor(prod[:, :, :], place[:, :, :], oh[k][:, :, :], ALU.mult))
                link(dve.tensor_reduce(slot_f[:, k, :], prod[:, :, :], AX.X, ALU.add))
            link(dve.tensor_copy(slot[:, :, :], slot_f[:, :, :]))
            link(dve.tensor_copy(pad_n[:, :], pad_i[:, :]))
            link(dve.scalar_tensor_tensor(pad_c[:, :], nblk[:, :], float(P), incl[:, NT - 1, :], ALU.mult, ALU.subtract))
            src3, dst3 = pad_c, cum2_a
            step = 1
            while step < E:
                link(dve.tensor_copy(dst3[:, 0:step], src3[:, 0:step]))
                link(dve.tensor_tensor(dst3[:, step:E], src3[:, step:E], src3[:, 0:E - step], ALU.add))
                src3, dst3 = dst3, (cum2_b if dst3 is cum2_a else cum2_a)
                step *= 2
            link(dve.tensor_tensor(pad_c[:, :], src3[:, :], pad_c[:, :], ALU.subtract))
            shape = [P, NPAD, E]
            link(dve.tensor_tensor(pad_w[:, :, :], pad_n[:, :].unsqueeze(2).broadcast_to(shape),
                                   pad_c[:, :].unsqueeze(1).broadcast_to(shape), ALU.is_ge))
            link(dve.tensor_tensor(pad_w[:, :, :], pad_w[:, :, :], incl[:, NT - 1, :].unsqueeze(1).broadcast_to(shape), ALU.mult))
            link(dve.tensor_reduce(pad_f[:, :], pad_w[:, :, :], AX.X, ALU.add))
            link(dve.tensor_tensor(pad[:, :], pad_f[:, :], pad_n[:, :], ALU.add))
            link(dve.tensor_tensor(cmpb[:, :, :], bidx[:, :].unsqueeze(2).broadcast_to([P, NBLK, E - 1]),
                                   cum[:, 0:E - 1].unsqueeze(1).broadcast_to([P, NBLK, E - 1]), ALU.is_ge))
            link(dve.tensor_reduce(blk_f[:, :], cmpb[:, :, :], AX.X, ALU.add))
            link(dve.tensor_scalar(blk_f[:, :], blk_f[:, :], 1.0, None, ALU.add))
            link(dve.tensor_scalar(wrap[:, :], blk_f[:, :], float(E), None, ALU.is_ge))
            link(dve.scalar_tensor_tensor(wrap[:, :], wrap[:, :], -float(E), blk_f[:, :], ALU.mult, ALU.add))
            link(dve.memset(blk_k[:, 0:NFIRST], 0))
            link(dve.memset(blk_w[:, 0:NFIRST], 0))
            link(dve.tensor_copy(blk_k[:, NFIRST:], blk_f[:, :]))
            link(dve.tensor_copy(blk_w[:, NFIRST:], wrap[:, :]))

            def probabilities():
                dve.wait_ge(s["exp"], 1)
                link(dve.tensor_tensor(den[:, :], ex[:, 0, :], ex[:, 1, :], ALU.add))
                link(dve.reciprocal(den[:, :], den[:, :]))
                for k in range(TOP):
                    link(dve.tensor_tensor(prob[:, k, :], ex[:, k, :], den[:, :], ALU.mult))
                link(dve.tensor_tensor(eq[:, :, :], oh[0][:, :, :], over_experts(prob[:, 0, :]), ALU.mult))
                link(dve.tensor_tensor(cand[:, :, :], oh[1][:, :, :], over_experts(prob[:, 1, :]), ALU.mult))
                link(dve.tensor_tensor(pmat[:, :, 1, 0:E], eq[:, :, :], cand[:, :, :], ALU.add))
                link(dve.memset(pmat[:, :, 1, E:E + 1], 1.0))
                link(dve.tensor_copy(ph16[:, :, :], pmat[:, :, 1, :]))
                link(dve.tensor_copy(pmat[:, :, 0, :], ph16[:, :, :]))
                link(dve.tensor_copy(pmat[:, :, 2, :], ph16[:, :, :]))
                dve.tensor_tensor(pmat[:, :, 1, :], pmat[:, :, 1, :], ph16[:, :, :], ALU.subtract).then_inc(s["probs"], 1)
            g_["probabilities"], g_["probs_done"] = probabilities, s["probs"]


def feed_forward(nc, t, sem, g_, shared, out):
    w_exp, blk_k, blk_w, slot, prob, pmat, ident, seen, ws_tile, bias, pick = (
        g_[k] for k in "w_exp blk_k blk_w slot prob pmat ident seen ws_tile bias pick".split())
    tag = "s_" if shared else "e_"
    N = NT - NFIRST if shared else NFIRST + NBLK
    W_SLOTS = 2 if shared else E
    sb = Map(nc, SBUF_LO + W_SLOTS * g_["PER_E"], g_["AUX_AT"])
    x_in = sb(tag + "x", [P, 2, D], F32)
    xT = sb(tag + "xT", [P, 2, 2, KD, P], F16)
    u = sb(tag + "u", [P, 2, D], F32)
    uT = sb(tag + "uT", [P, 2, KD, P], F16)
    g = sb(tag + "g", [P, D], F32)
    gT = sb(tag + "gT", [P, 2, 2, KD, P], F16)
    y = sb(tag + "y", [P, 2, D], F32)
    if shared:
        x1 = sb("s_x1", [P, 2, D], F32)
        yf = sb("s_yf", [P, NFIRST, D], F32)
        yr = sb("s_yr", [P, NFIRST, TOP, D], F32)
        of = sb("s_of", [P, NFIRST, D], F32)
        ya = sb("s_ya", [P, 2, TOP, D], F32)
        acc = sb("s_acc", [P, 2, D], F32)
        K3 = 3 * (E + 1)
        bd_raw = sb("bd_raw", [K3, D], F32)
        bd_16 = sb("bd_16", [K3, D], F32)
        bd_hi = sb("bd_hi", [K3, D], F16)
        bd = sb("bd", [K3, D], F16)
        low3 = sb("low3", [K3, 1], F32)
        pT = sb("pT", [K3, NT, P], F16)
    else:
        raw = sb("e_raw", [P, 2, 2, D], F32)
    names = "xT_t xT_h xT_l u_mm u_r uT_t uT_h uT_l g_mm silu g_r gT_t gT_h gT_l y_mm y_r"
    if shared:
        names += """ d_loaded low3 bd0 bd1 pT_t pT_c acc0 acc1
            first_ld first_ga first_0 first_1 first_2 first_mm first_r first_st"""
    else:
        names += " scattered"
    s = {n: sem(tag + n) for n in names.split()}
    x_ld = [sem(tag + "x_loaded0"), sem(tag + "x_loaded1")]
    if shared:
        x1_ld = [sem("s_x1_loaded0"), sem("s_x1_loaded1")]
        ga = [sem("s_gathered0"), sem("s_gathered1")]
    else:
        raw_ld = [sem("e_raw_loaded0"), sem("e_raw_loaded1")]
    y_st = [sem(tag + "y_stored0"), sem(tag + "y_stored1")]

    def live(n, lag):
        return not isinstance(n, int) or 0 <= n - lag < N

    def tile(n):
        return n + NFIRST

    def first_tile(n):
        return isinstance(n, int) and n < NFIRST

    def first_tiles(n):
        return range((n - 2) * NFIRST // 2, (n - 1) * NFIRST // 2)

    def run(eng, step, after=None):
        peeled = 4 if shared else NFIRST + 2
        for n in range(peeled):
            step(n, n % 2, n // 2)
            if after:
                after(n)
        with eng.Fori(peeled // 2, N // 2 - 1) as i:
            step(i * 2, 0, i)
            step(i * 2 + 1, 1, i)
        for n in range(N - 2, N + 2):
            step(n, n % 2, n // 2)

    with ExitStack() as ps:
        def bank(name):
            return ps.enter_context(nc.psum_tensor(tag + name, [P, 512], F32))
        psX, psU, psUT, psG, psGT, psY = (bank(n) for n in ("psX", "psU", "psUT", "psG", "psGT", "psY"))
        psP = [bank(f"psP{k}") for k in range(2)]
        block = ps.enter_context(nc.Block())

        @block.sync
        def _(sp):
            def load(n, j):
                at_least(sp, s["xT_t"], n - 1)
                if shared:
                    src, row = g_["xn_dram"], tile(n)
                elif first_tile(n):
                    src, row = g_["xn_dram"], n
                else:
                    src, row = g_["xs_dram"], n - NFIRST
                sp.dma_start(x_in[:, j], src[ds(row * P, P), :]).then_inc(x_ld[j], 16)

            def store(n, j, rows):
                sp.wait_ge(s["y_r"], n + 1)
                sp.dma_start(rows, y[:, j]).then_inc(y_st[j], 16)

            out_rows = out.rearrange("b s d -> (b s) d") if shared else None

            def step(n, j, i):
                first_slots = not shared and isinstance(n, int) and n + 2 == NFIRST
                if not first_slots and (not isinstance(n, int) or n + 2 < N):
                    load(n + 2, j)
                if shared and live(n, 0):
                    at_least(sp, s["acc0"], n - 1)
                    sp.dma_start(x1[:, j], g_["x1_dram"][ds(tile(n) * P, P), :]).then_inc(x1_ld[j], 16)
                if live(n, 2):
                    if shared:
                        dst, row = out_rows, tile(n - 2)
                    elif first_tile(n - 2):
                        dst, row = g_["yf_dram"], n - 2
                    else:
                        dst, row = g_["ys_dram"], n - 2 - NFIRST
                    store(n - 2, j, dst[ds(row * P, P), :])
                if first_slots:
                    sp.wait_ge(s["scattered"], 16 * (TOP * NT + NPAD))
                    load(n + 2, j)
            load(0, 0)
            load(1, 1)

            def rows_of(dr):
                return dr.rearrange("(n p) d -> p n d", p=P)

            def first(n):
                if n == 0:
                    sp.dma_start(yf[:, :, :], rows_of(g_["yf_dram"])).then_inc(s["first_ld"], 16)
                    sp.dma_start(of[:, :, :], rows_of(g_["x1_dram"][0:NFIRST * P, :])).then_inc(s["first_ld"], 16)
            run(sp, step, first if shared else None)
            if shared:
                sp.wait_ge(s["first_r"], NFIRST)
                sp.dma_start(rows_of(out_rows[0:NFIRST * P, :]), of[:, :, :]).then_inc(s["first_st"], 16)
                sp.wait_ge(s["first_st"], 16)
            for q in y_st:
                sp.wait_ge(q, 8 * N)

        @block.gpsimd
        def _(pool):
            if shared:
                pool.memset(low3[:, :], -1.0).then_inc(s["low3"], 1)
                pool.wait_ge(s["low3"], 1)
                pool.affine_select(out=low3[:, :], in_=low3[:, :], compare_op=ALU.is_ge, fill=0.0, base=-2 * (E + 1),
                                   pattern=[[0, 1]], channel_multiplier=1).then_inc(s["low3"], 1)
                def gather(dst, tile_, k, done):
                    pool.indirect_dma_start(dst, None, g_["ys_dram"],
                                            bass.IndirectOffsetOnAxis(ap=slot[:, k, tile_:tile_ + 1], axis=0)).then_inc(done, 16)
                for k in range(TOP):
                    for n in range(2):
                        gather(ya[:, n, k, :], tile(n), k, ga[n])
                for m in range(NFIRST):
                    for k in range(TOP):
                        gather(yr[:, m, k, :], m, k, s["first_ga"])
                for n in range(2, N):
                    pool.wait_ge(s["acc1"], n - 1)
                    for k in range(TOP):
                        gather(ya[:, n % 2, k, :], tile(n), k, ga[n % 2])
            else:
                for k in range(TOP):
                    for n in range(NT):
                        pool.indirect_dma_start(g_["xs_dram"], bass.IndirectOffsetOnAxis(ap=slot[:, k, n:n + 1], axis=0),
                                                g_["xn2"][:, n, :], None).then_inc(s["scattered"], 16)
                for q in range(NPAD):
                    pool.indirect_dma_start(g_["xs_dram"], bass.IndirectOffsetOnAxis(ap=g_["pad"][:, q:q + 1], axis=0),
                                            g_["zero"][:, :], None).then_inc(s["scattered"], 16)
                def load(k, half, m):
                    g_["load_half"](pool, raw[:, half], raw_ld[half], k, half, m)

                def halves(k, last):
                    for m in range(NM):
                        for half in range(2):
                            n = k * (2 * NM) + 2 * m + half
                            for piece in range(3):
                                g_["split_half"](pool, raw[:, half], raw_ld[half], (k - E_EARLY) * NM + m + 1, k, half, m, n, piece)
                            if last and m == NM - 1:
                                continue
                            pool.wait_ge(g_["split_done"], n + 2)
                            if not isinstance(k, int):
                                pool.tensor_tensor(seen[:, :], ws_tile[:, :], ws_tile[:, :], ALU.add)
                            load(*((k, half, m + 1) if m < NM - 1 else (k + 1, half, 0)))
                for half in range(2):
                    load(E_EARLY, half, 0)
                pool.wait_ge(s["scattered"], 16 * (TOP * NT + NPAD))
                pool.wait_ge(g_["probs_done"], 1)
                with pool.Fori(E_EARLY, E - 1) as k:
                    halves(k, False)
                halves(E - 1, False)
                pool.wait_ge(s["y_mm"], NFIRST)
                halves(E, False)
                pool.wait_ge(s["y_mm"], NFIRST + B * S // P)
                halves(E + 1, True)

        @block.scalar
        def _(act):
            if shared:
                for r in range(3):
                    act.dma_start(bd_raw[r * (E + 1):r * (E + 1) + E, :], t["L0_ffn_bdown"]).then_inc(s["d_loaded"], 16)
                    act.dma_start(bd_raw[r * (E + 1) + E:(r + 1) * (E + 1), :],
                                  t["L0_ffn_bsd"].rearrange("(o n) -> o n", o=1)).then_inc(s["d_loaded"], 16)

            def hi_part(dst, src):
                return act.activation(dst, src[:, :].rearrange("p (k n) -> p k n", n=P), ACT.Copy)

            def step(n, j, i):
                if live(n, 0):
                    act.wait_ge(s["u_mm"], n + 1)
                    at_least(act, s["g_r"], n - 1)
                    at_least(act, s["uT_t"], n - 1)
                    act.activation(u[:, j], psU[:, :], ACT.Copy, scale=1.0 / WS).then_inc(s["u_r"], 1)
                if live(n, 1):
                    act.wait_ge(s["gT_t"], n)
                    at_least(act, s["y_mm"], n - 2)
                    hi_part(gT[:, (j + 1) % 2, 0], psGT).then_inc(s["gT_h"], 1)
                if live(n, 0):
                    act.wait_ge(s["uT_t"], n + 1)
                    at_least(act, s["g_mm"], n)
                    hi_part(uT[:, 0], psUT).then_inc(s["uT_h"], 1)
                if live(n, 2) and not shared:
                    act.wait_ge(s["y_mm"], n - 1)
                    at_least(act, y_st[j], 16 * (i - 1))
                    act.activation(y[:, j], psY[:, :], ACT.Copy, scale=1.0 / WS).then_inc(s["y_r"], 1)
                if live(n, -1):
                    act.wait_ge(s["xT_t"], n + 2)
                    at_least(act, s["u_mm"], n)
                    hi_part(xT[:, (j + 1) % 2, 0], psX).then_inc(s["xT_h"], 1)
                if live(n, 0):
                    act.wait_ge(s["g_mm"], n + 1)
                    at_least(act, s["gT_t"], n)
                    act.activation(g[:, :], psG[:, :], ACT.Silu, scale=1.0 / WS).then_inc(s["silu"], 1)
            step(-1, 1, -1)
            run(act, step)

        @block.vector
        def _(dve):
            def finish(tiles):
                dve.wait_ge(s["first_ld"], 32)
                dve.wait_ge(s["first_ga"], 16 * TOP * NFIRST)
                for m in tiles:
                    for k in range(TOP):
                        dve.scalar_tensor_tensor(of[:, m], yr[:, m, k, :], prob[:, k, m:m + 1], of[:, m], ALU.mult, ALU.add).then_inc(s[f"first_{k}"], 1)
                        dve.wait_ge(s[f"first_{k}"], m + 1)
                    dve.tensor_tensor(of[:, m], of[:, m], yf[:, m], ALU.add).then_inc(s["first_2"], 1)
                    dve.wait_ge(s["first_2"], m + 1)
                    dve.wait_ge(s["first_mm"], m + 1)
                    dve.scalar_tensor_tensor(of[:, m], psP[m % 2][:, :], 1.0 / WS, of[:, m], ALU.mult, ALU.add).then_inc(s["first_r"], 1)

            def prepare(n):
                if n == 0:
                    dve.wait_ge(s["d_loaded"], 16 * 6)
                    dve.wait_ge(s["low3"], 2)
                    dve.tensor_scalar(bd_hi[:, :], bd_raw[:, :], WS, None, ALU.mult).then_inc(s["bd0"], 1)
                    dve.tensor_scalar(bd_16[:, :], bd_raw[:, :], WS, None, ALU.mult).then_inc(s["bd0"], 1)
                    dve.wait_ge(s["bd0"], 2)
                    dve.scalar_tensor_tensor(bd[:, :], bd_hi[:, :], low3[:, :], bd_16[:, :], ALU.mult, ALU.add).then_inc(s["bd1"], 1)
                if n >= 2:
                    return finish(first_tiles(n))
                for q in (2 * n, 2 * n + 1):
                    dve.wait_ge(s["pT_t"], q + 1)
                    dve.tensor_copy(pT[:, 4 * q:4 * q + 4, :].rearrange("p n t -> p (n t)"), psP[q % 2][0:K3, :]).then_inc(s["pT_c"], 1)

            def lo_part(pair, src):
                return dve.tensor_tensor(pair[:, 1], src[:, :].rearrange("p (k n) -> p k n", n=P), pair[:, 0], ALU.subtract)

            def total(n, j, nth, tile_):
                dve.wait_ge(ga[j], 32 * (nth + 1))
                dve.wait_ge(x1_ld[j], 16 * (nth + 1))
                p0, p1 = (prob[:, k, ds(tile_, 1)] for k in range(TOP))
                dve.scalar_tensor_tensor(acc[:, 0], ya[:, j, 0, :], p0, x1[:, j], ALU.mult, ALU.add).then_inc(s["acc0"], 1)
                dve.wait_ge(s["acc0"], n + 1)
                dve.scalar_tensor_tensor(acc[:, 1], ya[:, j, 1, :], p1, acc[:, 0], ALU.mult, ALU.add).then_inc(s["acc1"], 1)
                dve.wait_ge(s["acc1"], n + 1)
                dve.wait_ge(s["y_mm"], n + 1)
                at_least(dve, y_st[j], 16 * nth)
                dve.scalar_tensor_tensor(y[:, j], psY[:, :], 1.0 / WS, acc[:, 1], ALU.mult, ALU.add).then_inc(s["y_r"], 1)

            def step(n, j, i):
                if live(n, 1):
                    dve.wait_ge(s["gT_h"], n)
                    lo_part(gT[:, (j + 1) % 2], psGT).then_inc(s["gT_l"], 1)
                if live(n, 0):
                    dve.wait_ge(s["uT_h"], n + 1)
                    lo_part(uT, psUT).then_inc(s["uT_l"], 1)
                if shared and live(n, 2):
                    total(n - 2, j, i - 1, tile(n - 2))
                if live(n, -1):
                    dve.wait_ge(s["xT_h"], n + 2)
                    lo_part(xT[:, (j + 1) % 2], psX).then_inc(s["xT_l"], 1)
                if live(n, 0):
                    dve.wait_ge(s["silu"], n + 1)
                    dve.tensor_tensor(g[:, :], g[:, :], u[:, j], ALU.mult).then_inc(s["g_r"], 1)
            step(-1, 1, -1)
            run(dve, step, prepare if shared else lambda n: g_["probabilities"]() if n == 0 else None)

        @block.tensor
        def _(pe):
            def transposes(dst, src, done):
                for c in range(KD):
                    ins = pe.transpose(dst[:, c * P:(c + 1) * P], src[:, c * P:(c + 1) * P], ident[:, :])
                ins.then_inc(done, 1)

            def product(dst, a, w, m, more=(), chunks=range(KD)):
                terms = []
                for c in chunks:
                    for x, part in ((0, 0), (1, 0), (0, 1)):
                        terms.append((a[:, x, c, :], w_exp[:, ds(w * 2 + c // 2, 1), m, part, c % 2, :].rearrange("p o n -> p (o n)")))
                terms[3:3] = more
                for k, (stationary, moving) in enumerate(terms):
                    ins = pe.matmul(dst[:, :], stationary, moving, start=(k == 0 and chunks[0] == 0),
                                    stop=(k == len(terms) - 1 and chunks[-1] == KD - 1))
                return ins

            def biased(m, k):
                return [(pick[:, ds(k, 1), :].rearrange("p o n -> p (o n)"), bias[:, m, :])]

            def turn(n):
                if shared or first_tile(n):
                    return 0
                return pe.value_load(blk_k[0:1, ds(n, 1)], min_val=0, max_val=E)

            def place(n):
                if shared or first_tile(n):
                    return (E + 1) % E if shared else 0
                return pe.value_load(blk_w[0:1, ds(n, 1)], min_val=0, max_val=E - 1)

            def step(n, j, i):
                if live(n, 0):
                    k, w = turn(n), place(n)
                    if not shared:
                        pe.wait_ge(g_["split_done"], k * (2 * NM) + 2 * NM + 1)
                    pe.wait_ge(s["xT_l"], n + 1)
                    at_least(pe, s["u_r"], n)
                    product(psU, xT[:, j], w, 0, biased(0, k)).then_inc(s["u_mm"], 1)
                if live(n, 1):
                    pe.wait_ge(s["g_r"], n)
                    at_least(pe, s["gT_l"], n - 1)
                    transposes(psGT, g, s["gT_t"])
                if live(n, 2):
                    w2 = place(n - 2)
                    pe.wait_ge(s["gT_l"], n - 1)
                    at_least(pe, s["y_r"], n - 2)
                    probs = [(pT[:, ds(tile(n - 2), 1), :].rearrange("p o n -> p (o n)"), bd[:, :])] if shared else []
                    product(psY, gT[:, j], w2, 2, probs, range(0, KD // 2))
                if live(n, 0):
                    pe.wait_ge(s["u_r"], n + 1)
                    at_least(pe, s["uT_l"], n)
                    transposes(psUT, u[:, j], s["uT_t"])
                if live(n, 2):
                    product(psY, gT[:, j], w2, 2, [], range(KD // 2, KD)).then_inc(s["y_mm"], 1)
                if live(n, -1):
                    pe.wait_ge(x_ld[(j + 1) % 2], (i + 1 if j == 0 else i + 2) * 16)
                    at_least(pe, s["xT_l"], n + 1)
                    transposes(psX, x_in[:, (j + 1) % 2], s["xT_t"])
                if live(n, 0):
                    pe.wait_ge(s["uT_l"], n + 1)
                    at_least(pe, s["silu"], n)
                    product(psG, uT, w, 1, biased(1, k)).then_inc(s["g_mm"], 1)
            def prepare(n):
                if n >= 2:
                    for m in first_tiles(n):
                        at_least(pe, s["first_r"], m - 1)
                        pe.matmul(psP[m % 2][:, :], pT[:, m, :], bd[:, :], start=True, stop=True).then_inc(s["first_mm"], 1)
                    return
                for q in (2 * n, 2 * n + 1):
                    at_least(pe, s["pT_c"], q - 1)
                    for c in range(4):
                        ins = pe.transpose(psP[q % 2][0:K3, c * P:(c + 1) * P], pmat[:, 4 * q + c, :, :].rearrange("p a e -> p (a e)"), ident[:, :])
                    ins.then_inc(s["pT_t"], 1)
                if n == 1:
                    pe.wait_ge(s["pT_c"], 4)
                    pe.wait_ge(s["bd1"], 1)
            step(-1, 1, -1)
            run(pe, step, prepare if shared else None)


def kernel(**inputs):
    import concourse.bacc as bacc
    from concourse.bass_utils import run_bass_kernel_spmd

    nc = bacc.Bacc("TRN2", target_bir_lowering=False, num_devices=1)
    arrays = {f"in_{name}_dram": np.ascontiguousarray(a) for name, a in inputs.items()}
    t = {name: nc.dram_tensor(f"in_{name}_dram", a.shape, mybir.dt.from_np(np.asarray(a).dtype), kind="ExternalInput").ap()
         for name, a in inputs.items()}
    out = nc.dram_tensor("out_0_dram", (B, S, D), F32, kind="ExternalOutput").ap()
    build(nc, t, out)
    r = run_bass_kernel_spmd(nc, [arrays], core_ids=[0])
    return r.results[0]["out_0_dram"]
```
